# Optimizing a Trainium2 kernel written in Bass

```python
import numpy as np
import jax
import jax.numpy as jnp

def _softmax(x, axis=-1):
    return jax.nn.softmax(x, axis=axis)

def _gelu(x):
    return jax.nn.gelu(x, approximate=True)

def _silu(x):
    return jax.nn.silu(x)

def _sigmoid(x):
    return jax.nn.sigmoid(x)

def _layernorm(x, axis=-1, eps=1e-05):
    m = jnp.mean(x, axis=axis, keepdims=True)
    v = jnp.var(x, axis=axis, keepdims=True)
    return (x - m) / jnp.sqrt(v + eps)

def _scatter_add(tgt, idx, src, axis=0):
    return tgt.at[idx].add(src)

def _segment_sum(src, seg, n):
    return jax.ops.segment_sum(src, seg, n)
kernel_name = 'mk_cond_seq_d4_seqx_r4_b224cb'

def setup_inputs(seed: int=0):
    np.random.seed(seed)
    _w = jnp.asarray

    def _rec_inputs():
        import jax
        import jax.numpy as jnp
        _rk = jax.random.key(seed)
        x = 7.22e-05 + 1 * jax.random.normal(jax.random.fold_in(_rk, 1), (16, 256, 256), jnp.float32)
        _lenS = 256 - jax.random.randint(jax.random.fold_in(_rk, 7), (16,), 0, max(1, 256 // 4) + 1, jnp.int32)
        _lenS2 = 256 - jax.random.randint(jax.random.fold_in(_rk, 8), (16,), 0, max(1, 256 // 4) + 1, jnp.int32)
        cond_1024 = 0.0061147 + 1.02565 * jax.random.normal(jax.random.fold_in(_rk, 11), (16, 256), jnp.float32)
        fside_BxS_0 = 0.0125939 + 0.993166 * jax.random.normal(jax.random.fold_in(_rk, 13), (16, 256), jnp.float32)
        _validS = jnp.arange(256)[None, :] < _lenS[:, None]
        _validS2 = jnp.arange(256)[None, :] < _lenS2[:, None]
        _causal = jnp.tril(jnp.ones((256, 256), dtype=bool))
        mask_BxS_bk0 = jnp.logical_not(jnp.broadcast_to(_validS[:, :], (16, 256)))
        return (x, cond_1024, fside_BxS_0, mask_BxS_bk0)
    x, cond_1024, fside_BxS_0, mask_BxS_bk0 = _rec_inputs()

    def _L0_cond_setup():
        import jax, jax.numpy as jnp
        import numpy as np
        DIM = 256
        FF_MULT = 2
        EPS = 1e-06

        def _ln(x):
            mu = jnp.mean(x, axis=-1, keepdims=True)
            var = jnp.mean(jnp.square(x - mu), axis=-1, keepdims=True)
            return (x - mu) * jax.lax.rsqrt(var + EPS)
        key = jax.random.key(seed)
        ks = jax.random.split(key, 12)
        b, n, d = (4, 512, DIM)
        h = FF_MULT * d
        s = lambda fan_in: 1.0 / np.sqrt(fan_in)
        return {'x': jax.random.normal(ks[0], (b, n, d), jnp.float32), 't': jax.random.normal(ks[1], (b, d), jnp.float32), 'ada_w': jax.random.normal(ks[2], (d, 6 * d), jnp.float32) * s(d), 'ada_b': jnp.zeros((6 * d,), jnp.float32), 'ssm_w1': jax.random.normal(ks[3], (d, d), jnp.float32) * s(d), 'ssm_b1': jnp.zeros((d,), jnp.float32), 'ssm_w2': jax.random.normal(ks[4], (d, d), jnp.float32) * s(d), 'ssm_b2': jnp.zeros((d,), jnp.float32), 'ff_w1': jax.random.normal(ks[5], (d, h), jnp.float32) * s(d), 'ff_b1': jnp.zeros((h,), jnp.float32), 'ff_w2': jax.random.normal(ks[6], (h, d), jnp.float32) * s(h), 'ff_b2': jnp.zeros((d,), jnp.float32)}
    _L0_cond_all = _L0_cond_setup()
    _L0_cond_in = {k: v for k, v in _L0_cond_all.items() if k in ('ada_w', 'ada_b', 'ssm_w1', 'ssm_b1', 'ssm_w2', 'ssm_b2', 'ff_w1', 'ff_b1', 'ff_w2', 'ff_b2')}
    del _L0_cond_all

    def _L1_cond_setup():
        import jax, jax.numpy as jnp
        import numpy as np
        B, T, DIM = (4, 256, 256)
        COND = 256
        HEADS, DH = (16, 64)
        INNER = HEADS * DH
        MLP = 1024
        EPS = 1e-05

        def _layernorm(x):
            mu = jnp.mean(x, axis=-1, keepdims=True)
            var = jnp.mean(jnp.square(x - mu), axis=-1, keepdims=True)
            return (x - mu) * jax.lax.rsqrt(var + EPS)

        def _modulate(x, shift, scale):
            return x * (1.0 + scale) + shift

        def _attention(x, W_qkv, W_out, b_out):
            Bq, Tq, _ = x.shape
            qkv = x @ W_qkv
            q, k, v = jnp.split(qkv, 3, axis=-1)
            q = q.reshape(Bq, Tq, HEADS, DH)
            k = k.reshape(Bq, Tq, HEADS, DH)
            v = v.reshape(Bq, Tq, HEADS, DH)
            scale = DH ** (-0.5)
            attn = jnp.einsum('bqhd,bkhd->bhqk', q, k) * scale
            attn = jax.nn.softmax(attn, axis=-1)
            out = jnp.einsum('bhqk,bkhd->bqhd', attn, v).reshape(Bq, Tq, INNER)
            return out @ W_out + b_out

        def _ff(x, W1, b1, W2, b2):
            return jax.nn.gelu(x @ W1 + b1, approximate=False) @ W2 + b2
        key = jax.random.key(seed)
        ks = jax.random.split(key, 12)
        s = 0.02
        return {'x': jax.random.normal(ks[0], (B, T, DIM), jnp.float32), 'c': jax.random.normal(ks[1], (B, 1, COND), jnp.float32), 'W_mod': jax.random.normal(ks[2], (COND, 6 * DIM), jnp.float32) * s, 'b_mod': jax.random.normal(ks[3], (6 * DIM,), jnp.float32) * s, 'W_qkv': jax.random.normal(ks[4], (DIM, 3 * INNER), jnp.float32) * s, 'W_out': jax.random.normal(ks[5], (INNER, DIM), jnp.float32) * s, 'b_out': jax.random.normal(ks[6], (DIM,), jnp.float32) * s, 'W1': jax.random.normal(ks[7], (DIM, MLP), jnp.float32) * s, 'b1': jax.random.normal(ks[8], (MLP,), jnp.float32) * s, 'W2': jax.random.normal(ks[9], (MLP, DIM), jnp.float32) * s, 'b2': jax.random.normal(ks[10], (DIM,), jnp.float32) * s}
    _L1_cond_all = _L1_cond_setup()
    _L1_cond_in = {k: v for k, v in _L1_cond_all.items() if k in ('W_mod', 'b_mod', 'W_qkv', 'W_out', 'b_out', 'W1', 'b1', 'W2', 'b2')}
    del _L1_cond_all

    def _L2_cond_setup():
        import jax, jax.numpy as jnp
        import numpy as np
        B, L, D = (8, 512, 256)
        FF_MULT = 2
        EPS = 1e-06

        def _layernorm(x):
            mu = jnp.mean(x, axis=-1, keepdims=True)
            var = jnp.mean(jnp.square(x - mu), axis=-1, keepdims=True)
            return (x - mu) / jnp.sqrt(var + EPS)

        def _ssm_fallback(u, w1, b1, w2, b2):
            h = jax.nn.gelu(u @ w1 + b1, approximate=False)
            return h @ w2 + b2
        key = jax.random.key(seed)
        ks = jax.random.split(key, 20)
        s = 0.02
        inp = {'x': jax.random.normal(ks[0], (B, L, D), jnp.float32), 't': jax.random.normal(ks[1], (B, D), jnp.float32), 'mask': jax.random.randint(ks[2], (B, L), 0, 2) > 0, 'ada_w': jax.random.normal(ks[3], (D, 3 * D), jnp.float32) * s, 'ada_b': jnp.zeros((3 * D,), jnp.float32), 'ssm_w1': jax.random.normal(ks[4], (D, D), jnp.float32) * s, 'ssm_b1': jnp.zeros((D,), jnp.float32), 'ssm_w2': jax.random.normal(ks[5], (D, D), jnp.float32) * s, 'ssm_b2': jnp.zeros((D,), jnp.float32), 'bwd_w1': jax.random.normal(ks[6], (D, D), jnp.float32) * s, 'bwd_b1': jnp.zeros((D,), jnp.float32), 'bwd_w2': jax.random.normal(ks[7], (D, D), jnp.float32) * s, 'bwd_b2': jnp.zeros((D,), jnp.float32), 'ffada_w': jax.random.normal(ks[8], (D, 3 * D), jnp.float32) * s, 'ffada_b': jnp.zeros((3 * D,), jnp.float32), 'ff_w1': jax.random.normal(ks[9], (D, FF_MULT * D), jnp.float32) * s, 'ff_b1': jnp.zeros((FF_MULT * D,), jnp.float32), 'ff_w2': jax.random.normal(ks[10], (FF_MULT * D, D), jnp.float32) * s, 'ff_b2': jnp.zeros((D,), jnp.float32)}
        return inp
    _L2_cond_all = _L2_cond_setup()
    _L2_cond_in = {k: v for k, v in _L2_cond_all.items() if k in ('ada_w', 'ada_b', 'ssm_w1', 'ssm_b1', 'ssm_w2', 'ssm_b2', 'bwd_w1', 'bwd_b1', 'bwd_w2', 'bwd_b2', 'ffada_w', 'ffada_b', 'ff_w1', 'ff_b1', 'ff_w2', 'ff_b2')}
    del _L2_cond_all

    def _L3_cond_setup():
        import jax, jax.numpy as jnp
        import numpy as np
        B, S, D = (8, 256, 256)
        EPS = 1e-05

        def _layernorm(h, g, b):
            mu = jnp.mean(h, axis=-1, keepdims=True)
            var = jnp.mean((h - mu) ** 2, axis=-1, keepdims=True)
            return (h - mu) * jax.lax.rsqrt(var + EPS) * g + b
        key = jax.random.key(seed)
        ks = jax.random.split(key, 16)

        def lin(k, fan_in, fan_out):
            bound = 1.0 / np.sqrt(fan_in)
            k1, k2 = jax.random.split(k)
            W = jax.random.uniform(k1, (fan_in, fan_out), jnp.float32, -bound, bound)
            b = jax.random.uniform(k2, (fan_out,), jnp.float32, -bound, bound)
            return (W, b)
        Wq, bq = lin(ks[0], D, D)
        Wk, bk = lin(ks[1], D, D)
        Wv, bv = lin(ks[2], D, D)
        W1, b1 = lin(ks[3], D, 4 * D)
        W2, b2 = lin(ks[4], 4 * D, D)
        Wc, bc = lin(ks[5], 2 * D, 6 * D)
        return {'x': jax.random.normal(ks[6], (B, S, D), jnp.float32), 't': jax.random.normal(ks[7], (B, D), jnp.float32), 'c': jax.random.normal(ks[8], (B, D), jnp.float32), 'Wq': Wq, 'bq': bq, 'Wk': Wk, 'bk': bk, 'Wv': Wv, 'bv': bv, 'W1': W1, 'b1': b1, 'W2': W2, 'b2': b2, 'Wc': Wc, 'bc': bc, 'ln1_g': jnp.ones((D,), jnp.float32), 'ln1_b': jnp.zeros((D,), jnp.float32), 'ln2_g': jnp.ones((D,), jnp.float32), 'ln2_b': jnp.zeros((D,), jnp.float32)}
    _L3_cond_all = _L3_cond_setup()
    _L3_cond_in = {k: v for k, v in _L3_cond_all.items() if k in ('Wq', 'bq', 'Wk', 'bk', 'Wv', 'bv', 'W1', 'b1', 'W2', 'b2', 'Wc', 'bc', 'ln1_g', 'ln1_b', 'ln2_g', 'ln2_b')}
    del _L3_cond_all
    return {'x': x, 'cond_1024': cond_1024, 'fside_BxS_0': fside_BxS_0, 'mask_BxS_bk0': mask_BxS_bk0, 'L0_cond_ada_w': _L0_cond_in['ada_w'], 'L0_cond_ada_b': _L0_cond_in['ada_b'], 'L0_cond_ssm_w1': _L0_cond_in['ssm_w1'], 'L0_cond_ssm_b1': _L0_cond_in['ssm_b1'], 'L0_cond_ssm_w2': _L0_cond_in['ssm_w2'], 'L0_cond_ssm_b2': _L0_cond_in['ssm_b2'], 'L0_cond_ff_w1': _L0_cond_in['ff_w1'], 'L0_cond_ff_b1': _L0_cond_in['ff_b1'], 'L0_cond_ff_w2': _L0_cond_in['ff_w2'], 'L0_cond_ff_b2': _L0_cond_in['ff_b2'], 'L1_cond_W_mod': _L1_cond_in['W_mod'], 'L1_cond_b_mod': _L1_cond_in['b_mod'], 'L1_cond_W_qkv': _L1_cond_in['W_qkv'], 'L1_cond_W_out': _L1_cond_in['W_out'], 'L1_cond_b_out': _L1_cond_in['b_out'], 'L1_cond_W1': _L1_cond_in['W1'], 'L1_cond_b1': _L1_cond_in['b1'], 'L1_cond_W2': _L1_cond_in['W2'], 'L1_cond_b2': _L1_cond_in['b2'], 'L2_cond_ada_w': _L2_cond_in['ada_w'], 'L2_cond_ada_b': _L2_cond_in['ada_b'], 'L2_cond_ssm_w1': _L2_cond_in['ssm_w1'], 'L2_cond_ssm_b1': _L2_cond_in['ssm_b1'], 'L2_cond_ssm_w2': _L2_cond_in['ssm_w2'], 'L2_cond_ssm_b2': _L2_cond_in['ssm_b2'], 'L2_cond_bwd_w1': _L2_cond_in['bwd_w1'], 'L2_cond_bwd_b1': _L2_cond_in['bwd_b1'], 'L2_cond_bwd_w2': _L2_cond_in['bwd_w2'], 'L2_cond_bwd_b2': _L2_cond_in['bwd_b2'], 'L2_cond_ffada_w': _L2_cond_in['ffada_w'], 'L2_cond_ffada_b': _L2_cond_in['ffada_b'], 'L2_cond_ff_w1': _L2_cond_in['ff_w1'], 'L2_cond_ff_b1': _L2_cond_in['ff_b1'], 'L2_cond_ff_w2': _L2_cond_in['ff_w2'], 'L2_cond_ff_b2': _L2_cond_in['ff_b2'], 'L3_cond_Wq': _L3_cond_in['Wq'], 'L3_cond_bq': _L3_cond_in['bq'], 'L3_cond_Wk': _L3_cond_in['Wk'], 'L3_cond_bk': _L3_cond_in['bk'], 'L3_cond_Wv': _L3_cond_in['Wv'], 'L3_cond_bv': _L3_cond_in['bv'], 'L3_cond_W1': _L3_cond_in['W1'], 'L3_cond_b1': _L3_cond_in['b1'], 'L3_cond_W2': _L3_cond_in['W2'], 'L3_cond_b2': _L3_cond_in['b2'], 'L3_cond_Wc': _L3_cond_in['Wc'], 'L3_cond_bc': _L3_cond_in['bc'], 'L3_cond_ln1_g': _L3_cond_in['ln1_g'], 'L3_cond_ln1_b': _L3_cond_in['ln1_b'], 'L3_cond_ln2_g': _L3_cond_in['ln2_g'], 'L3_cond_ln2_b': _L3_cond_in['ln2_b']}

def reference(x, cond_1024, fside_BxS_0, mask_BxS_bk0, L0_cond_ada_w, L0_cond_ada_b, L0_cond_ssm_w1, L0_cond_ssm_b1, L0_cond_ssm_w2, L0_cond_ssm_b2, L0_cond_ff_w1, L0_cond_ff_b1, L0_cond_ff_w2, L0_cond_ff_b2, L1_cond_W_mod, L1_cond_b_mod, L1_cond_W_qkv, L1_cond_W_out, L1_cond_b_out, L1_cond_W1, L1_cond_b1, L1_cond_W2, L1_cond_b2, L2_cond_ada_w, L2_cond_ada_b, L2_cond_ssm_w1, L2_cond_ssm_b1, L2_cond_ssm_w2, L2_cond_ssm_b2, L2_cond_bwd_w1, L2_cond_bwd_b1, L2_cond_bwd_w2, L2_cond_bwd_b2, L2_cond_ffada_w, L2_cond_ffada_b, L2_cond_ff_w1, L2_cond_ff_b1, L2_cond_ff_w2, L2_cond_ff_b2, L3_cond_Wq, L3_cond_bq, L3_cond_Wk, L3_cond_bk, L3_cond_Wv, L3_cond_bv, L3_cond_W1, L3_cond_b1, L3_cond_W2, L3_cond_b2, L3_cond_Wc, L3_cond_bc, L3_cond_ln1_g, L3_cond_ln1_b, L3_cond_ln2_g, L3_cond_ln2_b):
    import jax
    import jax.numpy as jnp

    def _L0_cond_ref(x, t, ada_w, ada_b, ssm_w1, ssm_b1, ssm_w2, ssm_b2, ff_w1, ff_b1, ff_w2, ff_b2):
        import jax, jax.numpy as jnp
        import numpy as np
        DIM = 256
        FF_MULT = 2
        EPS = 1e-06

        def _ln(x):
            mu = jnp.mean(x, axis=-1, keepdims=True)
            var = jnp.mean(jnp.square(x - mu), axis=-1, keepdims=True)
            return (x - mu) * jax.lax.rsqrt(var + EPS)
        emb = jnp.dot(jax.nn.silu(t), ada_w) + ada_b
        shift_msa, scale_msa, gate_msa, shift_mlp, scale_mlp, gate_mlp = jnp.split(emb, 6, axis=-1)
        norm = _ln(x) * (1.0 + scale_msa[:, None]) + shift_msa[:, None]
        h = jax.nn.gelu(jnp.dot(norm, ssm_w1) + ssm_b1, approximate=False)
        ssm_out = jnp.dot(h, ssm_w2) + ssm_b2
        x = x + gate_msa[:, None] * ssm_out
        norm2 = _ln(x) * (1.0 + scale_mlp[:, None]) + shift_mlp[:, None]
        hf = jax.nn.gelu(jnp.dot(norm2, ff_w1) + ff_b1, approximate=True)
        ff_out = jnp.dot(hf, ff_w2) + ff_b2
        x = x + gate_mlp[:, None] * ff_out
        return x

    def _L1_cond_ref(x, c, W_mod, b_mod, W_qkv, W_out, b_out, W1, b1, W2, b2):
        import jax, jax.numpy as jnp
        import numpy as np
        B, T, DIM = (4, 256, 256)
        COND = 256
        HEADS, DH = (16, 64)
        INNER = HEADS * DH
        MLP = 1024
        EPS = 1e-05

        def _layernorm(x):
            mu = jnp.mean(x, axis=-1, keepdims=True)
            var = jnp.mean(jnp.square(x - mu), axis=-1, keepdims=True)
            return (x - mu) * jax.lax.rsqrt(var + EPS)

        def _modulate(x, shift, scale):
            return x * (1.0 + scale) + shift

        def _attention(x, W_qkv, W_out, b_out):
            Bq, Tq, _ = x.shape
            qkv = x @ W_qkv
            q, k, v = jnp.split(qkv, 3, axis=-1)
            q = q.reshape(Bq, Tq, HEADS, DH)
            k = k.reshape(Bq, Tq, HEADS, DH)
            v = v.reshape(Bq, Tq, HEADS, DH)
            scale = DH ** (-0.5)
            attn = jnp.einsum('bqhd,bkhd->bhqk', q, k) * scale
            attn = jax.nn.softmax(attn, axis=-1)
            out = jnp.einsum('bhqk,bkhd->bqhd', attn, v).reshape(Bq, Tq, INNER)
            return out @ W_out + b_out

        def _ff(x, W1, b1, W2, b2):
            return jax.nn.gelu(x @ W1 + b1, approximate=False) @ W2 + b2
        mod = jax.nn.silu(c) @ W_mod + b_mod
        sh_msa, sc_msa, g_msa, sh_mlp, sc_mlp, g_mlp = jnp.split(mod, 6, axis=-1)
        x = x + g_msa * _attention(_modulate(_layernorm(x), sh_msa, sc_msa), W_qkv, W_out, b_out)
        x = x + g_mlp * _ff(_modulate(_layernorm(x), sh_mlp, sc_mlp), W1, b1, W2, b2)
        return x

    def _L2_cond_ref(x, t, mask, ada_w, ada_b, ssm_w1, ssm_b1, ssm_w2, ssm_b2, bwd_w1, bwd_b1, bwd_w2, bwd_b2, ffada_w, ffada_b, ff_w1, ff_b1, ff_w2, ff_b2):
        import jax, jax.numpy as jnp
        import numpy as np
        B, L, D = (8, 512, 256)
        FF_MULT = 2
        EPS = 1e-06

        def _layernorm(x):
            mu = jnp.mean(x, axis=-1, keepdims=True)
            var = jnp.mean(jnp.square(x - mu), axis=-1, keepdims=True)
            return (x - mu) / jnp.sqrt(var + EPS)

        def _ssm_fallback(u, w1, b1, w2, b2):
            h = jax.nn.gelu(u @ w1 + b1, approximate=False)
            return h @ w2 + b2
        m = mask[:, :, None]
        emb = jax.nn.silu(t) @ ada_w + ada_b
        shift, scale, gate_msa = jnp.split(emb, 3, axis=1)
        norm = _layernorm(x) * (1.0 + scale[:, None]) + shift[:, None]
        norm = jnp.where(m, norm, 0.0)
        fwd = _ssm_fallback(norm, ssm_w1, ssm_b1, ssm_w2, ssm_b2)
        bwd = jnp.flip(_ssm_fallback(jnp.flip(norm, axis=1), bwd_w1, bwd_b1, bwd_w2, bwd_b2), axis=1)
        ssm_out = jnp.where(m, fwd + bwd, 0.0)
        x = x + gate_msa[:, None] * ssm_out
        ff_ada = jax.nn.silu(t) @ ffada_w + ffada_b
        shift_mlp, scale_mlp, gate_mlp = jnp.split(ff_ada, 3, axis=1)
        ff_norm = _layernorm(x) * (1.0 + scale_mlp[:, None]) + shift_mlp[:, None]
        h = jax.nn.gelu(ff_norm @ ff_w1 + ff_b1, approximate=True)
        ff_out = h @ ff_w2 + ff_b2
        return x + gate_mlp[:, None] * ff_out

    def _L3_cond_ref(x, t, c, Wq, bq, Wk, bk, Wv, bv, W1, b1, W2, b2, Wc, bc, ln1_g, ln1_b, ln2_g, ln2_b):
        import jax, jax.numpy as jnp
        import numpy as np
        B, S, D = (8, 256, 256)
        EPS = 1e-05

        def _layernorm(h, g, b):
            mu = jnp.mean(h, axis=-1, keepdims=True)
            var = jnp.mean((h - mu) ** 2, axis=-1, keepdims=True)
            return (h - mu) * jax.lax.rsqrt(var + EPS) * g + b
        dim = x.shape[-1]
        cond = jnp.concatenate([t, c], axis=-1) @ Wc + bc
        a1, g1, be1, a2, g2, be2 = jnp.split(cond[:, None, :], 6, axis=-1)
        h = _layernorm(x, ln1_g, ln1_b) * (1.0 + g1) + be1
        Q = h @ Wq + bq
        K = h @ Wk + bk
        V = h @ Wv + bv
        scores = jnp.einsum('bsd,btd->bst', Q, K) / jnp.sqrt(jnp.float32(dim))
        attn = jax.nn.softmax(scores, axis=-1) @ V
        x = x + a1 * attn
        h = _layernorm(x, ln2_g, ln2_b) * (1.0 + g2) + be2
        h = jax.nn.gelu(h @ W1 + b1, approximate=False)
        h = jax.nn.gelu(h @ W2 + b2, approximate=False)
        x = x + a2 * h
        return x
    x = _L0_cond_ref(x, cond_1024, L0_cond_ada_w, L0_cond_ada_b, L0_cond_ssm_w1, L0_cond_ssm_b1, L0_cond_ssm_w2, L0_cond_ssm_b2, L0_cond_ff_w1, L0_cond_ff_b1, L0_cond_ff_w2, L0_cond_ff_b2)
    x = _L1_cond_ref(x, cond_1024[:, None, :], L1_cond_W_mod, L1_cond_b_mod, L1_cond_W_qkv, L1_cond_W_out, L1_cond_b_out, L1_cond_W1, L1_cond_b1, L1_cond_W2, L1_cond_b2)
    x = _L2_cond_ref(x, cond_1024, mask_BxS_bk0, L2_cond_ada_w, L2_cond_ada_b, L2_cond_ssm_w1, L2_cond_ssm_b1, L2_cond_ssm_w2, L2_cond_ssm_b2, L2_cond_bwd_w1, L2_cond_bwd_b1, L2_cond_bwd_w2, L2_cond_bwd_b2, L2_cond_ffada_w, L2_cond_ffada_b, L2_cond_ff_w1, L2_cond_ff_b1, L2_cond_ff_w2, L2_cond_ff_b2)
    x = _L3_cond_ref(x, fside_BxS_0, cond_1024, L3_cond_Wq, L3_cond_bq, L3_cond_Wk, L3_cond_bk, L3_cond_Wv, L3_cond_bv, L3_cond_W1, L3_cond_b1, L3_cond_W2, L3_cond_b2, L3_cond_Wc, L3_cond_bc, L3_cond_ln1_g, L3_cond_ln1_b, L3_cond_ln2_g, L3_cond_ln2_b)
    return x

_drawn_inputs = setup_inputs


def setup_inputs(seed=0):
    import zlib

    import numpy as np

    out = dict(_drawn_inputs(seed))
    spreads = {'L0_cond_ada_b': (0.0, 0.1),
     'L0_cond_ssm_b1': (0.0, 0.1),
     'L0_cond_ssm_b2': (0.0, 0.1),
     'L0_cond_ff_b1': (0.0, 0.304),
     'L0_cond_ff_b2': (0.0, 0.1),
     'L2_cond_ada_b': (0.0, 0.8),
     'L2_cond_ssm_b1': (0.0, 0.8),
     'L2_cond_ssm_b2': (0.0, 0.8),
     'L2_cond_bwd_b1': (0.0, 0.8),
     'L2_cond_bwd_b2': (0.0, 0.8),
     'L2_cond_ffada_b': (0.0, 0.8),
     'L2_cond_ff_b1': (0.0, 0.8),
     'L2_cond_ff_b2': (0.0, 0.533),
     'L3_cond_ln1_g': (1.0, 0.6),
     'L3_cond_ln1_b': (0.0, 0.8),
     'L3_cond_ln2_g': (1.0, 0.6),
     'L3_cond_ln2_b': (0.0, 2.0)}
    factors = {'L1_cond_b_mod': 8.0,
     'L1_cond_W_qkv': 3.856,
     'L1_cond_W_out': 3.917,
     'L1_cond_b_out': 8.0,
     'L1_cond_W1': 3.349,
     'L1_cond_b1': 8.0,
     'L1_cond_W2': 3.261,
     'L1_cond_b2': 8.0,
     'L2_cond_ada_w': 6.353,
     'L2_cond_ssm_w1': 8.0,
     'L2_cond_ssm_w2': 8.0,
     'L2_cond_bwd_w1': 8.0,
     'L2_cond_bwd_w2': 8.0,
     'L2_cond_ffada_w': 3.015,
     'L2_cond_ff_w1': 4.333,
     'L2_cond_ff_w2': 4.128,
     'L3_cond_Wq': 3.253,
     'L3_cond_bq': 36.236,
     'L3_cond_Wk': 3.257,
     'L3_cond_bk': 64.0,
     'L3_cond_bv': 23.044,
     'L3_cond_b1': 64.0,
     'L3_cond_b2': 64.0,
     'L3_cond_bc': 12.824,
     'L3_cond_W1': 4.206,
     'L3_cond_W2': 3.681}
    for name, (base, spread) in spreads.items():
        noise = np.random.default_rng([zlib.crc32(name.encode()), seed]).standard_normal(out[name].shape)
        drawn = base * np.exp(spread * noise) if base else spread * noise
        out[name] = jnp.asarray(drawn.astype(out[name].dtype))
    for name, factor in factors.items():
        out[name] = (out[name] * factor).astype(out[name].dtype)
    return out
```

```python
from contextlib import ExitStack

import concourse.bass as bass
from concourse import mybir

ALU = mybir.AluOpType
ACT = mybir.ActivationFunctionType
F32 = mybir.dt.float32
F32R = mybir.dt.float32r
I32 = mybir.dt.int32
U8 = mybir.dt.uint8
AX_X = mybir.AxisListType.X

P = 128
BATCH, SEQ, D = 16, 256, 256
TPB = SEQ // P
DC = D // P
ROWW = TPB * D
HEADS, DH = 16, 64
INNER = HEADS * DH
PAIRS = HEADS // 2
GB = 2
GROUPS = BATCH // GB
GW = GB * SEQ
NPH = 8
L1_ATTN, L2_SSM, L3_ATTN, L3_FF = 2, 4, 6, 7

HID = {0: 256, 1: 512, 3: 1024, 4: 512, 5: 512, 7: 1024}
ACTF = {0: ACT.Gelu, 1: ACT.Gelu_apprx_tanh, 3: ACT.Gelu, 4: ACT.Gelu, 5: ACT.Gelu_apprx_tanh, 7: ACT.Gelu}
EPS = [1e-6, 1e-6, 1e-5, 1e-5, 1e-6, 1e-6, 1e-5, 1e-5]


def bass_cond_blocks(nc, t, out):
    def two(w1, w2):
        return [(t[w1], "w1", 0, 0), (t[w2], "w2", 0, 0)]

    PARTS = {
        0: two("L0_cond_ssm_w1", "L0_cond_ssm_w2"),
        1: two("L0_cond_ff_w1", "L0_cond_ff_w2"),
        2: two("L1_cond_W_qkv", "L1_cond_W_out"),
        3: two("L1_cond_W1", "L1_cond_W2"),
        4: [(t["L2_cond_ssm_w1"], "w1", 0, 0), (t["L2_cond_bwd_w1"], "w1", 0, 256),
            (t["L2_cond_ssm_w2"], "w2", 0, 0), (t["L2_cond_bwd_w2"], "w2", 2, 0)],
        5: two("L2_cond_ff_w1", "L2_cond_ff_w2"),
        6: [(t["L3_cond_Wq"], "w1", 0, 0), (t["L3_cond_Wk"], "w1", 0, 256), (t["L3_cond_Wv"], "w1", 0, 512)],
        7: two("L3_cond_W1", "L3_cond_W2"),
    }
    W1_COLS = {**HID, 2: 3 * INNER, 6: 3 * D}
    W2_CHUNKS = {**{p: h // P for p, h in HID.items()}, 2: INNER // P, 6: 0}
    SLICES = [1] + [GROUPS if p - 1 in HID else BATCH for p in range(1, NPH)]
    SLICE_BASE = [sum(SLICES[:p]) for p in range(NPH + 1)]
    LOAD_BASE = [sum(16 * len(PARTS[q]) * SLICES[q] for q in range(p)) for p in range(NPH + 1)]

    ADA = [("L0_cond_ada_w", "L0_cond_ada_b", 0), ("L1_cond_W_mod", "L1_cond_b_mod", 0),
           ("L2_cond_ada_w", "L2_cond_ada_b", 0), ("L2_cond_ffada_w", "L2_cond_ffada_b", 0),
           ("L3_cond_Wc", "L3_cond_bc", 1)]
    COND = [(0, 0, 1, 2, "L0_cond_ssm_b2"), (0, 3, 4, 5, "L0_cond_ff_b2"),
            (1, 0, 1, 2, "L1_cond_b_out"), (1, 3, 4, 5, "L1_cond_b2"),
            (2, 0, 1, 2, "L2_cond_ssm_b2"), (3, 0, 1, 2, "L2_cond_ff_b2"),
            (4, 2, 1, 0, "L3_cond_bv"), (4, 5, 4, 3, "L3_cond_b2")]
    BIASES = {0: ["L0_cond_ssm_b1"], 1: ["L0_cond_ff_b1"], 3: ["L1_cond_b1"],
              4: ["L2_cond_ssm_b1", "L2_cond_bwd_b1"], 5: ["L2_cond_ff_b1"],
              6: ["L3_cond_bq", "L3_cond_bk"], 7: ["L3_cond_b1"]}
    VEC_SRC, BIAS_AT, ADAB_AT, LN_AT = [], {}, {}, {}

    def vec_rows(src):
        at = sum(v.shape[0] // P for v in VEC_SRC)
        VEC_SRC.append(src)
        return at
    for p, names in BIASES.items():
        BIAS_AT[p] = [vec_rows(t[n]) for n in names][0]
    for p, (m, sh, sc, _, _) in enumerate(COND):
        for s, sec in enumerate((sc, sh)):
            ADAB_AT[p, s] = vec_rows(t[ADA[m][1]][sec * D:(sec + 1) * D])
    for j in range(2):
        for v in "gb":
            LN_AT[v, j] = vec_rows(t[f"L3_cond_ln{j + 1}_{v}"])
    NVEC = sum(v.shape[0] // P for v in VEC_SRC)
    NC = BATCH * DC

    def before(per):
        return [sum(per(q) for q in range(p)) for p in range(NPH + 1)]
    CHUNK_BASE = before(lambda q: GROUPS * HID[q] // P if q in HID else 0)
    GROUP_BASE = before(lambda q: GROUPS if q in HID else 0)

    gate_scratch = nc.dram_tensor("gate_scratch", (NPH, BATCH, 2 * D), F32).ap()

    ctx = ExitStack()
    with ctx:
        def sb(name, shape, dt=F32, scope=ctx):
            return scope.enter_context(nc.sbuf_tensor(name, shape, dt))

        def sem(name):
            return ctx.enter_context(nc.semaphore(name))

        x = sb("x", [P, BATCH * ROWW])
        stage = sb("stage", [P, 1024])
        mod = sb("mod", [P, NPH, 2, DC, BATCH])
        vecs = sb("vecs", [P, NVEC])
        biases = vecs
        ident = sb("ident", [P, P])
        maski = sb("maski", [P, BATCH * TPB], I32)
        spacer = sb("spacer", [P, 8])
        mcur = sb("mcur", [P, GB, TPB], I32)
        stats = sb("stats", [P, TPB, 6])
        meanvar = sb("meanvar", [P, TPB, 2])
        vareps = sb("vareps", [P, TPB])
        rstd = sb("rstd", [P, TPB])
        mhalf = sb("mhalf", [P, TPB])
        xn = sb("xn", [P, ROWW])
        nf = sb("nf", [P, ROWW])

        pro = ExitStack()
        adaw, kcs = [], []
        for n, (w, _, _) in enumerate(ADA):
            kc = t[w].shape[0] // P
            kcs.append(kc)
            adaw.append(sb(f"adaw{n}", [P, kc, t[w].shape[1]], scope=pro))
        condrows = sb("condrows", [3 * NC, P], scope=pro)
        mask8 = sb("mask8", [3 * NC, P], U8, scope=pro)
        vecrows = sb("vecrows", [NVEC, P], scope=pro)
        condT = sb("condT", [P, 2, BATCH, DC], scope=pro)
        siluT = sb("siluT", [P, BATCH, DC], scope=pro)
        be = sb("be", [P, 2, DC, BATCH], scope=pro)
        gain = sb("gain", [P, 2, DC, BATCH], scope=pro)
        growb = sb("growb", [BATCH, NPH, D], scope=pro)
        b2row = sb("b2row", [BATCH, NPH, D], scope=pro)
        bwdrow = sb("bwdrow", [BATCH, D], scope=pro)
        grow = sb("grow", [BATCH, NPH, 2, D], scope=pro)
        pro.close()

        WB = [sb("WBhi", [P, 4096], F32R), sb("WBlo", [P, 4096], F32R)]

        ffn = ExitStack()
        nT = [[sb(f"nT{k}_{i}", [P, DC, GW], F32R, ffn) for k in ("hi", "lo")] for i in range(2)]
        hf = [sb(f"hf{i}", [P, GW], scope=ffn) for i in range(2)]
        hh = [sb(f"hh{i}", [P, GW], F32R, ffn) for i in range(2)]
        hl = [sb(f"hl{i}", [P, GW], F32R, ffn) for i in range(2)]
        xb = sb("xb", [P, GB, ROWW], scope=ffn)
        upd = sb("upd", [P, GB, ROWW], scope=ffn)
        act2 = sb("act2", [P, GB, ROWW], scope=ffn)
        gates = sb("gates", [P, 2 * GB, 2 * D], scope=ffn)
        ffn.close()

        att = ctx
        aT = [sb(f"aT{k}", [P, DC, SEQ], F32R, att) for k in ("hi", "lo")]
        qkf = [sb(f"qkf{i}", [P, 2 * SEQ], scope=att) for i in range(2)]
        qz = [[sb(f"qz{k}{i}", [P, 2 * SEQ], F32R, att) for k in ("hi", "lo")] for i in range(2)]
        kk = [[sb(f"kk{k}{i}", [P, SEQ], F32R, att) for k in ("hi", "lo")] for i in range(2)]
        vf = sb("vf", [P, 512], scope=att)
        vv = [sb(f"v{k}", [P, TPB, INNER], F32R, att) for k in ("hi", "lo")]
        prob = [sb(f"prob{i}", [P, TPB, SEQ], scope=att) for i in range(2)]
        ptf = [sb(f"ptf{i}", [P, 2 * SEQ], scope=att) for i in range(2)]
        pt = [[sb(f"pt{k}{i}", [P, 2 * SEQ], F32R, att) for k in ("hi", "lo")] for i in range(2)]
        of = [sb(f"of{i}", [P, SEQ], scope=att) for i in range(2)]
        oT = [[sb(f"oT{k}{i}", [P, SEQ], F32R, att) for k in ("hi", "lo")] for i in range(2)]
        axb = sb("axb", [P, ROWW], scope=att)
        aupd = sb("aupd", [P, ROWW], scope=att)
        agate = sb("agate", [P, 2 * D], scope=att)
        smax = [sb(f"smax{i}", [P, TPB], scope=att) for i in range(2)]
        nmax = [sb(f"nmax{i}", [P, TPB], scope=att) for i in range(2)]
        rsum = [sb(f"rsum{i}", [P, TPB], scope=att) for i in range(2)]
        rinv = [sb(f"rinv{i}", [P, TPB], scope=att) for i in range(2)]
        WA = [sb("WAhi", [P, 8192], F32R), sb("WAlo", [P, 8192], F32R)]

        bank = [ctx.enter_context(nc.psum_tensor(f"bank{i}", [P, 512], F32)) for i in range(8)]
        T_BANK = bank[7]

        def w_tiles(p):
            W = WA if p % 2 == 0 else WB
            n1 = DC * W1_COLS[p]
            v1 = [w[:, 0:n1].rearrange("p (k m) -> p k m", k=DC) for w in W]
            if not W2_CHUNKS[p]:
                return v1, None
            v2 = [w[:, n1:n1 + W2_CHUNKS[p] * D].rearrange("p (k m) -> p k m", m=D) for w in W]
            return v1, v2

        pro_loads = sem("pro_loads"); x_loaded = sem("x_loaded"); mask_rows = sem("mask_rows"); cond_tp = sem("cond_tp"); cond_cols = sem("cond_cols")
        consts = sem("consts"); ident_zero = sem("ident_zero"); silu_ready = sem("silu_ready"); mod_mm = sem("mod_mm")
        mod_step = sem("mod_step"); gate_rows = sem("gate_rows"); gates_stored = sem("gates_stored")
        w_loaded = sem("w_loaded"); w_hi = sem("w_hi"); w_lo = sem("w_lo")
        phase_end = sem("phase_end")
        gate_loaded = [sem(f"gate_loaded{i}") for i in range(2 * GB)]
        ln_stats_s = sem("ln_stats"); ln_mv = sem("ln_mv"); ln_ve = sem("ln_ve"); ln_rstd = sem("ln_rstd")
        ln_xn = sem("ln_xn"); ln_tp = sem("ln_tp"); ln_nf = sem("ln_nf"); ln_hi = sem("ln_hi"); ln_lo = sem("ln_lo")
        u_mm = sem("u_mm"); h_act = sem("h_act"); h_hi = sem("h_hi"); h_lo = sem("h_lo")
        w2_mm = sem("w2_mm"); y_taken = sem("y_taken"); xb_ready = sem("xb_ready");
        gelu2 = sem("gelu2"); gated2 = sem("gated2")
        x_new = sem("x_new"); x_tmp = sem("x_tmp"); x_stored = sem("x_stored")
        zeros = sem("zeros")
        proj_mm = sem("proj_mm"); proj_ev = sem("proj_ev"); qk_hi = sem("qk_hi"); qk_lo = sem("qk_lo")
        v_hi = sem("v_hi"); v_lo = sem("v_lo"); s_mm = sem("s_mm"); max_ready = sem("max_ready")
        nmax_ready = sem("nmax_ready"); pool_step = sem("pool_step"); exp_ready = sem("exp_ready"); rinv_ready = sem("rinv_ready")
        prob_ready = sem("prob_ready"); pt_mm = sem("pt_mm"); pt_ev = sem("pt_ev"); pt_hi = sem("pt_hi")
        pt_lo = sem("pt_lo"); pv_mm = sem("pv_mm"); o_ev = sem("o_ev"); o_hi = sem("o_hi"); o_lo = sem("o_lo")
        out_mm = sem("out_mm"); ay_taken = sem("ay_taken"); axb_ready = sem("axb_ready")
        aupd_ready = sem("aupd_ready"); ax_new = sem("ax_new"); agate_loaded = sem("agate_loaded")
        b_q = sem("b_q"); b_k = sem("b_k"); b_v = sem("b_v"); q_ev = sem("q_ev"); k_ev = sem("k_ev"); v_ev = sem("v_ev")
        q_hi = sem("q_hi"); q_lo = sem("q_lo"); k_hi = sem("k_hi"); k_lo = sem("k_lo")

        ENGINES = 4

        def end_phase(eng, p, signs=True):
            if signs:
                eng.drain().then_inc(phase_end, 1)
            eng.wait_ge(phase_end, ENGINES * (p + 2))

        def xs(b):
            return x[:, bass.ds(b * ROWW, ROWW)]

        def split3(pe, dst, lhs, rhs, start, stop):
            pe.matmul(dst, lhs[1], rhs[0], start=start, stop=False, skip_group_check=True)
            pe.matmul(dst, lhs[0], rhs[1], start=False, stop=False, skip_group_check=True)
            return pe.matmul(dst, lhs[0], rhs[0], start=False, stop=stop, skip_group_check=True)

        def slice_views(p, s):
            n, at, views = SLICES[p], 0, []
            for w, which, k0, m0 in PARTS[p]:
                kc, m = w.shape[0] // P, w.shape[1]
                ms = m // n
                src = w.rearrange("(k p) m -> p k m", p=P)[:, :, bass.ds(s * ms, ms)]
                st = stage[:, at:at + kc * ms].rearrange("p (k m) -> p k m", k=kc)
                tiles = w_tiles(p)[0 if which == "w1" else 1]
                hi, lo = (v[:, k0:k0 + kc, bass.ds(s * ms + m0, ms)] for v in tiles)
                views.append((src, st, hi, lo))
                at += kc * ms
            return views

        def weights_load(sp, p, s):
            if p < NPH:
                if p > 0:
                    sp.wait_ge(w_lo, SLICE_BASE[p] + s)
                for src, st, _, _ in slice_views(p, s):
                    sp.dma_start(st, src).then_inc(w_loaded, 16)

        def weights_hi(dve, p, s):
            if p < NPH:
                views = slice_views(p, s)
                dve.wait_ge(w_loaded, LOAD_BASE[p] + 16 * len(views) * (s + 1))
                dve.memset(spacer[:, 0:1], 0.0)
                for _, st, hi, _ in views:
                    last = dve.tensor_copy(hi, st)
                last.then_inc(w_hi, 1)

        def weights_lo(pool, p, s):
            if p < NPH:
                pool.wait_ge(w_hi, SLICE_BASE[p] + s + 1)
                for _, st, hi, lo in slice_views(p, s):
                    last = pool.tensor_tensor(lo, st, hi.bitcast(F32), ALU.subtract)
                last.then_inc(w_lo, 1)

        def ln_stats(dve, p, b):
            u = p * BATCH + b
            for k in range(TPB):
                last = dve.bn_stats(stats[:, k, :], x[:, bass.ds(b * ROWW + k * D, D)])
            last.then_inc(ln_stats_s, 1)
            dve.wait_ge(ln_stats_s, u + 1)
            dve.memset(spacer[:, 1:2], 0.0)
            for k in range(TPB):
                last = dve.bn_aggr(meanvar[:, k, :], stats[:, k, :])
            last.then_inc(ln_mv, 1)
            dve.wait_ge(ln_mv, u + 1)
            dve.tensor_scalar(vareps[:, :], meanvar[:, :, 1], EPS[p], None, ALU.add).then_inc(ln_ve, 1)

        def ln_rsqrt(pool, p, b):
            pool.wait_ge(ln_ve, p * BATCH + b + 1)
            pool.tensor_tensor(rstd[:, :], vareps[:, :], mhalf[:, :], ALU.pow).then_inc(ln_rstd, 1)

        def ln_norm(dve, p, b):
            u = p * BATCH + b
            dve.wait_ge(ln_rstd, u + 1)
            dve.wait_ge(ln_tp, u)
            for k in range(TPB):
                last = dve.tensor_scalar(xn[:, k * D:(k + 1) * D], x[:, bass.ds(b * ROWW + k * D, D)],
                                         meanvar[:, k, 0:1], rstd[:, k:k + 1], ALU.subtract, ALU.mult)
            last.then_inc(ln_xn, 1)

        def ln_transpose(pe, p, b):
            u = p * BATCH + b
            pe.wait_ge(ln_xn, u + 1)
            pe.wait_ge(ln_nf, u)
            for c in range(DC):
                for k in range(TPB):
                    last = pe.transpose(T_BANK[:, c * SEQ + k * P:c * SEQ + (k + 1) * P],
                                        xn[:, k * D + c * P:k * D + (c + 1) * P], ident[:, :])
            last.then_inc(ln_tp, 1)

        def ln_modulate(act, p, b):
            u = p * BATCH + b
            act.wait_ge(ln_tp, u + 1)
            act.wait_ge(ln_lo, u)
            for c in range(DC):
                last = act.activation(nf[:, c * SEQ:(c + 1) * SEQ], T_BANK[:, c * SEQ:(c + 1) * SEQ],
                                      ACT.Identity, scale=mod[:, p, 0, c, bass.ds(b, 1)],
                                      bias=mod[:, p, 1, c, bass.ds(b, 1)])
            last.then_inc(ln_nf, 1)

        def ln_split(dve, p, b, hi, lo):
            u = p * BATCH + b
            src = nf[:, :].rearrange("p (c r) -> p c r", c=DC)
            dve.wait_ge(ln_nf, u + 1)
            dve.tensor_copy(hi, src).then_inc(ln_hi, 1)
            dve.wait_ge(ln_hi, u + 1)
            dve.tensor_tensor(lo, src, hi.bitcast(F32), ALU.subtract).then_inc(ln_lo, 1)

        U_BANKS, Y_BANKS = bank[0:2], bank[2:4]

        def ff_hidden(pe, p, g, i, c, w1):
            n = CHUNK_BASE[p] + (HID[p] // P) * g + c
            if c == 0:
                pe.wait_ge(ln_lo, p * BATCH + GB * g + GB)
            if p or i or c > 1:
                pe.wait_ge(h_act, n - 1)
            for k in range(DC):
                last = split3(pe, U_BANKS[c % 2][:, :], [w[:, k, c * P:(c + 1) * P] for w in w1],
                              [m[:, k, :] for m in nT[i]], k == 0, k == DC - 1)
            last.then_inc(u_mm, 1)

        def ff_output(pe, p, g, c, w2):
            n = CHUNK_BASE[p] + (HID[p] // P) * g + c
            pe.wait_ge(h_lo, n + 1)
            if c == 0:
                pe.wait_ge(y_taken, GB * (GROUP_BASE[p] + g))
            for r in range(GB * TPB):
                last = split3(pe, Y_BANKS[r // TPB][:, (r % TPB) * D:(r % TPB + 1) * D],
                              [h[:, r * P:(r + 1) * P] for h in (hh[c % 2], hl[c % 2])],
                              [w[:, c, :] for w in w2], c == 0 and r % TPB == 0, c == HID[p] // P - 1)
            last.then_inc(w2_mm, 1)

        def ff_tensor(pe, p, g, i, last_group):
            C = HID[p] // P
            w1, w2 = w_tiles(p)
            ff_hidden(pe, p, g, i, 0, w1)
            ff_hidden(pe, p, g, i, 1, w1)
            for c in range(C):
                ff_output(pe, p, g, c, w2)
                if c < GB and not last_group:
                    ln_transpose(pe, p, GB * (g + 1) + c)
                if c + 2 < C:
                    ff_hidden(pe, p, g, i, c + 2, w1)

        def ff_scalar(act, p, g, i, last_group):
            C = HID[p] // P
            def hidden(c):
                n = CHUNK_BASE[p] + C * g + c
                act.wait_ge(u_mm, n + 1)
                if p or i or c > 1:
                    act.wait_ge(h_lo, n - 1)
                b = BIAS_AT[p] + c
                act.activation(hf[c % 2][:, :], U_BANKS[c % 2][:, :], ACTF[p],
                               bias=biases[:, b:b + 1]).then_inc(h_act, 1)
            hidden(0)
            hidden(1)
            for c in range(C):
                if c < GB and not last_group:
                    ln_modulate(act, p, GB * (g + 1) + c)
                if c + 2 < C:
                    hidden(c + 2)
            if p == L3_FF:
                for j in range(GB):
                    act.wait_ge(y_taken, GB * (GROUP_BASE[p] + g) + j + 1)
                    act.activation(act2[:, j, :], upd[:, j, :], ACT.Gelu).then_inc(gelu2, 1)

        def ff_vector(dve, p, g, i, last_group):
            C = HID[p] // P
            def hidden_hi(c):
                n = CHUNK_BASE[p] + C * g + c
                dve.wait_ge(h_act, n + 1)
                if p or i or c > 1:
                    dve.wait_ge(w2_mm, n - 1)
                dve.tensor_copy(hh[c % 2][:, :], hf[c % 2][:, :]).then_inc(h_hi, 1)
            nxt = [GB * (g + 1) + j for j in range(GB)]
            def split_next(j):
                if not last_group:
                    dve_hi_lo = [m[:, :, j * SEQ:(j + 1) * SEQ] for m in nT[1 - i]]
                    dve.wait_ge(u_mm, CHUNK_BASE[p] + C * g + 1)
                    ln_split(dve, p, nxt[j], *dve_hi_lo)
            if not last_group:
                ln_stats(dve, p, nxt[0])
            hidden_hi(0)
            if not last_group:
                ln_norm(dve, p, nxt[0])
                ln_stats(dve, p, nxt[1])
            hidden_hi(1)
            if not last_group:
                ln_norm(dve, p, nxt[1])
            for c in range(C):
                if c < GB:
                    split_next(c)
                if c + 2 < C:
                    hidden_hi(c + 2)
            for j in range(GB):
                n = GB * (GROUP_BASE[p] + g) + j
                slot = GB * i + j
                dve.wait_ge(w2_mm, CHUNK_BASE[p] + C * (g + 1))
                dve.wait_ge(gate_loaded[slot], 8 * (GROUP_BASE[p] + g - i) + 16)
                dve.wait_ge(x_new, GB * (GROUP_BASE[p] + g))
                half = 1 if p == L3_FF else 0
                row = gates[:, slot, half * D:(half + 1) * D].unsqueeze(1).to_broadcast([P, TPB, D])
                dve.tensor_tensor(upd[:, j, :].rearrange("p (k d) -> p k d", k=TPB),
                                  Y_BANKS[j][:, :].rearrange("p (k d) -> p k d", k=TPB), row,
                                  ALU.add if half else ALU.mult).then_inc(y_taken, 1)
            for j in range(GB):
                n = GB * (GROUP_BASE[p] + g) + j
                b = GB * g + j
                if p == L3_FF:
                    dve.wait_ge(gated2, n - GB * GROUP_BASE[L3_FF] + 1)
                    dve.tensor_tensor(xs(b), xs(b), act2[:, j, :], ALU.add).then_inc(x_new, 1)
                    continue
                dve.wait_ge(y_taken, n + 1)
                dve.wait_ge(xb_ready, n + 1)
                if p == L2_SSM:
                    dve.memset(spacer[:, 2 + j:3 + j], 0.0)
                    dve.tensor_copy(act2[:, j, :], xs(b))
                    dve.tensor_copy(mcur[:, j, :], maski[:, bass.ds(b * TPB, TPB)])
                    dve.tensor_tensor(upd[:, j, :], upd[:, j, :], xb[:, j, :], ALU.add).then_inc(x_tmp, 1)
                    dve.wait_ge(x_tmp, 2 * (GB * g + j) + 1)
                    dve.memset(spacer[:, 4 + j:5 + j], 0.0)
                    for k in range(TPB):
                        last = dve.copy_predicated(act2[:, j, k * D:(k + 1) * D],
                                                   mcur[:, j, k:k + 1].to_broadcast([P, D]),
                                                   upd[:, j, k * D:(k + 1) * D])
                    last.then_inc(x_tmp, 1)
                    dve.wait_ge(x_tmp, 2 * (GB * g + j) + 2)
                    dve.memset(spacer[:, 6 + j:7 + j], 0.0)
                    dve.tensor_copy(xs(b), act2[:, j, :]).then_inc(x_new, 1)
                else:
                    dve.tensor_tensor(xs(b), upd[:, j, :], xb[:, j, :], ALU.add).then_inc(x_new, 1)
            weights_hi(dve, p + 1, g)

        def ff_gpsimd(pool, p, g, i, last_group):
            C = HID[p] // P
            def hidden_lo(c):
                n = CHUNK_BASE[p] + C * g + c
                pool.wait_ge(h_hi, n + 1)
                pool.tensor_tensor(hl[c % 2][:, :], hf[c % 2][:, :], hh[c % 2][:, :].bitcast(F32),
                                   ALU.subtract).then_inc(h_lo, 1)
            if not last_group:
                ln_rsqrt(pool, p, GB * (g + 1))
            hidden_lo(0)
            if not last_group:
                ln_rsqrt(pool, p, GB * (g + 1) + 1)
            for c in range(1, C):
                hidden_lo(c)
            for j in range(GB):
                n = GB * (GROUP_BASE[p] + g) + j
                row = [gates[:, GB * i + j, h * D:(h + 1) * D].unsqueeze(1).to_broadcast([P, TPB, D])
                       for h in range(2)]
                pool.wait_ge(gate_loaded[GB * i + j], 8 * (GROUP_BASE[p] + g - i) + 16)
                if p == L3_FF:
                    m = n - GB * GROUP_BASE[p]
                    pool.wait_ge(gelu2, m + 1)
                    v = act2[:, j, :].rearrange("p (k d) -> p k d", k=TPB)
                    pool.tensor_tensor(v, v, row[0], ALU.mult).then_inc(gated2, 1)
                else:
                    pool.wait_ge(x_new, GB * (GROUP_BASE[p] + g))
                    pool.tensor_tensor(xb[:, j, :].rearrange("p (k d) -> p k d", k=TPB),
                                       xs(GB * g + j).rearrange("p (k d) -> p k d", k=TPB),
                                       row[1], ALU.add).then_inc(xb_ready, 1)
            weights_lo(pool, p + 1, g)

        def ff_sync(sp, p, g, i, last_group):
            for j in range(GB):
                if i or p:
                    sp.wait_ge(x_new, GB * (GROUP_BASE[p] + g) - GB)
                sp.dma_start(gates[:, GB * i + j, :],
                             gate_scratch[p, bass.ds(GB * g + j, 1), :].to_broadcast([P, 2 * D])
                             ).then_inc(gate_loaded[GB * i + j], 16)
            weights_load(sp, p + 1, g)
            if p == L3_FF:
                for j in range(GB):
                    b = GB * g + j
                    sp.wait_ge(x_new, GB * (GROUP_BASE[p] + g) + j + 1)
                    sp.dma_start(out[bass.ds(b, 1), :, :].rearrange("b (k p) d -> p (b k) d", p=P),
                                 xs(b).rearrange("p (k d) -> p k d", k=TPB)).then_inc(x_stored, 16)

        def ff_phase(eng, p, body):
            first = 0
            if p == 0:
                body(eng, p, 0, 0, False)
                body(eng, p, 1, 1, False)
                first = 1
            with eng.Fori(first, GROUPS // 2 - 1) as pair:
                body(eng, p, 2 * pair, 0, False)
                body(eng, p, 2 * pair + 1, 1, False)
            body(eng, p, GROUPS - 2, 0, False)
            body(eng, p, GROUPS - 1, 1, True)

        PROJ, SB_, PTB, OB, YB = bank[0:2], bank[2:4], bank[4], bank[5], bank[6]
        PROJ_AT = {0: ("qk", 2), 1: ("v", 1, 0), 2: ("qk", 3), 3: ("v", 1, 1), 4: ("qk", 4), 6: ("qk", 5),
                   8: ("qk", 6), 10: ("qk", 7), 12: ("qk", 0), 13: ("v", 0, 0), 14: ("qk", 1), 15: ("v", 0, 1)}
        PROJ_SLOTS = sorted(PROJ_AT)
        NPROJ = len(PROJ_AT)
        AHEAD = [s for s in PROJ_SLOTS if s >= 12]
        LN_SLOT = 11
        SCALE = float(DH) ** -0.5
        A = L1_ATTN

        def proj_tensor(pe, b, s):
            what = PROJ_AT[s]
            k = len(AHEAD) + NPROJ * b + PROJ_SLOTS.index(s)
            own = b + 1 if s >= 12 else b
            ring = PROJ[PROJ_SLOTS.index(s) % 2]
            (w, _), cols = w_tiles(A), what[1]
            pe.wait_ge(ln_lo, A * BATCH + own + 1)
            if not (isinstance(k, int) and k < 2):
                pe.wait_ge(proj_ev, k - 1)
            if what[0] == "qk":
                for h in range(2):
                    for c in range(DC):
                        col = h * INNER + cols * P
                        last = split3(pe, ring[:, h * SEQ:(h + 1) * SEQ], [v[:, c, col:col + P] for v in w],
                                      [m[:, c, :] for m in aT], c == 0, c == DC - 1)
            else:
                _, half, tile = what
                col = 2 * INNER + half * 512
                for c in range(DC):
                    last = split3(pe, ring[:, :], [m[:, c, tile * P:(tile + 1) * P] for m in aT],
                                  [v[:, c, col:col + 512] for v in w], c == 0, c == DC - 1)
            last.then_inc(proj_mm, 1)

        def item(b, s):
            what = PROJ_AT[s]
            own = b + 1 if s >= 12 else b
            return PAIRS * own + what[1] if what[0] == "qk" else 2 * TPB * own + 2 * what[1] + what[2]

        def early(n, k):
            return isinstance(n, int) and n < k

        def proj_scalar(act, b, s):
            what, n = PROJ_AT[s], item(b, s)
            k = len(AHEAD) + NPROJ * b + PROJ_SLOTS.index(s)
            act.wait_ge(proj_mm, k + 1)
            if what[0] == "qk":
                if not early(n, 2):
                    act.wait_ge(qk_lo, n - 1)
                dst = qkf[what[1] % 2]
            else:
                if not early(n, 1):
                    act.wait_ge(v_lo, n)
                dst = vf
            act.activation(dst[:, :], PROJ[PROJ_SLOTS.index(s) % 2][:, :], ACT.Copy).then_inc(proj_ev, 1)

        def v_slice(what):
            return [m[:, what[2], what[1] * 512:(what[1] + 1) * 512] for m in vv]

        def proj_vector(dve, b, s):
            what, n = PROJ_AT[s], item(b, s)
            k = len(AHEAD) + NPROJ * b + PROJ_SLOTS.index(s)
            dve.wait_ge(proj_ev, k + 1)
            if what[0] == "qk":
                i = what[1] % 2
                if not early(n, 2):
                    dve.wait_ge(s_mm, 2 * n - 2)
                dve.tensor_copy(qz[i][0][0:DH, 0:SEQ], qkf[i][0:DH, 0:SEQ])
                dve.tensor_copy(qz[i][0][DH:P, SEQ:2 * SEQ], qkf[i][DH:P, 0:SEQ])
                dve.tensor_copy(kk[i][0][:, :], qkf[i][:, SEQ:2 * SEQ]).then_inc(qk_hi, 1)
            else:
                own = b + 1 if s >= 12 else b
                if not early(own, 1):
                    dve.wait_ge(pv_mm, HEADS * (own - 1) + 8 * (what[1] + 1))
                dve.tensor_copy(v_slice(what)[0], vf[:, :]).then_inc(v_hi, 1)

        def proj_gpsimd(pool, b, s):
            what, n = PROJ_AT[s], item(b, s)
            if what[0] == "qk":
                i = what[1] % 2
                pool.wait_ge(qk_hi, n + 1)
                def lo(dst, src, hi):
                    return pool.tensor_tensor(dst, src, hi.bitcast(F32), ALU.subtract)
                lo(kk[i][1][:, :], qkf[i][:, SEQ:2 * SEQ], kk[i][0][:, :])
                lo(qz[i][1][0:DH, 0:SEQ], qkf[i][0:DH, 0:SEQ], qz[i][0][0:DH, 0:SEQ]).then_inc(pool_step, 1)
                pool.wait_ge(pool_step, 2 * n + 1)
                lo(qz[i][1][DH:P, SEQ:2 * SEQ], qkf[i][DH:P, 0:SEQ], qz[i][0][DH:P, SEQ:2 * SEQ]).then_inc(pool_step, 1)
                pool.wait_ge(pool_step, 2 * n + 2)
                pool.nop().then_inc(qk_lo, 1)
            else:
                pool.wait_ge(v_hi, n + 1)
                hi, lo = v_slice(what)
                pool.tensor_tensor(lo, vf[:, :], hi.bitcast(F32), ALU.subtract).then_inc(v_lo, 1)

        def scores(pe, H, h):
            i, j = h // 2 % 2, h % 2
            pe.wait_ge(qk_lo, PAIRS_OF(H, h) + 1)
            if not early(H, 2):
                pe.wait_ge(exp_ready, H - 1)
            for q in range(TPB):
                last = split3(pe, SB_[h % 2][:, q * SEQ:(q + 1) * SEQ],
                              [m[:, j * SEQ + q * P:j * SEQ + (q + 1) * P] for m in qz[i]],
                              [m[:, :] for m in kk[i]], True, True)
            last.then_inc(s_mm, 1)

        def PAIRS_OF(H, h):
            return H // 2 if isinstance(H, int) else (H_B[0] * PAIRS + h // 2)

        H_B = [0]

        def score_max(dve, H, src, i, scale, base):
            n = base + H
            dve.wait_ge(s_mm, n + 1)
            dve.tensor_reduce(smax[i][:, :], src.rearrange("p (q k) -> p q k", q=TPB), AX_X,
                              ALU.max).then_inc(max_ready, 1)
            dve.wait_ge(max_ready, n + 1)
            if not early(n, 2):
                dve.wait_ge(exp_ready, n - 1)
            dve.tensor_scalar(nmax[i][:, :], smax[i][:, :], -scale, None, ALU.mult).then_inc(nmax_ready, 1)

        def score_exp(act, H, src, i, dst, scale, base):
            n = base + H
            act.wait_ge(nmax_ready, n + 1)
            if not early(n, 2):
                act.wait_ge(pt_mm, n - 1)
                act.wait_ge(rinv_ready, n - 1)
            for q in range(TPB):
                last = act.activation(dst[:, q, :], src[:, q * SEQ:(q + 1) * SEQ], ACT.Exp, scale=scale,
                                      bias=nmax[i][:, q:q + 1], accum_out=rsum[i][:, q:q + 1])
            last.then_inc(exp_ready, 1)

        def prob_scale(dve, H, i, dst, base):
            n = base + H
            dve.wait_ge(exp_ready, n + 1)
            if not early(n, 2):
                dve.wait_ge(prob_ready, n - 1)
            dve.reciprocal(rinv[i][:, :], rsum[i][:, :]).then_inc(rinv_ready, 1)
            dve.wait_ge(rinv_ready, n + 1)
            for q in range(TPB):
                last = dve.tensor_scalar(dst[:, q, :], dst[:, q, :], rinv[i][:, q:q + 1], None, ALU.mult)
            last.then_inc(prob_ready, 1)

        def prob_transpose(pe, H, src, base):
            n = base + H
            pe.wait_ge(prob_ready, n + 1)
            if not early(n, 1):
                pe.wait_ge(pt_ev, n)
            for c in range(TPB):
                for q in range(TPB):
                    last = pe.transpose(PTB[:, c * SEQ + q * P:c * SEQ + (q + 1) * P],
                                        src[:, q, c * P:(c + 1) * P], ident[:, :])
            last.then_inc(pt_mm, 1)

        def pt_read(act, H, i, base):
            n = base + H
            act.wait_ge(pt_mm, n + 1)
            if not early(n, 2):
                act.wait_ge(pt_lo, n - 1)
            act.activation(ptf[i][:, :], PTB[:, :], ACT.Copy).then_inc(pt_ev, 1)

        def pt_split(dve, H, i, base):
            n = base + H
            dve.wait_ge(pt_ev, n + 1)
            if not early(n, 2):
                dve.wait_ge(pv_mm, n - 1)
            dve.tensor_copy(pt[i][0][:, :], ptf[i][:, :]).then_inc(pt_hi, 1)

        def pt_rest(pool, H, i, base):
            pool.wait_ge(pt_hi, base + H + 1)
            pool.tensor_tensor(pt[i][1][:, :], ptf[i][:, :], pt[i][0][:, :].bitcast(F32),
                               ALU.subtract).then_inc(pt_lo, 1)

        def head_values(pe, H, h, v_items):
            pe.wait_ge(pt_lo, H + 1)
            pe.wait_ge(v_lo, v_items)
            if not early(H, 1):
                pe.wait_ge(o_ev, H)
            for c in range(TPB):
                last = split3(pe, OB[0:DH, (h % 2) * SEQ:(h % 2 + 1) * SEQ],
                              [m[:, c, h * DH:(h + 1) * DH] for m in vv],
                              [m[:, c * SEQ:(c + 1) * SEQ] for m in pt[h % 2]], c == 0, c == TPB - 1)
            last.then_inc(pv_mm, 1)

        def o_read(act, H, h, pair):
            act.wait_ge(pv_mm, H + 1)
            if not early(pair, 2):
                act.wait_ge(o_lo, pair - 1)
            j, i = h % 2, h // 2 % 2
            act.activation(of[i][j * DH:(j + 1) * DH, :], OB[0:DH, j * SEQ:(j + 1) * SEQ],
                           ACT.Copy).then_inc(o_ev, 1)

        def o_split(dve, pair, i):
            dve.wait_ge(o_ev, 2 * pair + 2)
            if not early(pair, 2):
                dve.wait_ge(out_mm, pair - 1)
            dve.tensor_copy(oT[i][0][:, :], of[i][:, :]).then_inc(o_hi, 1)
            dve.wait_ge(o_hi, pair + 1)
            dve.tensor_tensor(oT[i][1][:, :], of[i][:, :], oT[i][0][:, :].bitcast(F32),
                              ALU.subtract).then_inc(o_lo, 1)

        def out_project(pe, pair, j, b):
            _, w2 = w_tiles(A)
            pe.wait_ge(o_lo, pair + 1)
            if j == 0 and not early(b, 1):
                pe.wait_ge(ay_taken, b)
            for r in range(TPB):
                last = split3(pe, YB[:, r * D:(r + 1) * D], [m[:, r * P:(r + 1) * P] for m in oT[j % 2]],
                              [w[:, j, :] for w in w2], j == 0 and r == 0, j == PAIRS - 1)
            last.then_inc(out_mm, 1)

        def res_vector(dve, p, b, src, done, count, n):
            dve.wait_ge(done, count)
            dve.wait_ge(agate_loaded, 16 * (n + 1))
            row = agate[:, 0:D].unsqueeze(1).to_broadcast([P, TPB, D])
            dve.tensor_tensor(aupd[:, :].rearrange("p (k d) -> p k d", k=TPB),
                              src[:, :].rearrange("p (k d) -> p k d", k=TPB), row, ALU.mult
                              ).then_inc(ay_taken, 1)
            dve.wait_ge(ay_taken, n + 1)
            dve.wait_ge(axb_ready, n + 1)
            dve.tensor_tensor(xs(b), aupd[:, :], axb[:, :], ALU.add).then_inc(ax_new, 1)

        def res_gpsimd(pool, b, n):
            pool.wait_ge(agate_loaded, 16 * (n + 1))
            if not early(n, 1):
                pool.wait_ge(ax_new, n)
            row = agate[:, D:2 * D].unsqueeze(1).to_broadcast([P, TPB, D])
            pool.tensor_tensor(axb[:, :].rearrange("p (k d) -> p k d", k=TPB),
                               xs(b).rearrange("p (k d) -> p k d", k=TPB), row, ALU.add
                               ).then_inc(axb_ready, 1)

        def gate_load(sp, p, b, n):
            if not early(n, 1):
                sp.wait_ge(ax_new, n)
            sp.dma_start(agate[:, :], gate_scratch[p, bass.ds(b, 1), :].to_broadcast([P, 2 * D])
                         ).then_inc(agate_loaded, 16)

        def mh_slots(b, first, last):
            for i in range(HEADS):
                def head(o):
                    h = i + o
                    if (h < 0 and first) or (h >= HEADS and last):
                        return None
                    return (HEADS * b + h, h % HEADS)
                yield i, head(2), head(0), head(-1), head(1)

        def mh_tensor(pe, b, first, last):
            for i, ahead, now, prev, _ in mh_slots(b, first, last):
                if i == LN_SLOT and not last:
                    ln_transpose(pe, A, b + 1)
                if i in PROJ_AT and not (last and i >= 12):
                    proj_tensor(pe, b, i)
                if ahead:
                    H_B[0] = b + 1 if i + 2 >= HEADS else b
                    scores(pe, *ahead)
                prob_transpose(pe, now[0], prob[i_prob(i)], 0)
                if prev:
                    own = b if i else b - 1
                    head_values(pe, *prev, 2 * TPB * own + (2 if prev[1] < 8 else 4))
                if i % 2 == 0 and (i >= 4 or not first):
                    j = (i // 2 - 2) % PAIRS
                    own = b if i >= 4 else b - 1
                    out_project(pe, PAIRS * own + j, j, own)
            if last:
                head_values(pe, HEADS * b + 15, 15, 2 * TPB * b + 4)
                out_project(pe, PAIRS * b + 6, 6, b)
                out_project(pe, PAIRS * b + 7, 7, b)

        def i_prob(i):
            return i % 2

        def mh_scalar(act, b, first, last):
            for i, ahead, now, prev, _ in mh_slots(b, first, last):
                if i == LN_SLOT and not last:
                    ln_modulate(act, A, b + 1)
                if i in PROJ_AT and not (last and i >= 12):
                    proj_scalar(act, b, i)
                if ahead:
                    score_exp(act, ahead[0], SB_[i % 2], i % 2, prob[i_prob(i)], SCALE, 0)
                pt_read(act, now[0], i % 2, 0)
                if prev:
                    own = b if i else b - 1
                    o_read(act, *prev, PAIRS * own + prev[1] // 2)
            if last:
                o_read(act, HEADS * b + 15, 15, PAIRS * b + 7)

        def mh_vector(dve, b, first, last):
            for i, ahead, now, prev, nxt in mh_slots(b, first, last):
                if nxt:
                    prob_scale(dve, nxt[0], (i + 1) % 2, prob[i_prob(i + 1)], 0)
                if i == 4 and not last:
                    ln_stats(dve, A, b + 1)
                if i == 6 and not last:
                    ln_norm(dve, A, b + 1)
                if i == LN_SLOT and not last:
                    dve.wait_ge(proj_mm, len(AHEAD) + NPROJ * b + PROJ_SLOTS.index(10) + 1)
                    ln_split(dve, A, b + 1, aT[0][:, :, :], aT[1][:, :, :])
                if ahead:
                    score_max(dve, ahead[0], SB_[i % 2][:, :], i % 2, SCALE, 0)
                if i in PROJ_AT and not (last and i >= 12):
                    proj_vector(dve, b, i)
                pt_split(dve, now[0], i % 2, 0)
                if i % 2 == 0 and prev:
                    own = b if i else b - 1
                    j = (i // 2 - 1) % PAIRS
                    o_split(dve, PAIRS * own + j, j % 2)
                if i == 3 and not first:
                    res_vector(dve, A, b - 1, YB, out_mm, PAIRS * b, b - 1)
                if i == 7:
                    weights_hi(dve, A + 1, b)
            if last:
                o_split(dve, PAIRS * b + 7, 1)
                res_vector(dve, A, b, YB, out_mm, PAIRS * b + PAIRS, b)

        def mh_gpsimd(pool, b, first, last):
            for i, ahead, now, prev, nxt in mh_slots(b, first, last):
                if i in PROJ_AT and not (last and i >= 12):
                    proj_gpsimd(pool, b, i)
                pt_rest(pool, now[0], i % 2, 0)
                if i == 5 and not last:
                    ln_rsqrt(pool, A, b + 1)
                if i == 7:
                    weights_lo(pool, A + 1, b)
                if i == 9:
                    res_gpsimd(pool, b, b)

        def mh_sync(sp, b, first, last):
            gate_load(sp, A, b, b)
            weights_load(sp, A + 1, b)

        def mh_start(name, eng):
            if name == "tensor":
                ln_transpose(eng, A, 0)
            if name == "scalar":
                ln_modulate(eng, A, 0)
            if name == "vector":
                eng.memset(qz[0][0][:, :].bitcast(F32), 0.0)
                eng.memset(qz[0][1][:, :].bitcast(F32), 0.0)
                eng.memset(qz[1][0][:, :].bitcast(F32), 0.0)
                eng.memset(qz[1][1][:, :].bitcast(F32), 0.0).then_inc(zeros, 1)
                eng.wait_ge(zeros, 1)
                ln_stats(eng, A, 0)
                ln_norm(eng, A, 0)
                ln_split(eng, A, 0, aT[0][:, :, :], aT[1][:, :, :])
            if name == "gpsimd":
                ln_rsqrt(eng, A, 0)
            f = {"tensor": proj_tensor, "scalar": proj_scalar, "vector": proj_vector, "gpsimd": proj_gpsimd}
            for s in AHEAD:
                f[name](eng, -1, s)
            for h in range(2):
                if name == "tensor":
                    scores(eng, h, h)
                if name == "vector":
                    score_max(eng, h, SB_[h][:, :], h, SCALE, 0)
                if name == "scalar":
                    score_exp(eng, h, SB_[h], h, prob[h], SCALE, 0)
            if name == "vector":
                prob_scale(eng, 0, 0, prob[0], 0)

        def att_phase(eng, body):
            body(eng, 0, True, False)
            with eng.Fori(1, BATCH - 1) as b:
                body(eng, b, False, False)
            body(eng, BATCH - 1, False, True)

        QB, KB, VB, S1, PT1, O1 = bank[0], bank[1], bank[2], bank[3], PTB, bank[5]
        S6 = L3_ATTN
        SCALE1 = float(D) ** -0.5
        H0 = HEADS * BATCH
        qk1, kk1, vv1 = qz[0], [qz[1][0], qz[1][1]], [m[:, 0, 0:512] for m in vv]
        kf1 = qkf[1]

        def sh_qk(pe, b, which):
            (w, _) = w_tiles(S6)
            pe.wait_ge(ln_lo, S6 * BATCH + b + 1)
            B, ev, s = ((QB, q_ev, b_q), (KB, k_ev, b_k))[which]
            if not early(b, 1):
                pe.wait_ge(ev, b)
            for m in range(DC):
                for c in range(DC):
                    col = which * D + m * P
                    last = split3(pe, B[:, m * SEQ:(m + 1) * SEQ], [v[:, c, col:col + P] for v in w],
                                  [a[:, c, :] for a in aT], c == 0, c == DC - 1)
            last.then_inc(s, 1)

        def sh_v(pe, b):
            (w, _) = w_tiles(S6)
            if not early(b, 1):
                pe.wait_ge(v_ev, b)
            for r in range(TPB):
                for c in range(DC):
                    last = split3(pe, VB[:, r * D:(r + 1) * D], [a[:, c, r * P:(r + 1) * P] for a in aT],
                                  [v[:, c, 2 * D:3 * D] for v in w], c == 0, c == DC - 1)
            last.then_inc(b_v, 1)

        def sh_scores(pe, b):
            pe.wait_ge(q_lo, b + 1)
            pe.wait_ge(k_lo, b + 1)
            pe.wait_ge(exp_ready, H0 + b)
            for q in range(TPB):
                for c in range(DC):
                    last = split3(pe, S1[:, q * SEQ:(q + 1) * SEQ],
                                  [m[:, c * SEQ + q * P:c * SEQ + (q + 1) * P] for m in qk1],
                                  [m[:, c * SEQ:(c + 1) * SEQ] for m in kk1], c == 0, c == DC - 1)
            last.then_inc(s_mm, 1)

        def sh_values(pe, b):
            pe.wait_ge(pt_lo, H0 + b + 1)
            pe.wait_ge(v_lo, 2 * TPB * BATCH + b + 1)
            pe.wait_ge(ay_taken, BATCH + b)
            for q in range(TPB):
                for c in range(TPB):
                    last = split3(pe, O1[:, q * D:(q + 1) * D],
                                  [m[:, c * SEQ + q * P:c * SEQ + (q + 1) * P] for m in pt[0]],
                                  [m[:, c * D:(c + 1) * D] for m in vv1], c == 0, c == TPB - 1)
            last.then_inc(pv_mm, 1)

        def sh_tensor(pe, b, first, last):
            sh_qk(pe, b, 0)
            sh_qk(pe, b, 1)
            if not first:
                prob_transpose(pe, b - 1, prob[0], H0)
            sh_v(pe, b)
            if not first:
                sh_values(pe, b - 1)
            sh_scores(pe, b)
            if last:
                prob_transpose(pe, b, prob[0], H0)
                sh_values(pe, b)
            else:
                ln_transpose(pe, S6, b + 1)

        def sh_scalar(act, b, first, last):
            for B, dst, mm, lo, ev, at in ((QB, qkf[0], b_q, q_lo, q_ev, 0), (KB, kf1, b_k, k_lo, k_ev, DC)):
                act.wait_ge(mm, b + 1)
                if not early(b, 1):
                    act.wait_ge(lo, b)
                for m in range(DC):
                    n = BIAS_AT[S6] + at + m
                    l = act.activation(dst[:, m * SEQ:(m + 1) * SEQ], B[:, m * SEQ:(m + 1) * SEQ],
                                       ACT.Identity, bias=biases[:, n:n + 1])
                l.then_inc(ev, 1)
            if not first:
                pt_read(act, b - 1, 0, H0)
            act.wait_ge(b_v, b + 1)
            act.wait_ge(v_lo, 2 * TPB * BATCH + b)
            act.activation(vf[:, :], VB[:, :], ACT.Copy).then_inc(v_ev, 1)
            score_exp(act, b, S1, 0, prob[0], SCALE1, H0)
            if last:
                pt_read(act, b, 0, H0)
            else:
                ln_modulate(act, S6, b + 1)

        def sh_vector(dve, b, first, last):
            for src, dst, ev, hi, s in ((qkf[0], qk1, q_ev, q_hi, 0), (kf1, kk1, k_ev, k_hi, 1)):
                dve.wait_ge(ev, b + 1)
                dve.wait_ge(s_mm, H0 + b)
                dve.tensor_copy(dst[0][:, :], src[:, :]).then_inc(hi, 1)
            if not first:
                pt_split(dve, b - 1, 0, H0)
            if not last:
                ln_stats(dve, S6, b + 1)
            dve.wait_ge(v_ev, b + 1)
            dve.wait_ge(pv_mm, H0 + b)
            dve.tensor_copy(vv1[0], vf[:, :]).then_inc(v_hi, 1)
            if not last:
                ln_norm(dve, S6, b + 1)
            score_max(dve, b, S1[:, :], 0, SCALE1, H0)
            if not first:
                res_vector(dve, S6, b - 1, O1, pv_mm, H0 + b, BATCH + b - 1)
            prob_scale(dve, b, 0, prob[0], H0)
            if not last:
                dve.wait_ge(b_v, b + 1)
                ln_split(dve, S6, b + 1, aT[0][:, :, :], aT[1][:, :, :])
            weights_hi(dve, S6 + 1, b)
            if last:
                pt_split(dve, b, 0, H0)
                res_vector(dve, S6, b, O1, pv_mm, H0 + b + 1, BATCH + b)

        def sh_gpsimd(pool, b, first, last):
            for src, dst, hi, lo in ((qkf[0], qk1, q_hi, q_lo), (kf1, kk1, k_hi, k_lo)):
                pool.wait_ge(hi, b + 1)
                pool.tensor_tensor(dst[1][:, :], src[:, :], dst[0][:, :].bitcast(F32), ALU.subtract
                                   ).then_inc(lo, 1)
            if not first:
                pt_rest(pool, b - 1, 0, H0)
            if not last:
                ln_rsqrt(pool, S6, b + 1)
            pool.wait_ge(v_hi, 2 * TPB * BATCH + b + 1)
            pool.tensor_tensor(vv1[1], vf[:, :], vv1[0].bitcast(F32), ALU.subtract).then_inc(v_lo, 1)
            res_gpsimd(pool, b, BATCH + b)
            weights_lo(pool, S6 + 1, b)
            if last:
                pt_rest(pool, b, 0, H0)

        def sh_sync(sp, b, first, last):
            gate_load(sp, S6, b, BATCH + b)
            weights_load(sp, S6 + 1, b)

        block = ctx.enter_context(nc.Block())

        def program(eng, name, ff_body, mh_body, sh_body, signs=True):
            for p in range(NPH):
                if p == L1_ATTN:
                    if name != "sync":
                        mh_start(name, eng)
                    att_phase(eng, mh_body)
                elif p == L3_ATTN:
                    ln_first(name, eng, p, 1)
                    att_phase(eng, sh_body)
                else:
                    ln_first(name, eng, p, GB)
                    ff_phase(eng, p, ff_body)
                if p < NPH - 1:
                    end_phase(eng, p, signs)

        def ln_first(name, eng, p, n):
            for b in range(n):
                if name == "tensor":
                    ln_transpose(eng, p, b)
                if name == "scalar":
                    ln_modulate(eng, p, b)
                if name == "gpsimd":
                    ln_rsqrt(eng, p, b)
                if name == "vector":
                    ln_stats(eng, p, b)
                    ln_norm(eng, p, b)
                    dst = [m[:, :, b * SEQ:(b + 1) * SEQ] for m in nT[0]] if p in HID else [m[:, :, :] for m in aT]
                    ln_split(eng, p, b, *dst)

        cond_srcs = [(condrows[n * NC:(n + 1) * NC, :], t[name].rearrange("b (k p) -> (b k) p", p=P))
                     for n, name in enumerate(("cond_1024", "fside_BxS_0"))]
        cond_srcs.append((mask8[2 * NC:3 * NC, :], t["mask_BxS_bk0"].rearrange("b (k p) -> (b k) p", p=P)))
        at = 0
        for v in VEC_SRC:
            k = v.shape[0] // P
            cond_srcs.append((vecrows[at:at + k, :], v.rearrange("(c p) -> c p", p=P)))
            at += k
        for n, (w, _, _) in enumerate(ADA):
            cond_srcs.append((adaw[n][:, :, :], t[w].rearrange("(k p) m -> p k m", p=P)))
        for p, (m, _, _, ga, b2) in enumerate(COND):
            cond_srcs.append((growb[:, p, :], t[ADA[m][1]][ga * D:(ga + 1) * D].partition_broadcast(BATCH)))
            cond_srcs.append((b2row[:, p, :], t[b2].partition_broadcast(BATCH)))
        cond_srcs.append((bwdrow[:, :], t["L2_cond_bwd_b2"].partition_broadcast(BATCH)))
        N_COND = 16 * len(cond_srcs)

        @block.sync
        def _(sp):
            weights_load(sp, 0, 0)
            for dst, src in cond_srcs[0::2]:
                sp.dma_start(dst, src).then_inc(pro_loads, 16)
            sp.dma_start(x[:, :].rearrange("p (n d) -> p n d", d=D),
                         t["x"].rearrange("b (k p) d -> p (b k) d", p=P)).then_inc(x_loaded, 16)
            sp.wait_ge(gate_rows, 1)
            sp.dma_start(gate_scratch.rearrange("q b n -> b q n"),
                         grow[:, :, :, :].rearrange("b q h n -> b q (h n)")).then_inc(gates_stored, 16)
            sp.wait_ge(gates_stored, 16)
            end_phase(sp, -1, False)
            program(sp, "sync", ff_sync, mh_sync, sh_sync, signs=False)
            sp.wait_ge(x_stored, 16 * BATCH)

        @block.scalar
        def _(act):
            for dst, src in cond_srcs[1::2]:
                act.dma_start(dst, src).then_inc(pro_loads, 16)
            act.wait_ge(cond_cols, 1)
            act.activation(siluT[:, :, :], condT[:, 0, :, :], ACT.Silu).then_inc(silu_ready, 1)
            end_phase(act, -1)
            program(act, "scalar", ff_scalar, mh_scalar, sh_scalar)

        @block.tensor
        def _(pe):
            pe.wait_ge(pro_loads, N_COND)
            pe.wait_ge(consts, 1)
            pe.wait_ge(mask_rows, 1)
            pe.transpose(bank[5][:, 0:3 * NC], condrows[:, :], ident[0:3 * NC, 0:3 * NC])
            pe.transpose(bank[6][:, 0:NVEC], vecrows[:, :], ident[0:NVEC, 0:NVEC]).then_inc(cond_tp, 1)
            pe.wait_ge(silu_ready, 1)
            pe.wait_ge(cond_cols, 1)
            for p, (m, sh, sc, ga, _) in enumerate(COND):
                if ADA[m][2]:
                    src = [condT[:, 1, :, k] for k in range(DC)] + [condT[:, 0, :, k] for k in range(DC)]
                else:
                    src = [siluT[:, :, k] for k in range(DC)]
                for s, sec in enumerate((sc, sh)):
                    for c in range(DC):
                        at = ((p * 2 + s) * DC + c) * BATCH
                        for k in range(kcs[m]):
                            last = pe.matmul(bank[0][:, at:at + BATCH],
                                             adaw[m][:, k, sec * D + c * P:sec * D + (c + 1) * P],
                                             src[k], start=k == 0, stop=k == kcs[m] - 1)
                for k in range(kcs[m]):
                    last = pe.matmul(bank[1 + p // 2][0:BATCH, (p % 2) * D:(p % 2 + 1) * D], src[k],
                                     adaw[m][:, k, ga * D:(ga + 1) * D], start=k == 0, stop=k == kcs[m] - 1)
            last.then_inc(mod_mm, 1)
            end_phase(pe, -1)
            program(pe, "tensor", ff_tensor, mh_tensor, sh_tensor)

        @block.vector
        def _(dve):
            step = [0]

            def then(ins):
                step[0] += 1
                ins.then_inc(mod_step, 1)
                dve.wait_ge(mod_step, step[0])

            weights_hi(dve, 0, 0)
            dve.memset(mhalf[:, :], -0.5)
            dve.wait_ge(pro_loads, N_COND)
            dve.tensor_copy(condrows[2 * NC:3 * NC, :], mask8[2 * NC:3 * NC, :]).then_inc(mask_rows, 1)
            dve.wait_ge(cond_tp, 1)
            dve.tensor_copy(condT[:, :, :, :].rearrange("p a b k -> p (a b k)"), bank[5][:, 0:2 * NC])
            dve.tensor_copy(maski[:, :], bank[5][:, 2 * NC:3 * NC])
            dve.tensor_copy(vecs[:, :], bank[6][:, 0:NVEC]).then_inc(cond_cols, 1)
            dve.wait_ge(cond_cols, 1)
            dve.wait_ge(mod_mm, 1)
            tform = bank[0][:, :].rearrange("p (q s c b) -> p q s c b", q=NPH, s=2, c=DC)
            for p in range(NPH):
                for c in range(DC):
                    own = (mod[:, p, 0, c, :], mod[:, p, 1, c, :])
                    if p >= L3_ATTN:
                        own = (gain[:, p - L3_ATTN, c, :], be[:, p - L3_ATTN, c, :])
                    dve.tensor_scalar(own[0], tform[:, p, 0, c, :], vecs[:, ADAB_AT[p, 0] + c:ADAB_AT[p, 0] + c + 1], 1.0, ALU.add, ALU.add)
                    last = dve.tensor_scalar(own[1], tform[:, p, 1, c, :], vecs[:, ADAB_AT[p, 1] + c:ADAB_AT[p, 1] + c + 1], None, ALU.add)
            dve.tensor_tensor(b2row[:, L2_SSM, :], b2row[:, L2_SSM, :], bwdrow[:, :], ALU.add)
            for p in range(NPH):
                last = dve.tensor_tensor(grow[:, p, 0, :], bank[1 + p // 2][0:BATCH, (p % 2) * D:(p % 2 + 1) * D],
                                         growb[:, p, :], ALU.add)
            then(last)
            for j in range(2):
                for c in range(DC):
                    dve.tensor_scalar(mod[:, L3_ATTN + j, 0, c, :], gain[:, j, c, :], vecs[:, LN_AT["g", j] + c:LN_AT["g", j] + c + 1], None, ALU.mult)
                    dve.scalar_tensor_tensor(mod[:, L3_ATTN + j, 1, c, :], gain[:, j, c, :], vecs[:, LN_AT["b", j] + c:LN_AT["b", j] + c + 1],
                                             be[:, j, c, :], ALU.mult, ALU.add)
            dve.tensor_tensor(grow[:, 0:L3_FF, 1, :], grow[:, 0:L3_FF, 0, :], b2row[:, 0:L3_FF, :], ALU.mult)
            dve.tensor_copy(grow[:, L3_FF, 1, :], b2row[:, L3_FF, :]).then_inc(gate_rows, 1)
            dve.wait_ge(x_loaded, 16)
            end_phase(dve, -1)
            program(dve, "vector", ff_vector, mh_vector, sh_vector)

        @block.gpsimd
        def _(pool):
            pool.memset(ident[:, :], 0.0).then_inc(ident_zero, 1)
            pool.wait_ge(ident_zero, 1)
            pool.affine_select(out=ident[:, :], in_=ident[:, :], compare_op=ALU.not_equal, fill=1.0, base=0,
                               pattern=[[-1, P]], channel_multiplier=1).then_inc(consts, 1)
            weights_lo(pool, 0, 0)
            end_phase(pool, -1)
            program(pool, "gpsimd", ff_gpsimd, mh_gpsimd, sh_gpsimd)


def kernel(**inputs):
    import numpy as _np
    import concourse.bacc as _bacc
    from concourse import mybir as _mybir
    from concourse.bass_utils import run_bass_kernel_spmd as _run

    nc = _bacc.Bacc("TRN2", target_bir_lowering=False, num_devices=1)
    arrays, aps = {}, {}
    for name, value in inputs.items():
        a = _np.ascontiguousarray(value)
        arrays[f"in_{name}"] = a
        aps[name] = nc.dram_tensor(f"in_{name}", a.shape, _mybir.dt.from_np(a.dtype), kind="ExternalInput").ap()
    out = nc.dram_tensor("out", (BATCH, SEQ, D), F32, kind="ExternalOutput").ap()
    bass_cond_blocks(nc, aps, out)
    r = _run(nc, [arrays], core_ids=[0])
    return r.results[0]["out"]
```

```python
from contextlib import ExitStack

import concourse.bass as bass
from concourse import mybir

ALU = mybir.AluOpType
ACT = mybir.ActivationFunctionType
F32 = mybir.dt.float32
F32R = mybir.dt.float32r
I32 = mybir.dt.int32
U8 = mybir.dt.uint8
AX_X = mybir.AxisListType.X

P = 128
BATCH, SEQ, D = 16, 256, 256
TPB = SEQ // P
DC = D // P
ROWW = TPB * D
HEADS, DH = 16, 64
INNER = HEADS * DH
PAIRS = HEADS // 2
GB = 2
GROUPS = BATCH // GB
GW = GB * SEQ
NPH = 8
L1_ATTN, L2_SSM, L3_ATTN, L3_FF = 2, 4, 6, 7

HID = {0: 256, 1: 512, 3: 1024, 4: 512, 5: 512, 7: 1024}
ACTF = {0: ACT.Gelu, 1: ACT.Gelu_apprx_tanh, 3: ACT.Gelu, 4: ACT.Gelu, 5: ACT.Gelu_apprx_tanh, 7: ACT.Gelu}
EPS = [1e-6, 1e-6, 1e-5, 1e-5, 1e-6, 1e-6, 1e-5, 1e-5]


def bass_cond_blocks(nc, t, out):
    def two(w1, w2):
        return [(t[w1], "w1", 0, 0), (t[w2], "w2", 0, 0)]

    PARTS = {
        0: two("L0_cond_ssm_w1", "L0_cond_ssm_w2"),
        1: two("L0_cond_ff_w1", "L0_cond_ff_w2"),
        2: two("L1_cond_W_qkv", "L1_cond_W_out"),
        3: two("L1_cond_W1", "L1_cond_W2"),
        4: [(t["L2_cond_ssm_w1"], "w1", 0, 0), (t["L2_cond_bwd_w1"], "w1", 0, 256),
            (t["L2_cond_ssm_w2"], "w2", 0, 0), (t["L2_cond_bwd_w2"], "w2", 2, 0)],
        5: two("L2_cond_ff_w1", "L2_cond_ff_w2"),
        6: [(t["L3_cond_Wq"], "w1", 0, 0), (t["L3_cond_Wk"], "w1", 0, 256), (t["L3_cond_Wv"], "w1", 0, 512)],
        7: two("L3_cond_W1", "L3_cond_W2"),
    }
    W1_COLS = {**HID, 2: 3 * INNER, 6: 3 * D}
    W2_CHUNKS = {**{p: h // P for p, h in HID.items()}, 2: INNER // P, 6: 0}
    SLICES = [1] + [GROUPS if p - 1 in HID else BATCH for p in range(1, NPH)]
    SLICE_BASE = [sum(SLICES[:p]) for p in range(NPH + 1)]
    LOAD_BASE = [sum(16 * len(PARTS[q]) * SLICES[q] for q in range(p)) for p in range(NPH + 1)]

    ADA = [("L0_cond_ada_w", "L0_cond_ada_b", 0), ("L1_cond_W_mod", "L1_cond_b_mod", 0),
           ("L2_cond_ada_w", "L2_cond_ada_b", 0), ("L2_cond_ffada_w", "L2_cond_ffada_b", 0),
           ("L3_cond_Wc", "L3_cond_bc", 1)]
    COND = [(0, 0, 1, 2, "L0_cond_ssm_b2"), (0, 3, 4, 5, "L0_cond_ff_b2"),
            (1, 0, 1, 2, "L1_cond_b_out"), (1, 3, 4, 5, "L1_cond_b2"),
            (2, 0, 1, 2, "L2_cond_ssm_b2"), (3, 0, 1, 2, "L2_cond_ff_b2"),
            (4, 2, 1, 0, "L3_cond_bv"), (4, 5, 4, 3, "L3_cond_b2")]
    BIASES = {0: ["L0_cond_ssm_b1"], 1: ["L0_cond_ff_b1"], 3: ["L1_cond_b1"],
              4: ["L2_cond_ssm_b1", "L2_cond_bwd_b1"], 5: ["L2_cond_ff_b1"],
              6: ["L3_cond_bq", "L3_cond_bk"], 7: ["L3_cond_b1"]}
    VEC_SRC, BIAS_AT, LN_AT = [], {}, {}

    def vec_rows(src):
        at = sum(v.shape[0] // P for v in VEC_SRC)
        VEC_SRC.append(src)
        return at
    for p, names in BIASES.items():
        BIAS_AT[p] = [vec_rows(t[n]) for n in names][0]
    for j in range(2):
        for v in "gb":
            LN_AT[v, j] = vec_rows(t[f"L3_cond_ln{j + 1}_{v}"])
    NVEC = sum(v.shape[0] // P for v in VEC_SRC)
    NC = BATCH * DC

    def before(per):
        return [sum(per(q) for q in range(p)) for p in range(NPH + 1)]
    CHUNK_BASE = before(lambda q: GROUPS * HID[q] // P if q in HID else 0)
    GROUP_BASE = before(lambda q: GROUPS if q in HID else 0)

    gate_scratch = nc.dram_tensor("gate_scratch", (NPH, BATCH, 2 * D), F32).ap()

    ctx = ExitStack()
    with ctx:
        def sb(name, shape, dt=F32, scope=ctx):
            return scope.enter_context(nc.sbuf_tensor(name, shape, dt))

        def sem(name):
            return ctx.enter_context(nc.semaphore(name))

        x = sb("x", [P, BATCH * ROWW])
        stage = sb("stage", [P, 1024])
        mod = sb("mod", [P, NPH, 2, DC, BATCH])
        vecs = sb("vecs", [P, NVEC])
        ident = sb("ident", [P, P])
        maski = sb("maski", [P, BATCH * TPB], I32)
        spacer = sb("spacer", [P, 8])
        mcur = sb("mcur", [P, GB, TPB], I32)
        stats = [sb(f"stats{j}", [P, TPB, 6]) for j in range(GB)]
        meanvar = [sb(f"meanvar{j}", [P, TPB, 2]) for j in range(GB)]
        vareps = [sb(f"vareps{j}", [P, TPB]) for j in range(GB)]
        rstd = [sb(f"rstd{j}", [P, TPB]) for j in range(GB)]
        mhalf = sb("mhalf", [P, TPB])
        xn = [sb(f"xn{j}", [P, ROWW]) for j in range(GB)]
        nf = [sb(f"nf{j}", [P, ROWW]) for j in range(GB)]

        pro = ExitStack()
        kcs = [t[w].shape[0] // P for w, _, _ in ADA]
        widths = [t[w].shape[1] for w, _, _ in ADA]
        adaw = [sb("adaw0", [P, kcs[0], widths[0]], scope=pro)]
        condrows = sb("condrows", [3 * NC, P], scope=pro)
        mask8 = sb("mask8", [3 * NC, P], U8, scope=pro)
        vecrows = sb("vecrows", [NVEC, P], scope=pro)
        pro.close()

        ffn = ExitStack()
        nT = [[sb(f"nT{k}_{i}", [P, DC, GW], F32R, ffn) for k in ("hi", "lo")] for i in range(2)]
        HRING = 4
        hf = [sb(f"hf{i}", [P, GW], scope=ffn) for i in range(HRING)]
        hh = [sb(f"hh{i}", [P, GW], F32R, ffn) for i in range(HRING)]
        hl = [sb(f"hl{i}", [P, GW], F32R, ffn) for i in range(HRING)]
        xb = sb("xb", [P, GB, ROWW], scope=ffn)
        upd = sb("upd", [P, GB, ROWW], scope=ffn)
        act2 = sb("act2", [P, GB, ROWW], scope=ffn)
        gates = sb("gates", [P, 2 * GB, 2 * D], scope=ffn)
        ffn.close()

        att = ctx
        aT = [sb(f"aT{k}", [P, DC, SEQ], F32R, att) for k in ("hi", "lo")]
        qkf = [sb(f"qkf{i}", [P, 2 * SEQ], scope=att) for i in range(2)]
        qz = [[sb(f"qz{k}{i}", [P, 2 * SEQ], F32R, att) for k in ("hi", "lo")] for i in range(2)]
        kk = [[sb(f"kk{k}{i}", [P, SEQ], F32R, att) for k in ("hi", "lo")] for i in range(2)]
        vf = sb("vf", [P, 512], scope=att)
        vv = [sb(f"v{k}", [P, TPB, INNER], F32R, att) for k in ("hi", "lo")]
        prob = [sb(f"prob{i}", [P, TPB, SEQ], scope=att) for i in range(2)]
        pt = [[sb(f"pt{k}{i}", [P, 2 * SEQ], F32R, att) for k in ("hi", "lo")] for i in range(2)]
        of = [sb(f"of{i}", [P, SEQ], scope=att) for i in range(2)]
        oT = [[sb(f"oT{k}{i}", [P, SEQ], F32R, att) for k in ("hi", "lo")] for i in range(2)]
        axb = sb("axb", [P, ROWW], scope=att)
        aupd = sb("aupd", [P, ROWW], scope=att)
        agate = sb("agate", [P, 2 * D], scope=att)
        smax = [sb(f"smax{i}", [P, TPB], scope=att) for i in range(2)]
        nmax = [sb(f"nmax{i}", [P, TPB], scope=att) for i in range(2)]
        rsum = [sb(f"rsum{i}", [P, TPB], scope=att) for i in range(2)]
        rinv = [sb(f"rinv{i}", [P, TPB], scope=att) for i in range(2)]
        front_a, front_b = DC * HID[0] + HID[0] // P * D, DC * HID[1] + HID[1] // P * D

        def weight_tile(name, words, front, others):
            scope = ExitStack()
            sb(f"{name}_front", [P, front], scope=scope)
            made = [sb(n, shape, scope=scope) for n, shape in others]
            scope.close()
            return sb(name, [P, words], F32R), made

        wahi, m = weight_tile("WAhi", 8192, front_a, [(f"adaw{n}", [P, kcs[n], widths[n]]) for n in (1, 2, 3)])
        adaw += m
        walo, m = weight_tile("WAlo", 8192, front_a, [("adaw4", [P, kcs[4], widths[4]])])
        adaw += m
        wbhi, (crow, gbrow) = weight_tile("WBhi", 4096, front_b,
                                          [("crow", [BATCH, 6 * D]),
                                           ("gbrow", [BATCH, 2 * D])])
        wblo, (abrow, b2row) = weight_tile("WBlo", 4096, front_b,
                                           [("abrow", [BATCH, 6 * D]),
                                            ("b2row", [BATCH, 2 * D])])
        WA, WB = [wahi, walo], [wbhi, wblo]
        bwdrow = sb("bwdrow", [BATCH, D])
        condT = sb("condT", [P, 2, BATCH, DC])
        siluT = sb("siluT", [P, BATCH, DC])
        gain = sb("gain", [P, 2, DC, BATCH])
        be = sb("be", [P, 2, DC, BATCH])

        bank = [ctx.enter_context(nc.psum_tensor(f"bank{i}", [P, 512], F32)) for i in range(8)]
        T_BANKS = [bank[7], bank[6]]
        C_BANK = bank[6]

        def w_tiles(p):
            W = WA if p % 2 == 0 else WB
            n1 = DC * W1_COLS[p]
            v1 = [w[:, 0:n1].rearrange("p (k m) -> p k m", k=DC) for w in W]
            if not W2_CHUNKS[p]:
                return v1, None
            v2 = [w[:, n1:n1 + W2_CHUNKS[p] * D].rearrange("p (k m) -> p k m", m=D) for w in W]
            return v1, v2

        pro_loads = sem("pro_loads"); x_loaded = sem("x_loaded"); mask_rows = sem("mask_rows"); cond_tp = sem("cond_tp"); cond_cols = sem("cond_cols")
        consts = sem("consts"); ident_zero = sem("ident_zero"); silu_ready = sem("silu_ready"); x_rest = sem("x_rest")
        c_loaded = sem("c_loaded"); c_mm = sem("c_mm"); c_done = sem("c_done"); c_stored = sem("c_stored")
        c_step = sem("c_step"); ada_loaded = [sem(f"ada_loaded{m}") for m in range(len(ADA))]
        w_loaded = sem("w_loaded"); w_hi = sem("w_hi"); w_lo = sem("w_lo")
        phase_end = sem("phase_end")
        gate_loaded = [sem(f"gate_loaded{i}") for i in range(2 * GB)]
        ln_stats_s = sem("ln_stats"); ln_mv = sem("ln_mv"); ln_ve = sem("ln_ve"); ln_rstd = sem("ln_rstd")
        ln_xn = sem("ln_xn"); ln_tp = sem("ln_tp"); ln_nf = sem("ln_nf"); ln_lo = sem("ln_lo")
        u_mm = sem("u_mm"); h_act = sem("h_act"); h_lo = sem("h_lo")
        w2_mm = sem("w2_mm"); y_taken = sem("y_taken"); xb_ready = sem("xb_ready");
        gelu2 = sem("gelu2"); gated2 = sem("gated2")
        x_new = sem("x_new"); x_tmp = sem("x_tmp"); x_stored = sem("x_stored")
        zeros = sem("zeros")
        proj_mm = sem("proj_mm"); proj_ev = sem("proj_ev"); qk_hi = sem("qk_hi"); qk_lo = sem("qk_lo")
        v_hi = sem("v_hi"); v_lo = sem("v_lo"); s_mm = sem("s_mm"); max_ready = sem("max_ready")
        nmax_ready = sem("nmax_ready"); pool_step = sem("pool_step"); exp_ready = sem("exp_ready"); rinv_ready = sem("rinv_ready")
        prob_ready = sem("prob_ready"); prob_ready1 = sem("prob_ready1"); pt_mm = sem("pt_mm"); pt_hi = sem("pt_hi")
        pt_lo = sem("pt_lo"); pv_mm = sem("pv_mm"); o_ev = sem("o_ev"); o_hi = sem("o_hi"); o_lo = sem("o_lo")
        out_mm = sem("out_mm"); ay_taken = sem("ay_taken"); axb_ready = sem("axb_ready")
        aupd_ready = sem("aupd_ready"); ax_new = sem("ax_new"); agate_loaded = sem("agate_loaded")
        b_q = sem("b_q"); b_k = sem("b_k"); b_v = sem("b_v")
        q_hi = sem("q_hi"); q_lo = sem("q_lo"); k_hi = sem("k_hi"); k_lo = sem("k_lo")

        ENGINES = 4

        def end_phase(eng, p, signs=True):
            if signs:
                eng.drain().then_inc(phase_end, 1)
            eng.wait_ge(phase_end, ENGINES * (p + 2))

        def xs(b):
            return x[:, bass.ds(b * ROWW, ROWW)]

        def split3(pe, dst, lhs, rhs, start, stop):
            pe.matmul(dst, lhs[1], rhs[0], start=start, stop=False, skip_group_check=True)
            pe.matmul(dst, lhs[0], rhs[1], start=False, stop=False, skip_group_check=True)
            return pe.matmul(dst, lhs[0], rhs[0], start=False, stop=stop, skip_group_check=True)

        def slice_views(p, s):
            n, at, views = SLICES[p], 0, []
            for w, which, k0, m0 in PARTS[p]:
                kc, m = w.shape[0] // P, w.shape[1]
                ms = m // n
                src = w.rearrange("(k p) m -> p k m", p=P)[:, :, bass.ds(s * ms, ms)]
                st = stage[:, at:at + kc * ms].rearrange("p (k m) -> p k m", k=kc)
                tiles = w_tiles(p)[0 if which == "w1" else 1]
                hi, lo = (v[:, k0:k0 + kc, bass.ds(s * ms + m0, ms)] for v in tiles)
                views.append((src, st, hi, lo))
                at += kc * ms
            return views

        def weights_load(sp, p, s):
            if p < NPH:
                if p > 0:
                    sp.wait_ge(w_lo, SLICE_BASE[p] + s)
                for src, st, _, _ in slice_views(p, s):
                    sp.dma_start(st, src).then_inc(w_loaded, 16)

        def weights_hi(dve, p, s):
            if p < NPH:
                views = slice_views(p, s)
                dve.wait_ge(w_loaded, LOAD_BASE[p] + 16 * len(views) * (s + 1))
                dve.memset(spacer[:, 0:1], 0.0)
                for _, st, hi, _ in views:
                    last = dve.tensor_copy(hi, st)
                last.then_inc(w_hi, 1)

        def weights_lo(pool, p, s):
            if p < NPH:
                pool.wait_ge(w_hi, SLICE_BASE[p] + s + 1)
                for _, st, hi, lo in slice_views(p, s):
                    last = pool.tensor_tensor(lo, st, hi.bitcast(F32), ALU.subtract)
                last.then_inc(w_lo, 1)

        def sets(p):
            return GB if p in HID else 1

        def ln_stats(dve, p, b, j):
            u = p * BATCH + b
            for k in range(TPB):
                last = dve.bn_stats(stats[j][:, k, :], x[:, bass.ds(b * ROWW + k * D, D)])
            last.then_inc(ln_stats_s, 1)
            dve.wait_ge(ln_stats_s, u + 1)
            if not early(u, sets(p)):
                dve.wait_ge(ln_xn, u + 1 - sets(p))
            dve.memset(spacer[:, 1:2], 0.0)
            for k in range(TPB):
                last = dve.bn_aggr(meanvar[j][:, k, :], stats[j][:, k, :])
            last.then_inc(ln_mv, 1)
            dve.wait_ge(ln_mv, u + 1)
            dve.tensor_scalar(vareps[j][:, :], meanvar[j][:, :, 1], EPS[p], None, ALU.add).then_inc(ln_ve, 1)

        def ln_rsqrt(pool, p, b, j):
            pool.wait_ge(ln_ve, p * BATCH + b + 1)
            pool.tensor_tensor(rstd[j][:, :], vareps[j][:, :], mhalf[:, :], ALU.pow).then_inc(ln_rstd, 1)

        def ln_norm(dve, p, b, j):
            u = p * BATCH + b
            dve.wait_ge(ln_rstd, u + 1)
            if not early(u, sets(p)):
                dve.wait_ge(ln_tp, u + 1 - sets(p))
            for k in range(TPB):
                last = dve.tensor_scalar(xn[j][:, k * D:(k + 1) * D], x[:, bass.ds(b * ROWW + k * D, D)],
                                         meanvar[j][:, k, 0:1], rstd[j][:, k:k + 1], ALU.subtract, ALU.mult)
            last.then_inc(ln_xn, 1)

        def t_bank(p, j):
            if p == L1_ATTN:
                return bank[1]
            return T_BANKS[0] if p == 0 else T_BANKS[j]

        def ln_transpose(pe, p, b, j):
            u = p * BATCH + b
            pe.wait_ge(ln_xn, u + 1)
            pe.wait_ge(ln_nf, u if p == 0 else u + 1 - sets(p))
            T = t_bank(p, j)
            for c in range(DC):
                for k in range(TPB):
                    last = pe.transpose(T[:, c * SEQ + k * P:c * SEQ + (k + 1) * P],
                                        xn[j][:, k * D + c * P:k * D + (c + 1) * P], ident[:, :])
            last.then_inc(ln_tp, 1)

        def ln_modulate(act, p, b, j, hi):
            u = p * BATCH + b
            T = t_bank(p, j)
            act.wait_ge(ln_tp, u + 1)
            if not early(u, sets(p)):
                act.wait_ge(ln_lo, u + 1 - sets(p))
            for c in range(DC):
                for dst in (nf[j][:, c * SEQ:(c + 1) * SEQ], hi[c]):
                    last = act.activation(dst, T[:, c * SEQ:(c + 1) * SEQ], ACT.Identity,
                                          scale=mod[:, p, 0, c, bass.ds(b, 1)],
                                          bias=mod[:, p, 1, c, bass.ds(b, 1)])
            last.then_inc(ln_nf, 1)

        def ln_rest(dve, p, b, j, hi, lo):
            dve.wait_ge(ln_nf, p * BATCH + b + 1)
            dve.tensor_tensor(lo, nf[j][:, :].rearrange("p (c r) -> p c r", c=DC), hi.bitcast(F32),
                              ALU.subtract).then_inc(ln_lo, 1)

        def early(n, k):
            return isinstance(n, int) and n < k

        PHASES_OF = [[p for p in range(NPH) if COND[p][0] == m] for m in range(len(ADA))]
        STEPS = []
        for m in range(len(ADA)):
            STEPS += [("rows", m, at, min(512, widths[m] - at)) for at in range(0, widths[m], 512)]
            STEPS.append(("turn", m, 0, 0))
        TURN = [STEPS.index(("turn", m, 0, 0)) for m in range(len(ADA))]
        FIRST = TURN[0] + 1
        STORED = [sum(2 * len(PHASES_OF[q]) for q in range(m + 1)) for m in range(len(ADA))]
        C_LOADS = [sum(1 + len(PHASES_OF[q]) + (L2_SSM in PHASES_OF[q]) for q in range(m + 1))
                   for m in range(len(ADA))]

        def cond_step_tensor(pe, k):
            kind, m, at, w = STEPS[k]
            if k:
                pe.wait_ge(c_done, k)
            if kind == "rows":
                if at == 0:
                    pe.wait_ge(ada_loaded[m], 16)
                if ADA[m][2]:
                    src = [condT[:, 1, :, c] for c in range(DC)] + [condT[:, 0, :, c] for c in range(DC)]
                else:
                    src = [siluT[:, :, c] for c in range(DC)]
                for c in range(kcs[m]):
                    last = pe.matmul(C_BANK[0:BATCH, 0:w], src[c], adaw[m][:, c, at:at + w],
                                     start=c == 0, stop=c == kcs[m] - 1)
            else:
                for n, p in enumerate(PHASES_OF[m]):
                    for s in range(2):
                        sec = COND[p][2 - s]
                        for c in range(DC):
                            o = ((n * 2 + s) * DC + c) * BATCH
                            last = pe.transpose(C_BANK[:, o:o + BATCH], crow[:, sec * D + c * P:sec * D + (c + 1) * P],
                                                ident[0:BATCH, 0:BATCH])
            last.then_inc(c_mm, 1)

        c_steps = [0]

        def cond_step_vector(dve, k):
            def then(ins):
                c_steps[0] += 1
                ins.then_inc(c_step, 1)
                dve.wait_ge(c_step, c_steps[0])

            kind, m, at, w = STEPS[k]
            dve.wait_ge(c_mm, k + 1)
            if kind == "rows":
                if at == 0:
                    dve.wait_ge(c_loaded, 16 * C_LOADS[m])
                    if m:
                        dve.wait_ge(c_stored, 16 * STORED[m - 1])
                dve.tensor_tensor(crow[:, at:at + w], C_BANK[0:BATCH, 0:w], abrow[:, at:at + w], ALU.add
                                  ).then_inc(c_done, 1)
                return
            turned = C_BANK[:, 0:128].rearrange("p (n s c b) -> p n s c b", n=2, s=2, c=DC)
            if L2_SSM in PHASES_OF[m]:
                then(dve.tensor_tensor(b2row[:, 0:D], b2row[:, 0:D], bwdrow[:, :], ALU.add))
            for n, p in enumerate(PHASES_OF[m]):
                ga = crow[:, COND[p][3] * D:(COND[p][3] + 1) * D]
                own = b2row[:, n * D:(n + 1) * D]
                if p == L3_FF:
                    dve.tensor_copy(gbrow[:, n * D:(n + 1) * D], own)
                else:
                    dve.tensor_tensor(gbrow[:, n * D:(n + 1) * D], ga, own, ALU.mult)
                block3 = p >= L3_ATTN
                j = p - L3_ATTN
                one = gain[:, j, :, :] if block3 else mod[:, p, 0, :, :]
                sh = be[:, j, :, :] if block3 else mod[:, p, 1, :, :]
                dve.tensor_scalar(one, turned[:, n, 0, :, :], 1.0, None, ALU.add)
                last = dve.tensor_copy(sh, turned[:, n, 1, :, :])
                if block3:
                    then(last)
                    for c in range(DC):
                        g, b = (vecs[:, LN_AT[v, j] + c:LN_AT[v, j] + c + 1] for v in "gb")
                        dve.tensor_scalar(mod[:, p, 0, c, :], gain[:, j, c, :], g, None, ALU.mult)
                        last = dve.scalar_tensor_tensor(mod[:, p, 1, c, :], gain[:, j, c, :], b, be[:, j, c, :],
                                                        ALU.mult, ALU.add)
            last.then_inc(c_done, 1)

        def cond_loads(sp, m):
            if m:
                sp.wait_ge(c_done, TURN[m - 1] + 1)
            sp.dma_start(abrow[:, 0:widths[m]], t[ADA[m][1]].partition_broadcast(BATCH)).then_inc(c_loaded, 16)
            for n, p in enumerate(PHASES_OF[m]):
                sp.dma_start(b2row[:, n * D:(n + 1) * D], t[COND[p][4]].partition_broadcast(BATCH)).then_inc(c_loaded, 16)
                if p == L2_SSM:
                    sp.dma_start(bwdrow[:, :], t["L2_cond_bwd_b2"].partition_broadcast(BATCH)).then_inc(c_loaded, 16)

        def cond_store(sp, m):
            sp.wait_ge(c_done, TURN[m] + 1)
            for n, p in enumerate(PHASES_OF[m]):
                ga = COND[p][3]
                sp.dma_start(gate_scratch[p, :, 0:D], crow[:, ga * D:(ga + 1) * D]).then_inc(c_stored, 16)
                sp.dma_start(gate_scratch[p, :, D:2 * D], gbrow[:, n * D:(n + 1) * D]).then_inc(c_stored, 16)

        def cond_tensor(pe, slot):
            if FIRST + slot < len(STEPS):
                cond_step_tensor(pe, FIRST + slot)

        def cond_vector(dve, slot):
            if FIRST + slot < len(STEPS):
                cond_step_vector(dve, FIRST + slot)

        def cond_sync(sp, g):
            for m in range(1, len(ADA)):
                if (TURN[m] - FIRST) // 2 == g:
                    cond_store(sp, m)
                    if m + 1 < len(ADA):
                        cond_loads(sp, m + 1)
            if g == GROUPS - 1:
                sp.wait_ge(c_stored, 16 * STORED[-1])

        U_BANKS, Y_BANKS = bank[0:2], [bank[2:4], bank[4:6]]
        LOOK = 2

        def chunks(p):
            return HID[p] // P

        def ahead_of(p):
            return LOOK // chunks(p) + 1 if chunks(p) <= LOOK else 1

        def chunk_no(p, g, c):
            return CHUNK_BASE[p] + chunks(p) * g + c

        def ring(p, i, c):
            return (chunks(p) * i + c) % HRING

        def ff_hidden(pe, p, g, i, c):
            w1, _ = w_tiles(p)
            n = chunk_no(p, g, c)
            if c == 0:
                pe.wait_ge(ln_lo, p * BATCH + GB * g + GB)
            if not early(n, 2):
                pe.wait_ge(h_act, n - 1)
            for k in range(DC):
                last = split3(pe, U_BANKS[c % 2][:, :], [w[:, k, c * P:(c + 1) * P] for w in w1],
                              [m[:, k, :] for m in nT[i]], k == 0, k == DC - 1)
            last.then_inc(u_mm, 1)

        def ff_activate(act, p, g, i, c):
            n, r = chunk_no(p, g, c), ring(p, i, c)
            act.wait_ge(u_mm, n + 1)
            if not early(n, HRING):
                act.wait_ge(h_lo, n + 1 - HRING)
                act.wait_ge(w2_mm, n + 1 - HRING)
            at = BIAS_AT[p] + c
            for dst in (hf[r], hh[r]):
                last = act.activation(dst[:, :], U_BANKS[c % 2][:, :], ACTF[p], bias=vecs[:, at:at + 1])
            last.then_inc(h_act, 1)

        def ff_rest(dve, p, g, i, c):
            n, r = chunk_no(p, g, c), ring(p, i, c)
            dve.wait_ge(h_act, n + 1)
            dve.tensor_tensor(hl[r][:, :], hf[r][:, :], hh[r][:, :].bitcast(F32), ALU.subtract).then_inc(h_lo, 1)

        def ff_output(pe, p, g, i, c):
            _, w2 = w_tiles(p)
            n, r4 = chunk_no(p, g, c), ring(p, i, c)
            pe.wait_ge(h_lo, n + 1)
            if c == 0 and not early(GROUP_BASE[p] + g, 2):
                pe.wait_ge(y_taken, GB * (GROUP_BASE[p] + g - 1))
            for r in range(GB * TPB):
                last = split3(pe, Y_BANKS[i][r // TPB][:, (r % TPB) * D:(r % TPB + 1) * D],
                              [h[:, r * P:(r + 1) * P] for h in (hh[r4], hl[r4])],
                              [w[:, c, :] for w in w2], c == 0 and r % TPB == 0, c == chunks(p) - 1)
            last.then_inc(w2_mm, 1)

        def gate_row(i, j, half):
            return gates[:, GB * i + j, half * D:(half + 1) * D].unsqueeze(1).to_broadcast([P, TPB, D])

        def gate_count(p, g, i):
            return 8 * (GROUP_BASE[p] + g - i) + 16

        def rows_of(tile):
            return tile.rearrange("p (k d) -> p k d", k=TPB)

        def ff_take(dve, p, g, i):
            for j in range(GB):
                dve.wait_ge(w2_mm, chunk_no(p, g + 1, 0))
                dve.wait_ge(gate_loaded[GB * i + j], gate_count(p, g, i))
                if not early(GROUP_BASE[p] + g, 1):
                    dve.wait_ge(x_new, GB * (GROUP_BASE[p] + g))
                half = 1 if p == L3_FF else 0
                dve.tensor_tensor(rows_of(upd[:, j, :]), rows_of(Y_BANKS[i][j][:, :]), gate_row(i, j, half),
                                  ALU.add if half else ALU.mult).then_inc(y_taken, 1)

        def ff_add(dve, p, g, i):
            for j in range(GB):
                n = GB * (GROUP_BASE[p] + g) + j
                b = GB * g + j
                if p == L3_FF:
                    dve.wait_ge(gated2, n - GB * GROUP_BASE[L3_FF] + 1)
                    dve.tensor_tensor(xs(b), xs(b), act2[:, j, :], ALU.add).then_inc(x_new, 1)
                    continue
                dve.wait_ge(y_taken, n + 1)
                dve.wait_ge(xb_ready, n + 1)
                if p == L2_SSM:
                    dve.memset(spacer[:, 2 + j:3 + j], 0.0)
                    dve.tensor_copy(act2[:, j, :], xs(b))
                    dve.tensor_copy(mcur[:, j, :], maski[:, bass.ds(b * TPB, TPB)])
                    dve.tensor_tensor(upd[:, j, :], upd[:, j, :], xb[:, j, :], ALU.add).then_inc(x_tmp, 1)
                    dve.wait_ge(x_tmp, 2 * b + 1)
                    dve.memset(spacer[:, 4 + j:5 + j], 0.0)
                    for k in range(TPB):
                        last = dve.copy_predicated(act2[:, j, k * D:(k + 1) * D],
                                                   mcur[:, j, k:k + 1].to_broadcast([P, D]),
                                                   upd[:, j, k * D:(k + 1) * D])
                    last.then_inc(x_tmp, 1)
                    dve.wait_ge(x_tmp, 2 * b + 2)
                    dve.memset(spacer[:, 6 + j:7 + j], 0.0)
                    dve.tensor_copy(xs(b), act2[:, j, :]).then_inc(x_new, 1)
                else:
                    dve.tensor_tensor(xs(b), upd[:, j, :], xb[:, j, :], ALU.add).then_inc(x_new, 1)

        def ff_gelu2(act, p, g):
            for j in range(GB):
                act.wait_ge(y_taken, GB * (GROUP_BASE[p] + g) + j + 1)
                act.activation(act2[:, j, :], upd[:, j, :], ACT.Gelu).then_inc(gelu2, 1)

        def ff_gate2(pool, p, g, i):
            for j in range(GB):
                pool.wait_ge(gate_loaded[GB * i + j], gate_count(p, g, i))
                pool.wait_ge(gelu2, GB * g + j + 1)
                pool.tensor_tensor(rows_of(act2[:, j, :]), rows_of(act2[:, j, :]), gate_row(i, j, 0),
                                   ALU.mult).then_inc(gated2, 1)

        def nT_unit(i, j):
            return [m[:, :, j * SEQ:(j + 1) * SEQ] for m in nT[i]]

        def ln_unit(name, eng, p, g, i, j):
            b = GB * g + j
            hi, lo = nT_unit(i, j)
            if name == "tensor":
                ln_transpose(eng, p, b, j)
            if name == "scalar":
                if not early(g, 2):
                    eng.wait_ge(u_mm, chunk_no(p, g - 1, 0))
                ln_modulate(eng, p, b, j, [hi[:, c, :] for c in range(DC)])
            if name == "vector":
                ln_rest(eng, p, b, j, hi, lo)

        def ff_body(name):
            def body(eng, p, g, i, left):
                C, ah = chunks(p), ahead_of(p)
                in_prev = left < GROUPS - 1
                la = (i + ah) % 2
                units = [(g + ah, la, j) for j in range(GB)] if left >= ah else []
                norms = [(GB * (g + ah + 1) + j, j) for j in range(GB)] if left >= ah + 1 else []
                for c in range(C):
                    k = c + LOOK
                    nxt = (g + k // C, (i + k // C) % 2, k % C) if k // C <= left else None
                    if name == "tensor":
                        for u in (units if C > GB and c == 0 else units[c:c + 1] if C <= GB else []):
                            ln_unit(name, eng, p, *u)
                        if nxt:
                            ff_hidden(eng, p, *nxt)
                        if p == 0:
                            cond_tensor(eng, C * g + c)
                        ff_output(eng, p, g, i, c)
                    if name == "scalar":
                        if c < len(units):
                            ln_unit(name, eng, p, *units[c])
                        if nxt:
                            ff_activate(eng, p, *nxt)
                        if p == L3_FF and c == 1 and in_prev:
                            ff_gelu2(eng, p, g - 1)
                    if name == "vector":
                        if c == 0 and in_prev:
                            ff_take(eng, p, g - 1, 1 - i)
                        if c < len(units):
                            ln_unit(name, eng, p, *units[c])
                        if nxt:
                            ff_rest(eng, p, *nxt)
                        if c == min(C - 1, 3 if p == L3_FF else 1) and in_prev:
                            ff_add(eng, p, g - 1, 1 - i)
                        if p == 0:
                            cond_vector(eng, C * g + c)
                        if C > GB and 2 <= c < 4:
                            for b, j in norms:
                                (ln_stats if c == 2 else ln_norm)(eng, p, b, j)
                if C <= GB and name == "vector":
                    if p == 0 and g == 0:
                        eng.wait_ge(x_rest, 16)
                    for b, j in norms:
                        ln_stats(eng, p, b, j)
                    for b, j in norms:
                        ln_norm(eng, p, b, j)
                if name == "vector":
                    weights_hi(eng, p + 1, g)
                    if left == 0:
                        ff_take(eng, p, g, i)
                        ff_add(eng, p, g, i)
                if name == "scalar" and left == 0 and p == L3_FF:
                    ff_gelu2(eng, p, g)
                if name == "gpsimd":
                    if p == L3_FF:
                        if in_prev:
                            ff_gate2(eng, p, g - 1, 1 - i)
                    else:
                        for j in range(GB):
                            eng.wait_ge(gate_loaded[GB * i + j], gate_count(p, g, i))
                            if not early(GROUP_BASE[p] + g, 1):
                                eng.wait_ge(x_new, GB * (GROUP_BASE[p] + g))
                            eng.tensor_tensor(rows_of(xb[:, j, :]), rows_of(xs(GB * g + j)), gate_row(i, j, 1),
                                              ALU.add).then_inc(xb_ready, 1)
                    for b, j in norms:
                        ln_rsqrt(eng, p, b, j)
                    weights_lo(eng, p + 1, g)
                    if left == 0 and p == L3_FF:
                        ff_gate2(eng, p, g, i)
                if name == "sync":
                    for j in range(GB):
                        if not early(GROUP_BASE[p] + g, 2):
                            eng.wait_ge(x_new, GB * (GROUP_BASE[p] + g - 1))
                        if p == 0 and g == 0 and j == 0:
                            eng.wait_ge(c_stored, 16 * STORED[0])
                        eng.dma_start(gates[:, GB * i + j, :],
                                      gate_scratch[p, bass.ds(GB * g + j, 1), :].to_broadcast([P, 2 * D])
                                      ).then_inc(gate_loaded[GB * i + j], 16)
                    weights_load(eng, p + 1, g)
                    if p == 0:
                        cond_sync(eng, g)
                    if p == L3_FF:
                        if in_prev:
                            x_store(eng, p, g - 1)
                        if left == 0:
                            x_store(eng, p, g)
            return body

        def x_store(sp, p, g):
            for j in range(GB):
                b = GB * g + j
                sp.wait_ge(x_new, GB * (GROUP_BASE[p] + g) + j + 1)
                sp.dma_start(out[bass.ds(b, 1), :, :].rearrange("b (k p) d -> p (b k) d", p=P),
                             xs(b).rearrange("p (k d) -> p k d", k=TPB)).then_inc(x_stored, 16)

        def ff_start(name, eng, p):
            ah = ahead_of(p)
            for g in range(ah + 1):
                for j in range(GB):
                    if name == "vector":
                        if p == 0 and g > 0:
                            eng.wait_ge(x_rest, 16)
                        ln_stats(eng, p, GB * g + j, j)
                    if name == "gpsimd":
                        ln_rsqrt(eng, p, GB * g + j, j)
                if name == "vector":
                    for j in range(GB):
                        ln_norm(eng, p, GB * g + j, j)
                if g < ah:
                    for j in range(GB):
                        ln_unit(name, eng, p, g, g % 2, j)
                if g == 0:
                    for c in range(LOOK):
                        f = {"tensor": ff_hidden, "scalar": ff_activate, "vector": ff_rest}.get(name)
                        if f:
                            f(eng, p, 0, 0, c)

        def ff_phase(name, eng, p):
            body = ff_body(name)
            ff_start(name, eng, p)
            if p == 0:
                for g in range(GROUPS):
                    body(eng, p, g, g % 2, GROUPS - 1 - g)
                return
            for g in range(2):
                body(eng, p, g, g, GROUPS - 1 - g)
            with eng.Fori(1, GROUPS // 2 - 1) as pair:
                for i in range(2):
                    body(eng, p, 2 * pair + i, i, 2)
            for g in range(GROUPS - 2, GROUPS):
                body(eng, p, g, g % 2, GROUPS - 1 - g)

        PROJ, SB_, PTB, OB, YB = bank[0:2], bank[2:4], (bank[4], bank[7]), bank[5], bank[6]
        PROJ_AT = {1: ("qk", 3), 2: ("v", 1, 0), 3: ("qk", 4), 4: ("v", 1, 1), 5: ("qk", 5), 7: ("qk", 6), 9: ("qk", 7),
                   11: ("qk", 0), 12: ("v", 0, 0), 13: ("qk", 1), 14: ("v", 0, 1), 15: ("qk", 2)}
        PROJ_SLOTS = sorted(PROJ_AT)
        NPROJ = len(PROJ_AT)
        LN_SLOT = 10
        AHEAD = [s for s in PROJ_SLOTS if s > LN_SLOT]
        LAST_OWN = 9
        SCALE = float(DH) ** -0.5
        A = L1_ATTN

        def proj_tensor(pe, b, s):
            what = PROJ_AT[s]
            k = len(AHEAD) + NPROJ * b + PROJ_SLOTS.index(s)
            own = b + 1 if s > LN_SLOT else b
            ring = PROJ[PROJ_SLOTS.index(s) % 2]
            (w, _), cols = w_tiles(A), what[1]
            pe.wait_ge(ln_lo, A * BATCH + own + 1)
            if not (isinstance(k, int) and k < 2):
                pe.wait_ge(proj_ev, k - 1)
            if what[0] == "qk":
                for h in range(2):
                    for c in range(DC):
                        col = h * INNER + cols * P
                        last = split3(pe, ring[:, h * SEQ:(h + 1) * SEQ], [v[:, c, col:col + P] for v in w],
                                      [m[:, c, :] for m in aT], c == 0, c == DC - 1)
            else:
                _, half, tile = what
                col = 2 * INNER + half * 512
                for c in range(DC):
                    last = split3(pe, ring[:, :], [m[:, c, tile * P:(tile + 1) * P] for m in aT],
                                  [v[:, c, col:col + 512] for v in w], c == 0, c == DC - 1)
            last.then_inc(proj_mm, 1)

        def item(b, s):
            what = PROJ_AT[s]
            own = b + 1 if s > LN_SLOT else b
            return PAIRS * own + what[1] if what[0] == "qk" else 2 * TPB * own + 2 * what[1] + what[2]

        def proj_scalar(act, b, s):
            what, n = PROJ_AT[s], item(b, s)
            k = len(AHEAD) + NPROJ * b + PROJ_SLOTS.index(s)
            act.wait_ge(proj_mm, k + 1)
            if what[0] == "qk":
                if not early(n, 2):
                    act.wait_ge(qk_lo, n - 1)
                dst = qkf[what[1] % 2]
            else:
                if not early(n, 1):
                    act.wait_ge(v_lo, n)
                dst = vf
            act.activation(dst[:, :], PROJ[PROJ_SLOTS.index(s) % 2][:, :], ACT.Copy).then_inc(proj_ev, 1)

        def v_slice(what):
            return [m[:, what[2], what[1] * 512:(what[1] + 1) * 512] for m in vv]

        def proj_vector(dve, b, s):
            what, n = PROJ_AT[s], item(b, s)
            k = len(AHEAD) + NPROJ * b + PROJ_SLOTS.index(s)
            dve.wait_ge(proj_ev, k + 1)
            if what[0] == "qk":
                i = what[1] % 2
                if not early(n, 2):
                    dve.wait_ge(s_mm, 2 * n - 2)
                dve.tensor_copy(qz[i][0][0:DH, 0:SEQ], qkf[i][0:DH, 0:SEQ])
                dve.tensor_copy(qz[i][0][DH:P, SEQ:2 * SEQ], qkf[i][DH:P, 0:SEQ])
                dve.tensor_copy(kk[i][0][:, :], qkf[i][:, SEQ:2 * SEQ]).then_inc(qk_hi, 1)
            else:
                own = b + 1 if s > LN_SLOT else b
                if not early(own, 1):
                    dve.wait_ge(pv_mm, HEADS * (own - 1) + 8 * (what[1] + 1))
                dve.tensor_copy(v_slice(what)[0], vf[:, :]).then_inc(v_hi, 1)

        def proj_gpsimd(pool, b, s):
            what, n = PROJ_AT[s], item(b, s)
            if what[0] == "qk":
                i = what[1] % 2
                pool.wait_ge(qk_hi, n + 1)
                def lo(dst, src, hi):
                    return pool.tensor_tensor(dst, src, hi.bitcast(F32), ALU.subtract)
                lo(kk[i][1][:, :], qkf[i][:, SEQ:2 * SEQ], kk[i][0][:, :])
                lo(qz[i][1][0:DH, 0:SEQ], qkf[i][0:DH, 0:SEQ], qz[i][0][0:DH, 0:SEQ]).then_inc(pool_step, 1)
                pool.wait_ge(pool_step, 2 * n + 1)
                lo(qz[i][1][DH:P, SEQ:2 * SEQ], qkf[i][DH:P, 0:SEQ], qz[i][0][DH:P, SEQ:2 * SEQ]).then_inc(pool_step, 1)
                pool.wait_ge(pool_step, 2 * n + 2)
                pool.nop().then_inc(qk_lo, 1)
            else:
                pool.wait_ge(v_hi, n + 1)
                hi, lo = v_slice(what)
                pool.tensor_tensor(lo, vf[:, :], hi.bitcast(F32), ALU.subtract).then_inc(v_lo, 1)

        def scores(pe, H, h):
            i, j = h // 2 % 2, h % 2
            pe.wait_ge(qk_lo, PAIRS_OF(H, h) + 1)
            if not early(H, 2):
                pe.wait_ge(exp_ready, H - 1)
            for q in range(TPB):
                last = split3(pe, SB_[h % 2][:, q * SEQ:(q + 1) * SEQ],
                              [m[:, j * SEQ + q * P:j * SEQ + (q + 1) * P] for m in qz[i]],
                              [m[:, :] for m in kk[i]], True, True)
            last.then_inc(s_mm, 1)

        def PAIRS_OF(H, h):
            return H // 2 if isinstance(H, int) else (H_B[0] * PAIRS + h // 2)

        H_B = [0]

        def score_max(dve, H, src, i, scale, base):
            n = base + H
            dve.wait_ge(s_mm, n + 1)
            dve.tensor_reduce(smax[i][:, :], src.rearrange("p (q k) -> p q k", q=TPB), AX_X,
                              ALU.max).then_inc(max_ready, 1)
            dve.wait_ge(max_ready, n + 1)
            if not early(n, 2):
                dve.wait_ge(exp_ready, n - 1)
            dve.tensor_scalar(nmax[i][:, :], smax[i][:, :], -scale, None, ALU.mult).then_inc(nmax_ready, 1)

        def score_exp(act, H, src, i, dst, scale, base):
            n = base + H
            act.wait_ge(nmax_ready, n + 1)
            if not early(n, 2):
                act.wait_ge(pt_mm, n - 1)
                act.wait_ge(rinv_ready, n - 1)
            for q in range(TPB):
                last = act.activation(dst[:, q, :], src[:, q * SEQ:(q + 1) * SEQ], ACT.Exp, scale=scale,
                                      bias=nmax[i][:, q:q + 1], accum_out=rsum[i][:, q:q + 1])
            last.then_inc(exp_ready, 1)

        def prob_scale(dve, H, i, dst, base):
            n = base + H
            dve.wait_ge(exp_ready, n + 1)
            if not early(n, 2):
                dve.wait_ge(prob_ready, n - 1)
                dve.wait_ge(prob_ready1, n - 1)
            dve.reciprocal(rinv[i][:, :], rsum[i][:, :]).then_inc(rinv_ready, 1)
            dve.wait_ge(rinv_ready, n + 1)
            dve.tensor_scalar(dst[:, 0, :], dst[:, 0, :], rinv[i][:, 0:1], None, ALU.mult).then_inc(prob_ready, 1)

        def prob_scale1(act, H, i, dst, base):
            act.wait_ge(rinv_ready, base + H + 1)
            act.activation(dst[:, 1, :], dst[:, 1, :], ACT.Copy, scale=rinv[i][:, 1:2]).then_inc(prob_ready1, 1)

        def prob_transpose(pe, H, src, i, base):
            n = base + H
            ring = 1 if base else 2
            pe.wait_ge(prob_ready, n + 1)
            pe.wait_ge(prob_ready1, n + 1)
            if not early(n, ring):
                pe.wait_ge(pt_lo, n + 1 - ring)
            for c in range(TPB):
                for q in range(TPB):
                    last = pe.transpose(PTB[i][:, c * SEQ + q * P:c * SEQ + (q + 1) * P],
                                        src[:, q, c * P:(c + 1) * P], ident[:, :])
            last.then_inc(pt_mm, 1)

        def pt_read(act, H, i, base):
            n = base + H
            act.wait_ge(pt_mm, n + 1)
            if not early(n, 2):
                act.wait_ge(pv_mm, n - 1)
            act.activation(pt[i][0][:, :], PTB[i][:, :], ACT.Copy).then_inc(pt_hi, 1)

        def pt_rest(dve, H, i, base):
            dve.wait_ge(pt_hi, base + H + 1)
            dve.tensor_tensor(pt[i][1][:, :], PTB[i][:, :], pt[i][0][:, :].bitcast(F32), ALU.subtract
                              ).then_inc(pt_lo, 1)

        def head_values(pe, H, h, v_items):
            pe.wait_ge(pt_lo, H + 1)
            pe.wait_ge(v_lo, v_items)
            if not early(H, 1):
                pe.wait_ge(o_ev, H)
            for c in range(TPB):
                last = split3(pe, OB[0:DH, (h % 2) * SEQ:(h % 2 + 1) * SEQ],
                              [m[:, c, h * DH:(h + 1) * DH] for m in vv],
                              [m[:, c * SEQ:(c + 1) * SEQ] for m in pt[h % 2]], c == 0, c == TPB - 1)
            last.then_inc(pv_mm, 1)

        def o_read(act, H, h, pair):
            act.wait_ge(pv_mm, H + 1)
            if not early(pair, 2):
                act.wait_ge(o_lo, pair - 1)
            j, i = h % 2, h // 2 % 2
            act.activation(of[i][j * DH:(j + 1) * DH, :], OB[0:DH, j * SEQ:(j + 1) * SEQ],
                           ACT.Copy).then_inc(o_ev, 1)

        def o_split(dve, pair, i):
            dve.wait_ge(o_ev, 2 * pair + 2)
            if not early(pair, 2):
                dve.wait_ge(out_mm, pair - 1)
            dve.tensor_copy(oT[i][0][:, :], of[i][:, :]).then_inc(o_hi, 1)

        def o_rest(pool, pair, i):
            pool.wait_ge(o_hi, pair + 1)
            pool.tensor_tensor(oT[i][1][:, :], of[i][:, :], oT[i][0][:, :].bitcast(F32),
                               ALU.subtract).then_inc(o_lo, 1)

        def out_project(pe, pair, j, b):
            _, w2 = w_tiles(A)
            pe.wait_ge(o_lo, pair + 1)
            if j == 0 and not early(b, 1):
                pe.wait_ge(ay_taken, b)
            for r in range(TPB):
                last = split3(pe, YB[:, r * D:(r + 1) * D], [m[:, r * P:(r + 1) * P] for m in oT[j % 2]],
                              [w[:, j, :] for w in w2], j == 0 and r == 0, j == PAIRS - 1)
            last.then_inc(out_mm, 1)

        def res_vector(dve, p, b, src, done, count, n):
            dve.wait_ge(done, count)
            dve.wait_ge(agate_loaded, 16 * (n + 1))
            row = agate[:, 0:D].unsqueeze(1).to_broadcast([P, TPB, D])
            dve.tensor_tensor(aupd[:, :].rearrange("p (k d) -> p k d", k=TPB),
                              src[:, :].rearrange("p (k d) -> p k d", k=TPB), row, ALU.mult
                              ).then_inc(ay_taken, 1)
            dve.wait_ge(ay_taken, n + 1)
            dve.wait_ge(axb_ready, n + 1)
            dve.tensor_tensor(xs(b), aupd[:, :], axb[:, :], ALU.add).then_inc(ax_new, 1)

        def res_gpsimd(pool, b, n):
            pool.wait_ge(agate_loaded, 16 * (n + 1))
            if not early(n, 1):
                pool.wait_ge(ax_new, n)
            row = agate[:, D:2 * D].unsqueeze(1).to_broadcast([P, TPB, D])
            pool.tensor_tensor(axb[:, :].rearrange("p (k d) -> p k d", k=TPB),
                               xs(b).rearrange("p (k d) -> p k d", k=TPB), row, ALU.add
                               ).then_inc(axb_ready, 1)

        def gate_load(sp, p, b, n):
            if not early(n, 1):
                sp.wait_ge(ax_new, n)
            sp.dma_start(agate[:, :], gate_scratch[p, bass.ds(b, 1), :].to_broadcast([P, 2 * D])
                         ).then_inc(agate_loaded, 16)

        aT_hi = [aT[0][:, c, :] for c in range(DC)]

        def mh_slots(b, first, last):
            for i in range(HEADS):
                def head(o):
                    h = i + o
                    if (h < 0 and first) or (h >= HEADS and last):
                        return None
                    return (HEADS * b + h, h % HEADS)
                yield i, head(2), head(0), head(-1), head(1)

        def mh_projected(name, eng, b, i, first, last):
            s = (i - 1) % HEADS
            if s in PROJ_AT and not (i == 0 and first) and not (last and i > LN_SLOT):
                f = {"scalar": proj_scalar, "vector": proj_vector, "gpsimd": proj_gpsimd}
                f[name](eng, b if i else b - 1, s)

        def mh_tensor(pe, b, first, last):
            for i, ahead, now, prev, _ in mh_slots(b, first, last):
                if i == LN_SLOT and not last:
                    pe.wait_ge(proj_ev, len(AHEAD) + NPROJ * b + PROJ_SLOTS.index(LAST_OWN))
                    ln_transpose(pe, A, b + 1, 0)
                if ahead:
                    H_B[0] = b + 1 if i + 2 >= HEADS else b
                    scores(pe, *ahead)
                prob_transpose(pe, now[0], prob[i % 2], i % 2, 0)
                if prev:
                    own = b if i else b - 1
                    head_values(pe, *prev, 2 * TPB * own + (2 if prev[1] < 8 else 4))
                if i in PROJ_AT and not (last and i > LN_SLOT):
                    proj_tensor(pe, b, i)
                if i % 2 == 0 and (i >= 4 or not first):
                    j = (i // 2 - 2) % PAIRS
                    own = b if i >= 4 else b - 1
                    out_project(pe, PAIRS * own + j, j, own)
            if last:
                head_values(pe, HEADS * b + 15, 15, 2 * TPB * b + 4)
                out_project(pe, PAIRS * b + 6, 6, b)
                out_project(pe, PAIRS * b + 7, 7, b)

        def mh_scalar(act, b, first, last):
            for i, ahead, now, prev, nxt in mh_slots(b, first, last):
                if nxt:
                    prob_scale1(act, nxt[0], (i + 1) % 2, prob[(i + 1) % 2], 0)
                mh_projected("scalar", act, b, i, first, last)
                if i == LN_SLOT and not last:
                    act.wait_ge(proj_mm, len(AHEAD) + NPROJ * b + PROJ_SLOTS.index(LAST_OWN) + 1)
                    ln_modulate(act, A, b + 1, 0, aT_hi)
                pt_read(act, now[0], i % 2, 0)
                if ahead:
                    score_exp(act, ahead[0], SB_[i % 2], i % 2, prob[i % 2], SCALE, 0)
                if prev:
                    own = b if i else b - 1
                    o_read(act, *prev, PAIRS * own + prev[1] // 2)
            if last:
                o_read(act, HEADS * b + 15, 15, PAIRS * b + 7)

        def mh_vector(dve, b, first, last):
            for i, ahead, now, prev, nxt in mh_slots(b, first, last):
                if nxt:
                    prob_scale(dve, nxt[0], (i + 1) % 2, prob[(i + 1) % 2], 0)
                if i % 2 and (i > 1 or not first):
                    o_split(dve, *mh_pair(b, i))
                if i == 6 and not last:
                    ln_norm(dve, A, b + 1, 0)
                if ahead:
                    score_max(dve, ahead[0], SB_[i % 2][:, :], i % 2, SCALE, 0)
                mh_projected("vector", dve, b, i, first, last)
                if i == LN_SLOT and not last:
                    ln_rest(dve, A, b + 1, 0, aT[0][:, :, :], aT[1][:, :, :])
                pt_rest(dve, now[0], i % 2, 0)
                if i == 4 and not last:
                    ln_stats(dve, A, b + 1, 0)
                if i == 3 and not first:
                    res_vector(dve, A, b - 1, YB, out_mm, PAIRS * b, b - 1)
                if i == 7:
                    weights_hi(dve, A + 1, b)
            if last:
                o_split(dve, PAIRS * b + 7, 1)
                res_vector(dve, A, b, YB, out_mm, PAIRS * b + PAIRS, b)

        def mh_pair(b, i):
            j = (i - 3) // 2
            return PAIRS * (b if j >= 0 else b - 1) + j % PAIRS, j % 2

        def mh_gpsimd(pool, b, first, last):
            for i, ahead, now, prev, nxt in mh_slots(b, first, last):
                if i % 2 and (i > 1 or not first):
                    o_rest(pool, *mh_pair(b, i))
                mh_projected("gpsimd", pool, b, i, first, last)
                if i == 5 and not last:
                    ln_rsqrt(pool, A, b + 1, 0)
                if i == 7:
                    weights_lo(pool, A + 1, b)
                if i == 9:
                    res_gpsimd(pool, b, b)
            if last:
                o_rest(pool, PAIRS * b + 7, 1)

        def mh_sync(sp, b, first, last):
            gate_load(sp, A, b, b)
            weights_load(sp, A + 1, b)

        def mh_start(name, eng):
            if name == "tensor":
                ln_transpose(eng, A, 0, 0)
            if name == "scalar":
                ln_modulate(eng, A, 0, 0, aT_hi)
            if name == "vector":
                eng.memset(qz[0][0][:, :].bitcast(F32), 0.0)
                eng.memset(qz[0][1][:, :].bitcast(F32), 0.0)
                eng.memset(qz[1][0][:, :].bitcast(F32), 0.0)
                eng.memset(qz[1][1][:, :].bitcast(F32), 0.0).then_inc(zeros, 1)
                eng.wait_ge(zeros, 1)
                ln_stats(eng, A, 0, 0)
                ln_norm(eng, A, 0, 0)
                ln_rest(eng, A, 0, 0, aT[0][:, :, :], aT[1][:, :, :])
            if name == "gpsimd":
                ln_rsqrt(eng, A, 0, 0)
            f = {"tensor": proj_tensor, "scalar": proj_scalar, "vector": proj_vector, "gpsimd": proj_gpsimd}
            for s in AHEAD:
                f[name](eng, -1, s)
            for h in range(2):
                if name == "tensor":
                    scores(eng, h, h)
                if name == "vector":
                    score_max(eng, h, SB_[h][:, :], h, SCALE, 0)
                if name == "scalar":
                    score_exp(eng, h, SB_[h], h, prob[h], SCALE, 0)
            if name == "vector":
                prob_scale(eng, 0, 0, prob[0], 0)
            if name == "scalar":
                prob_scale1(eng, 0, 0, prob[0], 0)

        def att_phase(eng, body, apart):
            body(eng, 0, True, False)
            with eng.Fori(1, BATCH - apart) as b:
                body(eng, b, False, False)
            for b in range(BATCH - apart, BATCH):
                body(eng, b, False, b == BATCH - 1)

        QB, KB, VB, S1, O1 = bank[0], bank[1], bank[2], bank[3], bank[5]
        S6 = L3_ATTN
        SCALE1 = float(D) ** -0.5
        H0 = HEADS * BATCH
        V0 = 2 * TPB * BATCH
        qk1, kk1, vv1 = qz[0], qz[1], [m[:, 0, 0:512] for m in vv]

        def sh_qk(pe, b, which):
            (w, _) = w_tiles(S6)
            pe.wait_ge(ln_lo, S6 * BATCH + b + 1)
            B, lo, s = ((QB, q_lo, b_q), (KB, k_lo, b_k))[which]
            if not early(b, 1):
                pe.wait_ge(lo, b)
            for m in range(DC):
                for c in range(DC):
                    col = which * D + m * P
                    last = split3(pe, B[:, m * SEQ:(m + 1) * SEQ], [v[:, c, col:col + P] for v in w],
                                  [a[:, c, :] for a in aT], c == 0, c == DC - 1)
            last.then_inc(s, 1)

        def sh_v(pe, b):
            (w, _) = w_tiles(S6)
            pe.wait_ge(v_lo, V0 + b)
            for r in range(TPB):
                for c in range(DC):
                    last = split3(pe, VB[:, r * D:(r + 1) * D], [a[:, c, r * P:(r + 1) * P] for a in aT],
                                  [v[:, c, 2 * D:3 * D] for v in w], c == 0, c == DC - 1)
            last.then_inc(b_v, 1)

        def sh_scores(pe, b):
            pe.wait_ge(q_lo, b + 1)
            pe.wait_ge(k_lo, b + 1)
            pe.wait_ge(exp_ready, H0 + b)
            for q in range(TPB):
                for c in range(DC):
                    last = split3(pe, S1[:, q * SEQ:(q + 1) * SEQ],
                                  [m[:, c * SEQ + q * P:c * SEQ + (q + 1) * P] for m in qk1],
                                  [m[:, c * SEQ:(c + 1) * SEQ] for m in kk1], c == 0, c == DC - 1)
            last.then_inc(s_mm, 1)

        def sh_values(pe, b):
            pe.wait_ge(pt_lo, H0 + b + 1)
            pe.wait_ge(v_lo, V0 + b + 1)
            pe.wait_ge(ay_taken, BATCH + b)
            for q in range(TPB):
                for c in range(TPB):
                    last = split3(pe, O1[:, q * D:(q + 1) * D],
                                  [m[:, c * SEQ + q * P:c * SEQ + (q + 1) * P] for m in pt[0]],
                                  [m[:, c * D:(c + 1) * D] for m in vv1], c == 0, c == TPB - 1)
            last.then_inc(pv_mm, 1)

        def sh_tensor(pe, b, first, last):
            sh_qk(pe, b, 0)
            sh_qk(pe, b, 1)
            if not first:
                prob_transpose(pe, b - 1, prob[0], 0, H0)
            if first:
                sh_v(pe, b)
            if not last:
                ln_transpose(pe, S6, b + 1, 0)
            if not first:
                sh_values(pe, b - 1)
                sh_v(pe, b)
            sh_scores(pe, b)
            if last:
                prob_transpose(pe, b, prob[0], 0, H0)
                sh_values(pe, b)

        QK_OF = ((QB, qk1, b_q, q_hi, q_lo, 0), (KB, kk1, b_k, k_hi, k_lo, DC))

        def sh_scalar(act, b, first, last):
            for B, dst, mm, hi, _, at in QK_OF:
                act.wait_ge(mm, b + 1)
                act.wait_ge(s_mm, H0 + b)
                for m in range(DC):
                    n = BIAS_AT[S6] + at + m
                    l = act.activation(dst[0][:, m * SEQ:(m + 1) * SEQ], B[:, m * SEQ:(m + 1) * SEQ],
                                       ACT.Identity, bias=vecs[:, n:n + 1])
                l.then_inc(hi, 1)
            if not first:
                pt_read(act, b - 1, 0, H0)
            act.wait_ge(b_v, b + 1)
            act.wait_ge(pv_mm, H0 + b)
            act.activation(vv1[0], VB[:, :], ACT.Copy).then_inc(v_hi, 1)
            if not last:
                ln_modulate(act, S6, b + 1, 0, aT_hi)
            score_exp(act, b, S1, 0, prob[0], SCALE1, H0)
            prob_scale1(act, b, 0, prob[0], H0)
            if last:
                pt_read(act, b, 0, H0)

        def sh_vector(dve, b, first, last):
            for B, dst, _, hi, lo, at in QK_OF:
                dve.wait_ge(hi, b + 1)
                for m in range(DC):
                    n = BIAS_AT[S6] + at + m
                    cols = slice(m * SEQ, (m + 1) * SEQ)
                    l = dve.scalar_tensor_tensor(dst[1][:, cols], B[:, cols], vecs[:, n:n + 1],
                                                 dst[0][:, cols].bitcast(F32), ALU.add, ALU.subtract)
                l.then_inc(lo, 1)
            if not first:
                pt_rest(dve, b - 1, 0, H0)
            dve.wait_ge(v_hi, V0 + b + 1)
            dve.tensor_tensor(vv1[1], VB[:, :], vv1[0].bitcast(F32), ALU.subtract).then_inc(v_lo, 1)
            if not last:
                ln_rest(dve, S6, b + 1, 0, aT[0][:, :, :], aT[1][:, :, :])
            if not first:
                res_vector(dve, S6, b - 1, O1, pv_mm, H0 + b, BATCH + b - 1)
            score_max(dve, b, S1[:, :], 0, SCALE1, H0)
            sh_norm(dve, b + 2, last or isinstance(b, int) and b + 2 >= BATCH)
            prob_scale(dve, b, 0, prob[0], H0)
            weights_hi(dve, S6 + 1, b)
            if last:
                pt_rest(dve, b, 0, H0)
                res_vector(dve, S6, b, O1, pv_mm, H0 + b + 1, BATCH + b)

        def sh_norm(dve, b, none):
            if not none:
                ln_stats(dve, S6, b, 0)
                ln_norm(dve, S6, b, 0)

        def sh_gpsimd(pool, b, first, last):
            if not (last or isinstance(b, int) and b + 2 >= BATCH):
                ln_rsqrt(pool, S6, b + 2, 0)
            res_gpsimd(pool, b, BATCH + b)
            weights_lo(pool, S6 + 1, b)

        def sh_sync(sp, b, first, last):
            gate_load(sp, S6, b, BATCH + b)
            weights_load(sp, S6 + 1, b)

        block = ctx.enter_context(nc.Block())

        def program(eng, name, mh_body, sh_body, signs=True):
            for p in range(NPH):
                if p == L1_ATTN:
                    if name != "sync":
                        mh_start(name, eng)
                    att_phase(eng, mh_body, 1)
                elif p == L3_ATTN:
                    sh_start(name, eng)
                    att_phase(eng, sh_body, 2)
                else:
                    ff_phase(name, eng, p)
                if p < NPH - 1:
                    end_phase(eng, p, signs)

        def sh_start(name, eng):
            if name == "tensor":
                ln_transpose(eng, S6, 0, 0)
            if name == "scalar":
                ln_modulate(eng, S6, 0, 0, aT_hi)
            for b in range(2):
                if name == "gpsimd":
                    ln_rsqrt(eng, S6, b, 0)
                if name == "vector":
                    sh_norm(eng, b, False)
                    if b == 0:
                        ln_rest(eng, S6, 0, 0, aT[0][:, :, :], aT[1][:, :, :])

        row_srcs = [(condrows[n * NC:(n + 1) * NC, :], t[name].rearrange("b (k p) -> (b k) p", p=P))
                    for n, name in enumerate(("cond_1024", "fside_BxS_0"))]
        row_srcs.append((mask8[2 * NC:3 * NC, :], t["mask_BxS_bk0"].rearrange("b (k p) -> (b k) p", p=P)))
        at = 0
        for v in VEC_SRC:
            k = v.shape[0] // P
            row_srcs.append((vecrows[at:at + k, :], v.rearrange("(c p) -> c p", p=P)))
            at += k

        @block.sync
        def _(sp):
            sp.dma_start(adaw[0][:, :, :], t[ADA[0][0]].rearrange("(k p) m -> p k m", p=P)).then_inc(ada_loaded[0], 16)
            rows = t["x"].rearrange("b (k p) d -> p (b k) d", p=P)
            xv = x[:, :].rearrange("p (n d) -> p n d", d=D)
            n = GB * TPB
            sp.dma_start(xv[:, 0:n, :], rows[:, 0:n, :]).then_inc(x_loaded, 16)
            weights_load(sp, 0, 0)
            cond_loads(sp, 0)
            sp.dma_start(xv[:, n:, :], rows[:, n:, :]).then_inc(x_rest, 16)
            for m in range(1, len(ADA)):
                sp.dma_start(adaw[m][:, :, :], t[ADA[m][0]].rearrange("(k p) m -> p k m", p=P)).then_inc(ada_loaded[m], 16)
            cond_store(sp, 0)
            cond_loads(sp, 1)
            end_phase(sp, -1, False)
            program(sp, "sync", mh_sync, sh_sync, signs=False)
            sp.wait_ge(x_stored, 16 * BATCH)

        @block.scalar
        def _(act):
            for dst, src in row_srcs:
                act.dma_start(dst, src).then_inc(pro_loads, 16)
            act.wait_ge(cond_cols, 1)
            act.activation(siluT[:, :, :], condT[:, 0, :, :], ACT.Silu).then_inc(silu_ready, 1)
            end_phase(act, -1)
            program(act, "scalar", mh_scalar, sh_scalar)

        @block.tensor
        def _(pe):
            pe.wait_ge(pro_loads, 16 * len(row_srcs))
            pe.wait_ge(consts, 1)
            pe.wait_ge(mask_rows, 1)
            pe.transpose(bank[5][:, 0:3 * NC], condrows[:, :], ident[0:3 * NC, 0:3 * NC])
            pe.transpose(bank[4][:, 0:NVEC], vecrows[:, :], ident[0:NVEC, 0:NVEC]).then_inc(cond_tp, 1)
            pe.wait_ge(silu_ready, 1)
            pe.wait_ge(cond_cols, 1)
            for k in range(FIRST):
                cond_step_tensor(pe, k)
            end_phase(pe, -1)
            program(pe, "tensor", mh_tensor, sh_tensor)

        @block.vector
        def _(dve):
            dve.memset(mhalf[:, :], -0.5)
            dve.wait_ge(pro_loads, 16 * len(row_srcs))
            dve.tensor_copy(condrows[2 * NC:3 * NC, :], mask8[2 * NC:3 * NC, :]).then_inc(mask_rows, 1)
            dve.wait_ge(cond_tp, 1)
            dve.tensor_copy(condT[:, :, :, :].rearrange("p a b k -> p (a b k)"), bank[5][:, 0:2 * NC])
            dve.tensor_copy(maski[:, :], bank[5][:, 2 * NC:3 * NC])
            dve.tensor_copy(vecs[:, :], bank[4][:, 0:NVEC]).then_inc(cond_cols, 1)
            dve.wait_ge(cond_cols, 1)
            weights_hi(dve, 0, 0)
            for k in range(FIRST):
                cond_step_vector(dve, k)
            dve.wait_ge(x_loaded, 16)
            end_phase(dve, -1)
            program(dve, "vector", mh_vector, sh_vector)

        @block.gpsimd
        def _(pool):
            pool.memset(ident[:, :], 0.0).then_inc(ident_zero, 1)
            pool.wait_ge(ident_zero, 1)
            pool.affine_select(out=ident[:, :], in_=ident[:, :], compare_op=ALU.not_equal, fill=1.0, base=0,
                               pattern=[[-1, P]], channel_multiplier=1).then_inc(consts, 1)
            weights_lo(pool, 0, 0)
            end_phase(pool, -1)
            program(pool, "gpsimd", mh_gpsimd, sh_gpsimd)


def kernel(**inputs):
    import numpy as _np
    import concourse.bacc as _bacc
    from concourse import mybir as _mybir
    from concourse.bass_utils import run_bass_kernel_spmd as _run

    nc = _bacc.Bacc("TRN2", target_bir_lowering=False, num_devices=1)
    arrays, aps = {}, {}
    for name, value in inputs.items():
        a = _np.ascontiguousarray(value)
        arrays[f"in_{name}"] = a
        aps[name] = nc.dram_tensor(f"in_{name}", a.shape, _mybir.dt.from_np(a.dtype), kind="ExternalInput").ap()
    out = nc.dram_tensor("out", (BATCH, SEQ, D), F32, kind="ExternalOutput").ap()
    bass_cond_blocks(nc, aps, out)
    r = _run(nc, [arrays], core_ids=[0])
    return r.results[0]["out"]
```

```python
from contextlib import ExitStack

import concourse.bass as bass
from concourse import mybir

ALU = mybir.AluOpType
ACT = mybir.ActivationFunctionType
F32 = mybir.dt.float32
F32R = mybir.dt.float32r
I32 = mybir.dt.int32
U8 = mybir.dt.uint8
AX_X = mybir.AxisListType.X

P = 128
BATCH, SEQ, D = 16, 256, 256
TPB = SEQ // P
DC = D // P
ROWW = TPB * D
HEADS, DH = 16, 64
INNER = HEADS * DH
PAIRS = HEADS // 2
GB = 2
GROUPS = BATCH // GB
GW = GB * SEQ
NPH = 8
L1_ATTN, L2_SSM, L3_ATTN, L3_FF = 2, 4, 6, 7

HID = {0: 256, 1: 512, 3: 1024, 4: 512, 5: 512, 7: 1024}
ACTF = {0: ACT.Gelu, 1: ACT.Gelu_apprx_tanh, 3: ACT.Gelu, 4: ACT.Gelu, 5: ACT.Gelu_apprx_tanh, 7: ACT.Gelu}
EPS = [1e-6, 1e-6, 1e-5, 1e-5, 1e-6, 1e-6, 1e-5, 1e-5]


def bass_cond_blocks(nc, t, out):
    def two(w1, w2):
        return [(t[w1], "w1", 0, 0), (t[w2], "w2", 0, 0)]

    PARTS = {
        0: two("L0_cond_ssm_w1", "L0_cond_ssm_w2"),
        1: two("L0_cond_ff_w1", "L0_cond_ff_w2"),
        2: two("L1_cond_W_qkv", "L1_cond_W_out"),
        3: two("L1_cond_W1", "L1_cond_W2"),
        4: [(t["L2_cond_ssm_w1"], "w1", 0, 0), (t["L2_cond_bwd_w1"], "w1", 0, 256),
            (t["L2_cond_ssm_w2"], "w2", 0, 0), (t["L2_cond_bwd_w2"], "w2", 2, 0)],
        5: two("L2_cond_ff_w1", "L2_cond_ff_w2"),
        6: [(t["L3_cond_Wq"], "w1", 0, 0), (t["L3_cond_Wk"], "w1", 0, 256), (t["L3_cond_Wv"], "w1", 0, 512)],
        7: two("L3_cond_W1", "L3_cond_W2"),
    }
    W1_COLS = {**HID, 2: 3 * INNER, 6: 3 * D}
    W2_CHUNKS = {**{p: h // P for p, h in HID.items()}, 2: INNER // P, 6: 0}
    SLICES = [1] + [GROUPS if p - 1 in HID else BATCH for p in range(1, NPH)]
    SLICE_BASE = [sum(SLICES[:p]) for p in range(NPH + 1)]
    LOAD_BASE = [sum(16 * len(PARTS[q]) * SLICES[q] for q in range(p)) for p in range(NPH + 1)]

    ADA = [("L0_cond_ada_w", "L0_cond_ada_b", 0), ("L1_cond_W_mod", "L1_cond_b_mod", 0),
           ("L2_cond_ada_w", "L2_cond_ada_b", 0), ("L2_cond_ffada_w", "L2_cond_ffada_b", 0),
           ("L3_cond_Wc", "L3_cond_bc", 1)]
    COND = [(0, 0, 1, 2, "L0_cond_ssm_b2"), (0, 3, 4, 5, "L0_cond_ff_b2"),
            (1, 0, 1, 2, "L1_cond_b_out"), (1, 3, 4, 5, "L1_cond_b2"),
            (2, 0, 1, 2, "L2_cond_ssm_b2"), (3, 0, 1, 2, "L2_cond_ff_b2"),
            (4, 2, 1, 0, "L3_cond_bv"), (4, 5, 4, 3, "L3_cond_b2")]
    BIASES = {0: ["L0_cond_ssm_b1"], 1: ["L0_cond_ff_b1"], 3: ["L1_cond_b1"],
              4: ["L2_cond_ssm_b1", "L2_cond_bwd_b1"], 5: ["L2_cond_ff_b1"],
              6: ["L3_cond_bq", "L3_cond_bk"], 7: ["L3_cond_b1"]}
    VEC_SRC, BIAS_AT, LN_AT = [], {}, {}

    def vec_rows(src):
        at = sum(v.shape[0] // P for v in VEC_SRC)
        VEC_SRC.append(src)
        return at
    for p, names in BIASES.items():
        BIAS_AT[p] = [vec_rows(t[n]) for n in names][0]
    for j in range(2):
        for v in "gb":
            LN_AT[v, j] = vec_rows(t[f"L3_cond_ln{j + 1}_{v}"])
    NVEC = sum(v.shape[0] // P for v in VEC_SRC)
    NC = BATCH * DC

    def before(per):
        return [sum(per(q) for q in range(p)) for p in range(NPH + 1)]
    CHUNK_BASE = before(lambda q: GROUPS * HID[q] // P if q in HID else 0)
    GROUP_BASE = before(lambda q: GROUPS if q in HID else 0)

    gate_scratch = nc.dram_tensor("gate_scratch", (NPH, BATCH, 2 * D), F32).ap()

    ctx = ExitStack()
    with ctx:
        def sb(name, shape, dt=F32, scope=ctx):
            return scope.enter_context(nc.sbuf_tensor(name, shape, dt))

        def sem(name):
            return ctx.enter_context(nc.semaphore(name))

        x = sb("x", [P, BATCH * ROWW])
        stage = sb("stage", [P, 1024])
        mod = sb("mod", [P, NPH, 2, DC, BATCH])
        vecs = sb("vecs", [P, NVEC])
        ident = sb("ident", [P, P])
        maski = sb("maski", [P, BATCH * TPB], I32)
        spacer = sb("spacer", [P, 8])
        mcur = sb("mcur", [P, GB, TPB], I32)
        stats = [sb(f"stats{j}", [P, TPB, 6]) for j in range(GB)]
        meanvar = [sb(f"meanvar{j}", [P, TPB, 2]) for j in range(GB)]
        vareps = [sb(f"vareps{j}", [P, TPB]) for j in range(GB)]
        rstd = [sb(f"rstd{j}", [P, TPB]) for j in range(GB)]
        mhalf = sb("mhalf", [P, TPB])
        xn = [sb(f"xn{j}", [P, ROWW]) for j in range(GB)]
        nf = [sb(f"nf{j}", [P, ROWW]) for j in range(GB)]

        pro = ExitStack()
        kcs = [t[w].shape[0] // P for w, _, _ in ADA]
        widths = [t[w].shape[1] for w, _, _ in ADA]
        adaw = [sb("adaw0", [P, kcs[0], widths[0]], scope=pro)]
        condrows = sb("condrows", [3 * NC, P], scope=pro)
        mask8 = sb("mask8", [3 * NC, P], U8, scope=pro)
        vecrows = sb("vecrows", [NVEC, P], scope=pro)
        pro.close()

        ffn = ExitStack()
        nT = [[sb(f"nT{k}_{i}", [P, DC, GW], F32R, ffn) for k in ("hi", "lo")] for i in range(2)]
        HRING = 4
        hf = [sb(f"hf{i}", [P, GW], scope=ffn) for i in range(HRING)]
        hh = [sb(f"hh{i}", [P, GW], F32R, ffn) for i in range(HRING)]
        hl = [sb(f"hl{i}", [P, GW], F32R, ffn) for i in range(HRING)]
        xb = sb("xb", [P, GB, ROWW], scope=ffn)
        upd = sb("upd", [P, GB, ROWW], scope=ffn)
        act2 = sb("act2", [P, GB, ROWW], scope=ffn)
        gates = sb("gates", [P, 2 * GB, 2 * D], scope=ffn)
        ffn.close()

        att = ctx
        aT = [sb(f"aT{k}", [P, DC, SEQ], F32R, att) for k in ("hi", "lo")]
        qkf = [sb(f"qkf{i}", [P, 2 * SEQ], scope=att) for i in range(2)]
        qz = [[sb(f"qz{k}{i}", [P, 2 * SEQ], F32R, att) for k in ("hi", "lo")] for i in range(2)]
        kk = [[sb(f"kk{k}{i}", [P, SEQ], F32R, att) for k in ("hi", "lo")] for i in range(2)]
        vf = sb("vf", [P, 512], scope=att)
        vv = [sb(f"v{k}", [P, TPB, INNER], F32R, att) for k in ("hi", "lo")]
        prob = [sb(f"prob{i}", [P, TPB, SEQ], scope=att) for i in range(2)]
        pt = [[sb(f"pt{k}{i}", [P, 2 * SEQ], F32R, att) for k in ("hi", "lo")] for i in range(2)]
        of = [sb(f"of{i}", [P, SEQ], scope=att) for i in range(2)]
        oT = [[sb(f"oT{k}{i}", [P, SEQ], F32R, att) for k in ("hi", "lo")] for i in range(2)]
        axb = sb("axb", [P, ROWW], scope=att)
        aupd = sb("aupd", [P, ROWW], scope=att)
        agate = sb("agate", [P, 2 * D], scope=att)
        smax = [sb(f"smax{i}", [P, TPB], scope=att) for i in range(2)]
        nmax = [sb(f"nmax{i}", [P, TPB], scope=att) for i in range(2)]
        rsum = [sb(f"rsum{i}", [P, TPB], scope=att) for i in range(2)]
        rinv = [sb(f"rinv{i}", [P, TPB], scope=att) for i in range(2)]
        front_a, front_b = DC * HID[0] + HID[0] // P * D, DC * HID[1] + HID[1] // P * D

        def weight_tile(name, words, front, others):
            scope = ExitStack()
            sb(f"{name}_front", [P, front], scope=scope)
            made = [sb(n, shape, scope=scope) for n, shape in others]
            scope.close()
            return sb(name, [P, words], F32R), made

        wahi, m = weight_tile("WAhi", 8192, front_a, [(f"adaw{n}", [P, kcs[n], widths[n]]) for n in (1, 2, 3)])
        adaw += m
        walo, m = weight_tile("WAlo", 8192, front_a, [("adaw4", [P, kcs[4], widths[4]])])
        adaw += m
        wbhi, (crow, gbrow) = weight_tile("WBhi", 4096, front_b,
                                          [("crow", [BATCH, 6 * D]),
                                           ("gbrow", [BATCH, 2 * D])])
        wblo, (abrow, b2row) = weight_tile("WBlo", 4096, front_b,
                                           [("abrow", [BATCH, 6 * D]),
                                            ("b2row", [BATCH, 2 * D])])
        WA, WB = [wahi, walo], [wbhi, wblo]
        bwdrow = sb("bwdrow", [BATCH, D])
        condT = sb("condT", [P, 2, BATCH, DC])
        siluT = sb("siluT", [P, BATCH, DC])
        gain = sb("gain", [P, 2, DC, BATCH])
        be = sb("be", [P, 2, DC, BATCH])

        bank = [ctx.enter_context(nc.psum_tensor(f"bank{i}", [P, 512], F32)) for i in range(8)]
        T_BANKS = [bank[7], bank[6]]
        C_BANK = bank[6]

        def w_tiles(p):
            W = WA if p % 2 == 0 else WB
            n1 = DC * W1_COLS[p]
            v1 = [w[:, 0:n1].rearrange("p (k m) -> p k m", k=DC) for w in W]
            if not W2_CHUNKS[p]:
                return v1, None
            v2 = [w[:, n1:n1 + W2_CHUNKS[p] * D].rearrange("p (k m) -> p k m", m=D) for w in W]
            return v1, v2

        pro_loads = sem("pro_loads"); cond_loaded = sem("cond_loaded"); mask_rows = sem("mask_rows")
        x_loaded = sem("x_loaded"); x_mid = sem("x_mid"); x_rest = sem("x_rest")
        cond_tp = sem("cond_tp"); cond_cols = sem("cond_cols"); silu_ready = sem("silu_ready")
        consts = sem("consts"); ident_zero = sem("ident_zero")
        c_loaded = sem("c_loaded"); c_mm = sem("c_mm"); c_done = sem("c_done"); c_stored = sem("c_stored")
        c_step = sem("c_step"); ada_loaded = [sem(f"ada_loaded{m}") for m in range(len(ADA))]
        w_loaded = sem("w_loaded"); w_hi = sem("w_hi"); w_lo = sem("w_lo")
        phase_end = sem("phase_end")
        gate_loaded = [sem(f"gate_loaded{i}") for i in range(2 * GB)]
        ln_stats_s = sem("ln_stats"); ln_mv = sem("ln_mv"); ln_ve = sem("ln_ve"); ln_rstd = sem("ln_rstd")
        ln_xn = sem("ln_xn"); ln_tp = sem("ln_tp"); ln_nf = sem("ln_nf"); ln_lo = sem("ln_lo")
        u_mm = sem("u_mm"); h_act = sem("h_act"); h_lo = sem("h_lo")
        w2_mm = sem("w2_mm"); y_taken = sem("y_taken"); xb_ready = sem("xb_ready")
        gelu2 = sem("gelu2"); gated2 = sem("gated2")
        x_new = sem("x_new"); x_tmp = sem("x_tmp"); x_stored = sem("x_stored")
        zeros = sem("zeros")
        proj_mm = sem("proj_mm"); proj_ev = sem("proj_ev"); qk_hi = sem("qk_hi"); qk_lo = sem("qk_lo")
        v_hi = sem("v_hi"); v_lo = sem("v_lo"); s_mm = sem("s_mm"); max_ready = sem("max_ready")
        nmax_ready = sem("nmax_ready"); pool_step = sem("pool_step"); exp_ready = sem("exp_ready"); rinv_ready = sem("rinv_ready")
        prob_ready = sem("prob_ready"); prob_ready1 = sem("prob_ready1"); pt_mm = sem("pt_mm"); pt_hi = sem("pt_hi")
        pt_lo = sem("pt_lo"); pv_mm = sem("pv_mm"); o_ev = sem("o_ev"); o_hi = sem("o_hi"); o_lo = sem("o_lo")
        out_mm = sem("out_mm"); ay_taken = sem("ay_taken"); axb_ready = sem("axb_ready")
        ax_new = sem("ax_new"); agate_loaded = sem("agate_loaded")
        b_q = sem("b_q"); b_k = sem("b_k"); b_v = sem("b_v")
        q_hi = sem("q_hi"); q_lo = sem("q_lo"); k_hi = sem("k_hi"); k_lo = sem("k_lo")

        ENGINES = 4

        def end_phase(eng, p, signs=True):
            if signs:
                eng.drain().then_inc(phase_end, 1)
            ends = 1 + sum(not chained(q + 1) for q in range(p + 1))
            eng.wait_ge(phase_end, ENGINES * ends)

        def xs(b):
            return x[:, bass.ds(b * ROWW, ROWW)]

        def split3(pe, dst, lhs, rhs, start, stop):
            pe.matmul(dst, lhs[1], rhs[0], start=start, stop=False, skip_group_check=True)
            pe.matmul(dst, lhs[0], rhs[1], start=False, stop=False, skip_group_check=True)
            return pe.matmul(dst, lhs[0], rhs[0], start=False, stop=stop, skip_group_check=True)

        def slice_views(p, s):
            n, at, views = SLICES[p], 0, []
            for w, which, k0, m0 in PARTS[p]:
                kc, m = w.shape[0] // P, w.shape[1]
                ms = m // n
                src = w.rearrange("(k p) m -> p k m", p=P)[:, :, bass.ds(s * ms, ms)]
                st = stage[:, at:at + kc * ms].rearrange("p (k m) -> p k m", k=kc)
                tiles = w_tiles(p)[0 if which == "w1" else 1]
                hi, lo = (v[:, k0:k0 + kc, bass.ds(s * ms + m0, ms)] for v in tiles)
                views.append((src, st, hi, lo))
                at += kc * ms
            return views

        def weights_load(sp, p, s):
            if p < NPH:
                if p > 0:
                    sp.wait_ge(w_lo, SLICE_BASE[p] + s)
                for src, st, _, _ in slice_views(p, s):
                    sp.dma_start(st, src).then_inc(w_loaded, 16)

        def weights_hi(dve, p, s):
            if p < NPH:
                views = slice_views(p, s)
                dve.wait_ge(w_loaded, LOAD_BASE[p] + 16 * len(views) * (s + 1))
                dve.memset(spacer[:, 0:1], 0.0)
                for _, st, hi, _ in views:
                    last = dve.tensor_copy(hi, st)
                last.then_inc(w_hi, 1)

        def weights_lo(pool, p, s):
            if p < NPH:
                pool.wait_ge(w_hi, SLICE_BASE[p] + s + 1)
                for _, st, hi, lo in slice_views(p, s):
                    last = pool.tensor_tensor(lo, st, hi.bitcast(F32), ALU.subtract)
                last.then_inc(w_lo, 1)

        def sets(p, b):
            after_one = p == L1_ATTN + 1 and early(b, 1)
            return 1 if p == L1_ATTN or after_one else GB

        def ln_stats(dve, p, b, j):
            u = p * BATCH + b
            if p and early(b, 2 * GB + 2):
                if p - 1 in HID:
                    dve.wait_ge(x_new, GB * GROUP_BASE[p - 1] + b + 1)
                else:
                    dve.wait_ge(ax_new, BATCH * (p == L3_FF) + b + 1)
                dve.memset(spacer[:, 1:2], 0.0)
            for k in range(TPB):
                last = dve.bn_stats(stats[j][:, k, :], x[:, bass.ds(b * ROWW + k * D, D)])
            last.then_inc(ln_stats_s, 1)
            dve.wait_ge(ln_stats_s, u + 1)
            if not early(u, sets(p, b)):
                dve.wait_ge(ln_xn, u + 1 - sets(p, b))
            dve.memset(spacer[:, 1:2], 0.0)
            for k in range(TPB):
                last = dve.bn_aggr(meanvar[j][:, k, :], stats[j][:, k, :])
            last.then_inc(ln_mv, 1)
            dve.wait_ge(ln_mv, u + 1)
            dve.tensor_scalar(vareps[j][:, :], meanvar[j][:, :, 1], EPS[p], None, ALU.add).then_inc(ln_ve, 1)

        def ln_rsqrt(pool, p, b, j):
            pool.wait_ge(ln_ve, p * BATCH + b + 1)
            pool.tensor_tensor(rstd[j][:, :], vareps[j][:, :], mhalf[:, :], ALU.pow).then_inc(ln_rstd, 1)

        def ln_norm(dve, p, b, j):
            u = p * BATCH + b
            dve.wait_ge(ln_rstd, u + 1)
            if not early(u, sets(p, b)):
                dve.wait_ge(ln_tp, u + 1 - sets(p, b))
            for k in range(TPB):
                last = dve.tensor_scalar(xn[j][:, k * D:(k + 1) * D], x[:, bass.ds(b * ROWW + k * D, D)],
                                         meanvar[j][:, k, 0:1], rstd[j][:, k:k + 1], ALU.subtract, ALU.mult)
            last.then_inc(ln_xn, 1)

        def head_norms(name, eng, p):
            for n in heads(p):
                if name == "gpsimd":
                    ln_rsqrt(eng, *n)
                else:
                    ln_stats(eng, *n)
            if name == "vector":
                for n in heads(p):
                    ln_norm(eng, *n)

        def t_bank(p, b, j):
            if p == L1_ATTN:
                return T_BANKS[0] if early(b, 1) else bank[1]
            if p == L1_ATTN + 1 and early(b, GB):
                return PROJ[j]
            return T_BANKS[0] if lone_bank(p, b) else T_BANKS[j]

        def lone_bank(p, b):
            return p == 0 or p == 1 and early(b, 2 * GB)

        def ln_transpose(pe, p, b, j):
            u = p * BATCH + b
            pe.wait_ge(ln_xn, u + 1)
            if not early(u, 1):
                shared = p == 0 or p == 1 and early(b, 2 * GB + 1)
                pe.wait_ge(ln_nf, u if shared else u + 1 - sets(p, b))
            if p == 1 and isinstance(b, int) and b == 2 * GB + 1:
                pe.wait_ge(c_done, len(STEPS))
            T = t_bank(p, b, j)
            for c in range(DC):
                for k in range(TPB):
                    last = pe.transpose(T[:, c * SEQ + k * P:c * SEQ + (k + 1) * P],
                                        xn[j][:, k * D + c * P:k * D + (c + 1) * P], ident[:, :])
            last.then_inc(ln_tp, 1)

        def ln_modulate(act, p, b, j, hi):
            u = p * BATCH + b
            T = t_bank(p, b, j)
            act.wait_ge(ln_tp, u + 1)
            if not early(u, sets(p, b)):
                act.wait_ge(ln_lo, u + 1 - sets(p, b))
            for c in range(DC):
                for dst in (nf[j][:, c * SEQ:(c + 1) * SEQ], hi[c]):
                    last = act.activation(dst, T[:, c * SEQ:(c + 1) * SEQ], ACT.Identity,
                                          scale=mod[:, p, 0, c, bass.ds(b, 1)],
                                          bias=mod[:, p, 1, c, bass.ds(b, 1)])
            last.then_inc(ln_nf, 1)

        def ln_rest(dve, p, b, j, hi, lo):
            dve.wait_ge(ln_nf, p * BATCH + b + 1)
            dve.tensor_tensor(lo, nf[j][:, :].rearrange("p (c r) -> p c r", c=DC), hi.bitcast(F32),
                              ALU.subtract).then_inc(ln_lo, 1)

        def early(n, k):
            return isinstance(n, int) and n < k

        PHASES_OF = [[p for p in range(NPH) if COND[p][0] == m] for m in range(len(ADA))]
        STEPS = []
        for m in range(len(ADA)):
            STEPS += [("rows", m, at, min(512, widths[m] - at)) for at in range(0, widths[m], 512)]
            STEPS.append(("turn", m, 0, 0))
        TURN = [STEPS.index(("turn", m, 0, 0)) for m in range(len(ADA))]
        FIRST = TURN[0] + 1
        STORED = [sum(2 * len(PHASES_OF[q]) for q in range(m + 1)) for m in range(len(ADA))]
        C_LOADS = [sum(1 + len(PHASES_OF[q]) + (L2_SSM in PHASES_OF[q]) for q in range(m + 1))
                   for m in range(len(ADA))]

        def c_bank(k):
            return (C_BANK, bank[0], bank[1])[k] if k < FIRST - 1 else C_BANK

        def cond_step_tensor(pe, k):
            kind, m, at, w = STEPS[k]
            B = c_bank(k)
            if k >= FIRST - 1:
                pe.wait_ge(c_done, k)
            if kind == "rows":
                if at == 0:
                    pe.wait_ge(ada_loaded[m], 16)
                if ADA[m][2]:
                    src = [condT[:, 1, :, c] for c in range(DC)] + [condT[:, 0, :, c] for c in range(DC)]
                else:
                    src = [siluT[:, :, c] for c in range(DC)]
                for c in range(kcs[m]):
                    last = pe.matmul(B[0:BATCH, 0:w], src[c], adaw[m][:, c, at:at + w],
                                     start=c == 0, stop=c == kcs[m] - 1)
            else:
                for n, p in enumerate(PHASES_OF[m]):
                    for s in range(2):
                        sec = COND[p][2 - s]
                        for c in range(DC):
                            o = ((n * 2 + s) * DC + c) * BATCH
                            last = pe.transpose(B[:, o:o + BATCH], crow[:, sec * D + c * P:sec * D + (c + 1) * P],
                                                ident[0:BATCH, 0:BATCH])
            last.then_inc(c_mm, 1)

        c_steps = [0]

        def cond_step_vector(dve, k):
            def then(ins):
                c_steps[0] += 1
                ins.then_inc(c_step, 1)
                dve.wait_ge(c_step, c_steps[0])

            kind, m, at, w = STEPS[k]
            dve.wait_ge(c_mm, k + 1)
            if kind == "rows":
                if at == 0:
                    dve.wait_ge(c_loaded, 16 * C_LOADS[m])
                    if m:
                        dve.wait_ge(c_stored, 16 * STORED[m - 1])
                dve.tensor_tensor(crow[:, at:at + w], c_bank(k)[0:BATCH, 0:w], abrow[:, at:at + w], ALU.add
                                  ).then_inc(c_done, 1)
                return
            turned = C_BANK[:, 0:128].rearrange("p (n s c b) -> p n s c b", n=2, s=2, c=DC)
            if L2_SSM in PHASES_OF[m]:
                then(dve.tensor_tensor(b2row[:, 0:D], b2row[:, 0:D], bwdrow[:, :], ALU.add))
            for n, p in enumerate(PHASES_OF[m]):
                ga = crow[:, COND[p][3] * D:(COND[p][3] + 1) * D]
                own = b2row[:, n * D:(n + 1) * D]
                if p == L3_FF:
                    dve.tensor_copy(gbrow[:, n * D:(n + 1) * D], own)
                else:
                    dve.tensor_tensor(gbrow[:, n * D:(n + 1) * D], ga, own, ALU.mult)
                block3 = p >= L3_ATTN
                j = p - L3_ATTN
                one = gain[:, j, :, :] if block3 else mod[:, p, 0, :, :]
                sh = be[:, j, :, :] if block3 else mod[:, p, 1, :, :]
                dve.tensor_scalar(one, turned[:, n, 0, :, :], 1.0, None, ALU.add)
                last = dve.tensor_copy(sh, turned[:, n, 1, :, :])
                if block3:
                    then(last)
                    for c in range(DC):
                        g, b = (vecs[:, LN_AT[v, j] + c:LN_AT[v, j] + c + 1] for v in "gb")
                        dve.tensor_scalar(mod[:, p, 0, c, :], gain[:, j, c, :], g, None, ALU.mult)
                        last = dve.scalar_tensor_tensor(mod[:, p, 1, c, :], gain[:, j, c, :], b, be[:, j, c, :],
                                                        ALU.mult, ALU.add)
            last.then_inc(c_done, 1)

        def cond_loads(sp, m):
            if m:
                sp.wait_ge(c_done, TURN[m - 1] + 1)
            sp.dma_start(abrow[:, 0:widths[m]], t[ADA[m][1]].partition_broadcast(BATCH)).then_inc(c_loaded, 16)
            for n, p in enumerate(PHASES_OF[m]):
                sp.dma_start(b2row[:, n * D:(n + 1) * D], t[COND[p][4]].partition_broadcast(BATCH)).then_inc(c_loaded, 16)
                if p == L2_SSM:
                    sp.dma_start(bwdrow[:, :], t["L2_cond_bwd_b2"].partition_broadcast(BATCH)).then_inc(c_loaded, 16)

        def cond_store(sp, m):
            sp.wait_ge(c_done, TURN[m] + 1)
            for n, p in enumerate(PHASES_OF[m]):
                ga = COND[p][3]
                sp.dma_start(gate_scratch[p, :, 0:D], crow[:, ga * D:(ga + 1) * D]).then_inc(c_stored, 16)
                sp.dma_start(gate_scratch[p, :, D:2 * D], gbrow[:, n * D:(n + 1) * D]).then_inc(c_stored, 16)

        def cond_tensor(pe, slot):
            if FIRST + slot < len(STEPS):
                cond_step_tensor(pe, FIRST + slot)

        def cond_vector(dve, slot):
            if FIRST + slot < len(STEPS):
                cond_step_vector(dve, FIRST + slot)

        def cond_sync(sp, g):
            for m in range(1, len(ADA)):
                if (TURN[m] - FIRST) // 2 == g:
                    cond_store(sp, m)
                    if m + 1 < len(ADA):
                        cond_loads(sp, m + 1)
            if g == GROUPS - 1:
                sp.wait_ge(c_stored, 16 * STORED[-1])

        U_BANKS, Y_BANKS = bank[0:2], [bank[2:4], bank[4:6]]
        LOOK = 2

        def chunks(p):
            return HID[p] // P

        def ahead_of(p):
            return LOOK // chunks(p) + 1 if chunks(p) <= LOOK else 1

        def chunk_no(p, g, c):
            return CHUNK_BASE[p] + chunks(p) * g + c

        def ring(p, i, c):
            return (chunks(p) * i + c) % HRING

        def ff_hidden(pe, p, g, i, c):
            w1, _ = w_tiles(p)
            n = chunk_no(p, g, c)
            if c == 0:
                pe.wait_ge(ln_lo, p * BATCH + GB * g + GB)
            if not early(n, 2):
                pe.wait_ge(h_act, n - 1)
            for k in range(DC):
                last = split3(pe, U_BANKS[c % 2][:, :], [w[:, k, c * P:(c + 1) * P] for w in w1],
                              [m[:, k, :] for m in nT[i]], k == 0, k == DC - 1)
            last.then_inc(u_mm, 1)

        def ff_activate(act, p, g, i, c):
            n, r = chunk_no(p, g, c), ring(p, i, c)
            act.wait_ge(u_mm, n + 1)
            if not early(n, HRING):
                act.wait_ge(h_lo, n + 1 - HRING)
                act.wait_ge(w2_mm, n + 1 - HRING)
            at = BIAS_AT[p] + c
            for dst in (hf[r], hh[r]):
                last = act.activation(dst[:, :], U_BANKS[c % 2][:, :], ACTF[p], bias=vecs[:, at:at + 1])
            last.then_inc(h_act, 1)

        def ff_rest(dve, p, g, i, c):
            n, r = chunk_no(p, g, c), ring(p, i, c)
            dve.wait_ge(h_act, n + 1)
            dve.tensor_tensor(hl[r][:, :], hf[r][:, :], hh[r][:, :].bitcast(F32), ALU.subtract).then_inc(h_lo, 1)

        def ff_output(pe, p, g, i, c):
            _, w2 = w_tiles(p)
            n, r4 = chunk_no(p, g, c), ring(p, i, c)
            pe.wait_ge(h_lo, n + 1)
            if c == 0 and not early(GROUP_BASE[p] + g, 2):
                pe.wait_ge(y_taken, GB * (GROUP_BASE[p] + g - 1))
            for r in range(GB * TPB):
                last = split3(pe, Y_BANKS[i][r // TPB][:, (r % TPB) * D:(r % TPB + 1) * D],
                              [h[:, r * P:(r + 1) * P] for h in (hh[r4], hl[r4])],
                              [w[:, c, :] for w in w2], c == 0 and r % TPB == 0, c == chunks(p) - 1)
            last.then_inc(w2_mm, 1)

        def gate_row(i, j, half):
            return gates[:, GB * i + j, half * D:(half + 1) * D].unsqueeze(1).to_broadcast([P, TPB, D])

        def gate_count(p, g, i):
            return 8 * (GROUP_BASE[p] + g - i) + 16

        def rows_of(tile):
            return tile.rearrange("p (k d) -> p k d", k=TPB)

        def ff_take(dve, p, g, i):
            for j in range(GB):
                dve.wait_ge(w2_mm, chunk_no(p, g + 1, 0))
                dve.wait_ge(gate_loaded[GB * i + j], gate_count(p, g, i))
                if not early(GROUP_BASE[p] + g, 1):
                    dve.wait_ge(x_new, GB * (GROUP_BASE[p] + g))
                half = 1 if p == L3_FF else 0
                dve.tensor_tensor(rows_of(upd[:, j, :]), rows_of(Y_BANKS[i][j][:, :]), gate_row(i, j, half),
                                  ALU.add if half else ALU.mult).then_inc(y_taken, 1)

        def ff_add(dve, p, g, i, batches=range(GB)):
            for j in batches:
                n = GB * (GROUP_BASE[p] + g) + j
                b = GB * g + j
                if p == L3_FF:
                    dve.wait_ge(gated2, n - GB * GROUP_BASE[L3_FF] + 1)
                    dve.tensor_tensor(xs(b), xs(b), act2[:, j, :], ALU.add).then_inc(x_new, 1)
                    continue
                dve.wait_ge(y_taken, n + 1)
                dve.wait_ge(xb_ready, n + 1)
                if p == L2_SSM:
                    dve.memset(spacer[:, 2 + j:3 + j], 0.0)
                    dve.tensor_copy(act2[:, j, :], xs(b))
                    dve.tensor_copy(mcur[:, j, :], maski[:, bass.ds(b * TPB, TPB)])
                    dve.tensor_tensor(upd[:, j, :], upd[:, j, :], xb[:, j, :], ALU.add).then_inc(x_tmp, 1)
                    dve.wait_ge(x_tmp, 2 * b + 1)
                    dve.memset(spacer[:, 4 + j:5 + j], 0.0)
                    for k in range(TPB):
                        last = dve.copy_predicated(act2[:, j, k * D:(k + 1) * D],
                                                   mcur[:, j, k:k + 1].to_broadcast([P, D]),
                                                   upd[:, j, k * D:(k + 1) * D])
                    last.then_inc(x_tmp, 1)
                    dve.wait_ge(x_tmp, 2 * b + 2)
                    dve.memset(spacer[:, 6 + j:7 + j], 0.0)
                    dve.tensor_copy(xs(b), act2[:, j, :]).then_inc(x_new, 1)
                else:
                    dve.tensor_tensor(xs(b), upd[:, j, :], xb[:, j, :], ALU.add).then_inc(x_new, 1)

        def ff_gelu2(act, p, g):
            for j in range(GB):
                act.wait_ge(y_taken, GB * (GROUP_BASE[p] + g) + j + 1)
                act.activation(act2[:, j, :], upd[:, j, :], ACT.Gelu).then_inc(gelu2, 1)

        def ff_gate2(pool, p, g, i):
            for j in range(GB):
                pool.wait_ge(gate_loaded[GB * i + j], gate_count(p, g, i))
                pool.wait_ge(gelu2, GB * g + j + 1)
                pool.tensor_tensor(rows_of(act2[:, j, :]), rows_of(act2[:, j, :]), gate_row(i, j, 0),
                                   ALU.mult).then_inc(gated2, 1)

        def nT_unit(i, j):
            return [m[:, :, j * SEQ:(j + 1) * SEQ] for m in nT[i]]

        def chained(p):
            return p in HID and p - 1 in HID

        def at(p, g):
            return (p + 1, g - GROUPS) if isinstance(g, int) and g >= GROUPS else (p, g)

        def heads(p):
            return [] if p == NPH else [(p, b, b) for b in range(1 if p == L1_ATTN else GB)]

        def ln_unit(name, eng, p, g, i, j):
            b = GB * g + j
            hi, lo = nT_unit(i, j)
            if name == "tensor":
                ln_transpose(eng, p, b, j)
            if name == "scalar":
                if not early(g, 2):
                    eng.wait_ge(u_mm, chunk_no(p, g - 1, 0))
                elif chained(p):
                    eng.wait_ge(u_mm, CHUNK_BASE[p] + (g - 1) * chunks(p - 1))
                ln_modulate(eng, p, b, j, [hi[:, c, :] for c in range(DC)])
            if name == "vector":
                ln_rest(eng, p, b, j, hi, lo)

        def head_unit(name, eng, p, b):
            hi, lo = nT_unit(0, b) if p in HID else (m[:, :, :] for m in aT)
            if name == "tensor":
                ln_transpose(eng, p, b, b)
            if name == "scalar":
                ln_modulate(eng, p, b, b, [hi[:, c, :] for c in range(DC)])
            if name == "vector":
                ln_rest(eng, p, b, b, hi, lo)

        def ff_body(name):
            def body(eng, p, g, i, left):
                C, ah = chunks(p), ahead_of(p)
                goes_on, follows = chained(p + 1), chained(p)
                ends = left == 0 and not goes_on and p < NPH - 1
                first = isinstance(g, int) and g == 0
                prev = (p - 1, GROUPS - 1, 1) if first and follows else None if first else (p, g - 1, 1 - i)
                reach = left + 2 * GB if goes_on else left
                la = (i + ah) % 2
                units = [(*at(p, g + ah), la, j) for j in range(GB)] if reach >= ah else []
                norms = []
                if reach >= ah + 1:
                    pn, gn = at(p, g + ah + 1)
                    norms = [(pn, GB * gn + j, j) for j in range(GB)]
                elif left == 0:
                    norms = heads(p + 1)
                if first and p == 1:
                    units, norms = [], []
                if isinstance(g, int) and g == 1 and follows and name == "vector":
                    eng.wait_ge(x_new, GB * GROUP_BASE[p])
                slices = [0, 1] if first else [g + 1] if left > 0 else []
                for c in range(C):
                    k = c + LOOK
                    nxt = None
                    if k // C <= reach:
                        pn, gn = at(p, g + k // C)
                        nxt = (pn, gn, (i + k // C) % 2, k % C if pn == p else k - C)
                    if nxt and nxt[0] != p and nxt[3] == 0 and name == "tensor":
                        eng.wait_ge(w_lo, SLICE_BASE[p + 2])
                    if name == "tensor":
                        for u in units if C > GB and c == 0 else []:
                            ln_unit(name, eng, *u)
                        if nxt:
                            ff_hidden(eng, *nxt)
                        for u in units[c:c + 1] if C <= GB else []:
                            ln_unit(name, eng, *u)
                        if p == 0:
                            cond_tensor(eng, C * g + c)
                        if ends and c == C - 1:
                            head_unit(name, eng, p + 1, 0)
                        ff_output(eng, p, g, i, c)
                    if name == "scalar":
                        if c < len(units) and C > GB:
                            ln_unit(name, eng, *units[c])
                        if nxt:
                            ff_activate(eng, *nxt)
                        if c < len(units) and C <= GB:
                            ln_unit(name, eng, *units[c])
                        if p == L3_FF and c == 1 and prev:
                            ff_gelu2(eng, p, g - 1)
                    if name == "vector":
                        if c == 0 and prev:
                            ff_take(eng, *prev)
                        if c < len(units) and C > GB:
                            ln_unit(name, eng, *units[c])
                        stats_at = 1 if C > GB else 0
                        if c == stats_at:
                            if p == 0 and first:
                                eng.wait_ge(x_rest, 16)
                                eng.memset(spacer[:, 1:2], 0.0)
                            for n in norms:
                                ln_stats(eng, *n)
                        if nxt:
                            ff_rest(eng, *nxt)
                        if c < len(units) and C <= GB:
                            ln_unit(name, eng, *units[c])
                        if c == stats_at + 1:
                            for n in norms:
                                ln_norm(eng, *n)
                            for s in slices[:1]:
                                weights_hi(eng, p + 1, s)
                        if C == GB and c == 1 and prev:
                            ff_add(eng, *prev)
                        if C > GB and 2 <= c < 4 and prev:
                            ff_add(eng, *prev, [c - 2])
                        if p == 0:
                            cond_vector(eng, C * g + c)
                if name == "vector":
                    for s in slices[1:]:
                        weights_hi(eng, p + 1, s)
                    if ends:
                        head_unit(name, eng, p + 1, 0)
                    if left == 0 and not goes_on:
                        ff_take(eng, p, g, i)
                        ff_add(eng, p, g, i)
                if name == "scalar" and ends:
                    eng.wait_ge(u_mm, chunk_no(p, g, 0))
                    head_unit(name, eng, p + 1, 0)
                if name == "scalar" and left == 0 and p == L3_FF:
                    ff_gelu2(eng, p, g)
                if name == "gpsimd":
                    for n in norms:
                        ln_rsqrt(eng, *n)
                    for s in slices[:1]:
                        weights_lo(eng, p + 1, s)
                    if p == L3_FF:
                        if prev:
                            ff_gate2(eng, p, g - 1, 1 - i)
                    else:
                        for j in range(GB):
                            eng.wait_ge(gate_loaded[GB * i + j], gate_count(p, g, i))
                            if not early(GROUP_BASE[p] + g, 1):
                                eng.wait_ge(x_new, GB * (GROUP_BASE[p] + g))
                            eng.tensor_tensor(rows_of(xb[:, j, :]), rows_of(xs(GB * g + j)), gate_row(i, j, 1),
                                              ALU.add).then_inc(xb_ready, 1)
                    for s in slices[1:]:
                        weights_lo(eng, p + 1, s)
                    if left == 0 and p == L3_FF:
                        ff_gate2(eng, p, g, i)
                if name == "sync":
                    for s in slices[:1]:
                        weights_load(eng, p + 1, s)
                    for j in range(GB):
                        if not early(GROUP_BASE[p] + g, 2):
                            eng.wait_ge(x_new, GB * (GROUP_BASE[p] + g - 1))
                        if p == 0 and g == 0 and j == 0:
                            eng.wait_ge(c_stored, 16 * STORED[0])
                        eng.dma_start(gates[:, GB * i + j, :],
                                      gate_scratch[p, bass.ds(GB * g + j, 1), :].to_broadcast([P, 2 * D])
                                      ).then_inc(gate_loaded[GB * i + j], 16)
                    for s in slices[1:]:
                        weights_load(eng, p + 1, s)
                    if p == 0:
                        cond_sync(eng, g)
                    if p == L3_FF:
                        if prev:
                            x_store(eng, p, g - 1)
                        if left == 0:
                            x_store(eng, p, g)
            return body

        def x_store(sp, p, g):
            for j in range(GB):
                b = GB * g + j
                sp.wait_ge(x_new, GB * (GROUP_BASE[p] + g) + j + 1)
                sp.dma_start(out[bass.ds(b, 1), :, :].rearrange("b (k p) d -> p (b k) d", p=P),
                             xs(b).rearrange("p (k d) -> p k d", k=TPB)).then_inc(x_stored, 16)

        def ff_norms(name, eng, p, g):
            ns = [(p, GB * g + j, j) for j in range(GB)]
            if name == "vector":
                for n in ns:
                    ln_stats(eng, *n)
                for n in ns:
                    ln_norm(eng, *n)
            if name == "gpsimd":
                for n in ns:
                    ln_rsqrt(eng, *n)

        def ff_start(name, eng, p):
            ah = ahead_of(p)
            f = {"tensor": ff_hidden, "scalar": ff_activate, "vector": ff_rest}.get(name)
            if p == 0 and name == "vector":
                eng.wait_ge(x_mid, 16)
                eng.memset(spacer[:, 1:2], 0.0)
            for g in range(ah):
                if g or p == 0:
                    for j in range(GB):
                        ln_unit(name, eng, p, g, g % 2, j)
                ff_norms(name, eng, p, g + 1)
                if f:
                    for c in [g] if ah > 1 else range(LOOK):
                        f(eng, p, 0, 0, c)

        def ff_phase(name, eng, p):
            body = ff_body(name)
            if not chained(p):
                ff_start(name, eng, p)
            if p == 0:
                for g in range(GROUPS):
                    body(eng, p, g, g % 2, GROUPS - 1 - g)
                return
            for g in range(2):
                body(eng, p, g, g, GROUPS - 1 - g)
            with eng.Fori(1, GROUPS // 2 - 1) as pair:
                for i in range(2):
                    body(eng, p, 2 * pair + i, i, 2)
            for g in range(GROUPS - 2, GROUPS):
                body(eng, p, g, g % 2, GROUPS - 1 - g)

        PROJ, SB_, PTB, OB, YB = bank[0:2], bank[2:4], (bank[4], bank[7]), bank[5], bank[6]
        PROJ_AT = {1: ("qk", 3), 2: ("v", 1, 0), 3: ("qk", 4), 4: ("v", 1, 1), 5: ("qk", 5), 7: ("qk", 6), 9: ("qk", 7),
                   11: ("qk", 0), 12: ("v", 0, 0), 13: ("qk", 1), 14: ("v", 0, 1), 15: ("qk", 2)}
        PROJ_SLOTS = sorted(PROJ_AT)
        NPROJ = len(PROJ_AT)
        LN_SLOT = 10
        AHEAD = [s for s in PROJ_SLOTS if s > LN_SLOT]
        HEAD_SLOTS = (12, 14)
        LAST_OWN = 9
        SCALE = float(DH) ** -0.5
        A = L1_ATTN

        def proj_tensor(pe, b, s):
            what = PROJ_AT[s]
            k = len(AHEAD) + NPROJ * b + PROJ_SLOTS.index(s)
            own = b + 1 if s > LN_SLOT else b
            ring = PROJ[PROJ_SLOTS.index(s) % 2]
            (w, _), cols = w_tiles(A), what[1]
            pe.wait_ge(ln_lo, A * BATCH + own + 1)
            if not (isinstance(k, int) and k < 2):
                pe.wait_ge(proj_ev, k - 1)
            if what[0] == "qk":
                for h in range(2):
                    for c in range(DC):
                        col = h * INNER + cols * P
                        last = split3(pe, ring[:, h * SEQ:(h + 1) * SEQ], [v[:, c, col:col + P] for v in w],
                                      [m[:, c, :] for m in aT], c == 0, c == DC - 1)
            else:
                _, half, tile = what
                col = 2 * INNER + half * 512
                for c in range(DC):
                    last = split3(pe, ring[:, :], [m[:, c, tile * P:(tile + 1) * P] for m in aT],
                                  [v[:, c, col:col + 512] for v in w], c == 0, c == DC - 1)
            last.then_inc(proj_mm, 1)

        def item(b, s):
            what = PROJ_AT[s]
            own = b + 1 if s > LN_SLOT else b
            return PAIRS * own + what[1] if what[0] == "qk" else 2 * TPB * own + 2 * what[1] + what[2]

        def proj_scalar(act, b, s):
            what, n = PROJ_AT[s], item(b, s)
            k = len(AHEAD) + NPROJ * b + PROJ_SLOTS.index(s)
            act.wait_ge(proj_mm, k + 1)
            if what[0] == "qk":
                if not early(n, 2):
                    act.wait_ge(qk_lo, n - 1)
                dst = qkf[what[1] % 2]
            else:
                if not early(n, 1):
                    act.wait_ge(v_lo, n)
                dst = vf
            act.activation(dst[:, :], PROJ[PROJ_SLOTS.index(s) % 2][:, :], ACT.Copy).then_inc(proj_ev, 1)

        def v_slice(what):
            return [m[:, what[2], what[1] * 512:(what[1] + 1) * 512] for m in vv]

        def proj_vector(dve, b, s):
            what, n = PROJ_AT[s], item(b, s)
            k = len(AHEAD) + NPROJ * b + PROJ_SLOTS.index(s)
            dve.wait_ge(proj_ev, k + 1)
            if what[0] == "qk":
                i = what[1] % 2
                if not early(n, 2):
                    dve.wait_ge(s_mm, 2 * n - 2)
                dve.tensor_copy(qz[i][0][0:DH, 0:SEQ], qkf[i][0:DH, 0:SEQ])
                dve.tensor_copy(qz[i][0][DH:P, SEQ:2 * SEQ], qkf[i][DH:P, 0:SEQ])
                dve.tensor_copy(kk[i][0][:, :], qkf[i][:, SEQ:2 * SEQ]).then_inc(qk_hi, 1)
            else:
                own = b + 1 if s > LN_SLOT else b
                if not early(own, 1):
                    dve.wait_ge(pv_mm, HEADS * (own - 1) + 8 * (what[1] + 1))
                dve.tensor_copy(v_slice(what)[0], vf[:, :]).then_inc(v_hi, 1)

        def proj_gpsimd(pool, b, s):
            what, n = PROJ_AT[s], item(b, s)
            if what[0] == "qk":
                i = what[1] % 2
                pool.wait_ge(qk_hi, n + 1)
                def lo(dst, src, hi):
                    return pool.tensor_tensor(dst, src, hi.bitcast(F32), ALU.subtract)
                lo(kk[i][1][:, :], qkf[i][:, SEQ:2 * SEQ], kk[i][0][:, :])
                lo(qz[i][1][0:DH, 0:SEQ], qkf[i][0:DH, 0:SEQ], qz[i][0][0:DH, 0:SEQ]).then_inc(pool_step, 1)
                pool.wait_ge(pool_step, 2 * n + 1)
                lo(qz[i][1][DH:P, SEQ:2 * SEQ], qkf[i][DH:P, 0:SEQ], qz[i][0][DH:P, SEQ:2 * SEQ]).then_inc(pool_step, 1)
                pool.wait_ge(pool_step, 2 * n + 2)
                pool.nop().then_inc(qk_lo, 1)
            else:
                pool.wait_ge(v_hi, n + 1)
                hi, lo = v_slice(what)
                pool.tensor_tensor(lo, vf[:, :], hi.bitcast(F32), ALU.subtract).then_inc(v_lo, 1)

        def scores(pe, H, h):
            i, j = h // 2 % 2, h % 2
            pe.wait_ge(qk_lo, PAIRS_OF(H, h) + 1)
            if not early(H, 2):
                pe.wait_ge(exp_ready, H - 1)
            for q in range(TPB):
                last = split3(pe, SB_[h % 2][:, q * SEQ:(q + 1) * SEQ],
                              [m[:, j * SEQ + q * P:j * SEQ + (q + 1) * P] for m in qz[i]],
                              [m[:, :] for m in kk[i]], True, True)
            last.then_inc(s_mm, 1)

        def PAIRS_OF(H, h):
            return H // 2 if isinstance(H, int) else (H_B[0] * PAIRS + h // 2)

        H_B = [0]

        def score_max(dve, H, src, i, scale, base):
            n = base + H
            dve.wait_ge(s_mm, n + 1)
            dve.tensor_reduce(smax[i][:, :], src.rearrange("p (q k) -> p q k", q=TPB), AX_X,
                              ALU.max).then_inc(max_ready, 1)
            dve.wait_ge(max_ready, n + 1)
            if not early(n, 2):
                dve.wait_ge(exp_ready, n - 1)
            dve.tensor_scalar(nmax[i][:, :], smax[i][:, :], -scale, None, ALU.mult).then_inc(nmax_ready, 1)

        def score_exp(act, H, src, i, dst, scale, base):
            n = base + H
            act.wait_ge(nmax_ready, n + 1)
            if not early(n, 2):
                act.wait_ge(pt_mm, n - 1)
                act.wait_ge(rinv_ready, n - 1)
            for q in range(TPB):
                last = act.activation(dst[:, q, :], src[:, q * SEQ:(q + 1) * SEQ], ACT.Exp, scale=scale,
                                      bias=nmax[i][:, q:q + 1], accum_out=rsum[i][:, q:q + 1])
            last.then_inc(exp_ready, 1)

        def prob_scale(dve, H, i, dst, base):
            n = base + H
            dve.wait_ge(exp_ready, n + 1)
            if not early(n, 2):
                dve.wait_ge(prob_ready, n - 1)
                dve.wait_ge(prob_ready1, n - 1)
            dve.reciprocal(rinv[i][:, :], rsum[i][:, :]).then_inc(rinv_ready, 1)
            dve.wait_ge(rinv_ready, n + 1)
            dve.tensor_scalar(dst[:, 0, :], dst[:, 0, :], rinv[i][:, 0:1], None, ALU.mult).then_inc(prob_ready, 1)

        def prob_scale1(act, H, i, dst, base):
            act.wait_ge(rinv_ready, base + H + 1)
            act.activation(dst[:, 1, :], dst[:, 1, :], ACT.Copy, scale=rinv[i][:, 1:2]).then_inc(prob_ready1, 1)

        def prob_transpose(pe, H, src, i, base):
            n = base + H
            ring = 1 if base else 2
            pe.wait_ge(prob_ready, n + 1)
            pe.wait_ge(prob_ready1, n + 1)
            if not early(n, ring):
                pe.wait_ge(pt_lo, n + 1 - ring)
            for c in range(TPB):
                for q in range(TPB):
                    last = pe.transpose(PTB[i][:, c * SEQ + q * P:c * SEQ + (q + 1) * P],
                                        src[:, q, c * P:(c + 1) * P], ident[:, :])
            last.then_inc(pt_mm, 1)

        def pt_read(act, H, i, base):
            n = base + H
            act.wait_ge(pt_mm, n + 1)
            if not early(n, 2):
                act.wait_ge(pv_mm, n - 1)
            act.activation(pt[i][0][:, :], PTB[i][:, :], ACT.Copy).then_inc(pt_hi, 1)

        def pt_rest(dve, H, i, base):
            dve.wait_ge(pt_hi, base + H + 1)
            dve.tensor_tensor(pt[i][1][:, :], PTB[i][:, :], pt[i][0][:, :].bitcast(F32), ALU.subtract
                              ).then_inc(pt_lo, 1)

        def head_values(pe, H, h, v_items):
            pe.wait_ge(pt_lo, H + 1)
            pe.wait_ge(v_lo, v_items)
            if not early(H, 1):
                pe.wait_ge(o_ev, H)
            for c in range(TPB):
                last = split3(pe, OB[0:DH, (h % 2) * SEQ:(h % 2 + 1) * SEQ],
                              [m[:, c, h * DH:(h + 1) * DH] for m in vv],
                              [m[:, c * SEQ:(c + 1) * SEQ] for m in pt[h % 2]], c == 0, c == TPB - 1)
            last.then_inc(pv_mm, 1)

        def o_read(act, H, h, pair):
            act.wait_ge(pv_mm, H + 1)
            if not early(pair, 2):
                act.wait_ge(o_lo, pair - 1)
            j, i = h % 2, h // 2 % 2
            act.activation(of[i][j * DH:(j + 1) * DH, :], OB[0:DH, j * SEQ:(j + 1) * SEQ],
                           ACT.Copy).then_inc(o_ev, 1)

        def o_split(dve, pair, i):
            dve.wait_ge(o_ev, 2 * pair + 2)
            if not early(pair, 2):
                dve.wait_ge(out_mm, pair - 1)
            dve.tensor_copy(oT[i][0][:, :], of[i][:, :]).then_inc(o_hi, 1)

        def o_rest(pool, pair, i):
            pool.wait_ge(o_hi, pair + 1)
            pool.tensor_tensor(oT[i][1][:, :], of[i][:, :], oT[i][0][:, :].bitcast(F32),
                               ALU.subtract).then_inc(o_lo, 1)

        def out_project(pe, pair, j, b):
            _, w2 = w_tiles(A)
            pe.wait_ge(o_lo, pair + 1)
            if j == 0 and not early(b, 1):
                pe.wait_ge(ay_taken, b)
            for r in range(TPB):
                last = split3(pe, YB[:, r * D:(r + 1) * D], [m[:, r * P:(r + 1) * P] for m in oT[j % 2]],
                              [w[:, j, :] for w in w2], j == 0 and r == 0, j == PAIRS - 1)
            last.then_inc(out_mm, 1)

        def res_vector(dve, p, b, src, done, count, n):
            dve.wait_ge(done, count)
            dve.wait_ge(agate_loaded, 16 * (n + 1))
            row = agate[:, 0:D].unsqueeze(1).to_broadcast([P, TPB, D])
            dve.tensor_tensor(aupd[:, :].rearrange("p (k d) -> p k d", k=TPB),
                              src[:, :].rearrange("p (k d) -> p k d", k=TPB), row, ALU.mult
                              ).then_inc(ay_taken, 1)
            dve.wait_ge(ay_taken, n + 1)
            dve.wait_ge(axb_ready, n + 1)
            dve.tensor_tensor(xs(b), aupd[:, :], axb[:, :], ALU.add).then_inc(ax_new, 1)

        def res_gpsimd(pool, b, n):
            pool.wait_ge(agate_loaded, 16 * (n + 1))
            if not early(n, 1):
                pool.wait_ge(ax_new, n)
            row = agate[:, D:2 * D].unsqueeze(1).to_broadcast([P, TPB, D])
            pool.tensor_tensor(axb[:, :].rearrange("p (k d) -> p k d", k=TPB),
                               xs(b).rearrange("p (k d) -> p k d", k=TPB), row, ALU.add
                               ).then_inc(axb_ready, 1)

        def gate_load(sp, p, b, n):
            if not early(n, 1):
                sp.wait_ge(ax_new, n)
            sp.dma_start(agate[:, :], gate_scratch[p, bass.ds(b, 1), :].to_broadcast([P, 2 * D])
                         ).then_inc(agate_loaded, 16)

        aT_hi = [aT[0][:, c, :] for c in range(DC)]

        def mh_slots(b, first, last):
            for i in range(HEADS):
                def head(o):
                    h = i + o
                    if (h < 0 and first) or (h >= HEADS and last):
                        return None
                    return (HEADS * b + h, h % HEADS)
                yield i, head(2), head(0), head(-1), head(1)

        def mh_projected(name, eng, b, i, first, last):
            s = (i - 1) % HEADS
            if s in PROJ_AT and not (i == 0 and first) and not (last and i > LN_SLOT):
                f = {"scalar": proj_scalar, "vector": proj_vector, "gpsimd": proj_gpsimd}
                f[name](eng, b if i else b - 1, s)

        def mh_tensor(pe, b, first, last):
            for i, ahead, now, prev, _ in mh_slots(b, first, last):
                if i == LN_SLOT and not last:
                    pe.wait_ge(proj_ev, len(AHEAD) + NPROJ * b + PROJ_SLOTS.index(LAST_OWN))
                    ln_transpose(pe, A, b + 1, 0)
                if last and i in HEAD_SLOTS:
                    pe.wait_ge(proj_ev, NPROJ * BATCH)
                    head_unit("tensor", pe, A + 1, HEAD_SLOTS.index(i))
                if ahead:
                    H_B[0] = b + 1 if i + 2 >= HEADS else b
                    scores(pe, *ahead)
                prob_transpose(pe, now[0], prob[i % 2], i % 2, 0)
                if prev:
                    own = b if i else b - 1
                    head_values(pe, *prev, 2 * TPB * own + (2 if prev[1] < 8 else 4))
                if i in PROJ_AT and not (last and i > LN_SLOT):
                    proj_tensor(pe, b, i)
                if i % 2 == 0 and (i >= 4 or not first):
                    j = (i // 2 - 2) % PAIRS
                    own = b if i >= 4 else b - 1
                    out_project(pe, PAIRS * own + j, j, own)
            if last:
                head_values(pe, HEADS * b + 15, 15, 2 * TPB * b + 4)
                out_project(pe, PAIRS * b + 6, 6, b)
                out_project(pe, PAIRS * b + 7, 7, b)

        def mh_scalar(act, b, first, last):
            for i, ahead, now, prev, nxt in mh_slots(b, first, last):
                if nxt:
                    prob_scale1(act, nxt[0], (i + 1) % 2, prob[(i + 1) % 2], 0)
                mh_projected("scalar", act, b, i, first, last)
                if i == LN_SLOT and not last:
                    act.wait_ge(proj_mm, len(AHEAD) + NPROJ * b + PROJ_SLOTS.index(LAST_OWN) + 1)
                    ln_modulate(act, A, b + 1, 0, aT_hi)
                if last and i in HEAD_SLOTS:
                    act.wait_ge(proj_mm, NPROJ * BATCH)
                    head_unit("scalar", act, A + 1, HEAD_SLOTS.index(i))
                pt_read(act, now[0], i % 2, 0)
                if ahead:
                    score_exp(act, ahead[0], SB_[i % 2], i % 2, prob[i % 2], SCALE, 0)
                if prev:
                    own = b if i else b - 1
                    o_read(act, *prev, PAIRS * own + prev[1] // 2)
            if last:
                o_read(act, HEADS * b + 15, 15, PAIRS * b + 7)

        def mh_vector(dve, b, first, last):
            for i, ahead, now, prev, nxt in mh_slots(b, first, last):
                if nxt:
                    prob_scale(dve, nxt[0], (i + 1) % 2, prob[(i + 1) % 2], 0)
                if i % 2 and (i > 1 or not first):
                    o_split(dve, *mh_pair(b, i))
                if i == 8 and not last:
                    ln_norm(dve, A, b + 1, 0)
                if ahead:
                    score_max(dve, ahead[0], SB_[i % 2][:, :], i % 2, SCALE, 0)
                mh_projected("vector", dve, b, i, first, last)
                if i == LN_SLOT and not last:
                    ln_rest(dve, A, b + 1, 0, aT[0][:, :, :], aT[1][:, :, :])
                if last and i in HEAD_SLOTS:
                    dve.wait_ge(qk_lo, PAIRS * BATCH)
                    head_unit("vector", dve, A + 1, HEAD_SLOTS.index(i))
                pt_rest(dve, now[0], i % 2, 0)
                if last and i == HEAD_SLOTS[0] - 2:
                    head_norms("vector", dve, A + 1)
                if i == 4 and not last:
                    ln_stats(dve, A, b + 1, 0)
                if i == 3 and not first:
                    res_vector(dve, A, b - 1, YB, out_mm, PAIRS * b, b - 1)
                if i == 7:
                    weights_hi(dve, A + 1, b)
            if last:
                o_split(dve, PAIRS * b + 7, 1)
                res_vector(dve, A, b, YB, out_mm, PAIRS * b + PAIRS, b)

        def mh_pair(b, i):
            j = (i - 3) // 2
            return PAIRS * (b if j >= 0 else b - 1) + j % PAIRS, j % 2

        def mh_gpsimd(pool, b, first, last):
            for i, ahead, now, prev, nxt in mh_slots(b, first, last):
                if i % 2 and (i > 1 or not first):
                    o_rest(pool, *mh_pair(b, i))
                mh_projected("gpsimd", pool, b, i, first, last)
                if i == 5 and not last:
                    ln_rsqrt(pool, A, b + 1, 0)
                if i == 7:
                    weights_lo(pool, A + 1, b)
                if i == 9:
                    res_gpsimd(pool, b, b)
                if last and i == HEAD_SLOTS[0] - 2:
                    head_norms("gpsimd", pool, A + 1)
            if last:
                o_rest(pool, PAIRS * b + 7, 1)

        def mh_sync(sp, b, first, last):
            weights_load(sp, A + 1, b)
            gate_load(sp, A, b, b)

        def mh_start(name, eng):
            if name == "vector":
                eng.memset(qz[0][0][:, :].bitcast(F32), 0.0)
                eng.memset(qz[0][1][:, :].bitcast(F32), 0.0)
                eng.memset(qz[1][0][:, :].bitcast(F32), 0.0)
                eng.memset(qz[1][1][:, :].bitcast(F32), 0.0).then_inc(zeros, 1)
                eng.wait_ge(zeros, 1)
            f = {"tensor": proj_tensor, "scalar": proj_scalar, "vector": proj_vector, "gpsimd": proj_gpsimd}
            for s in AHEAD:
                f[name](eng, -1, s)
            for h in range(2):
                if name == "tensor":
                    scores(eng, h, h)
                if name == "vector":
                    score_max(eng, h, SB_[h][:, :], h, SCALE, 0)
                if name == "scalar":
                    score_exp(eng, h, SB_[h], h, prob[h], SCALE, 0)
            if name == "vector":
                prob_scale(eng, 0, 0, prob[0], 0)
            if name == "scalar":
                prob_scale1(eng, 0, 0, prob[0], 0)

        def mh_phase(eng, body):
            body(eng, 0, True, False)
            with eng.Fori(1, BATCH - 1) as b:
                body(eng, b, False, False)
            body(eng, BATCH - 1, False, True)

        QB, KB, VB, S1, O1 = bank[0], bank[1], bank[2], bank[3], bank[5]
        S6 = L3_ATTN
        SCALE1 = float(D) ** -0.5
        H0 = HEADS * BATCH
        V0 = 2 * TPB * BATCH
        qk1, kk1 = qz
        vv1 = [[m[:, 0, i * ROWW:(i + 1) * ROWW] for m in vv] for i in range(2)]
        a1 = [[m[:, :, :] for m in aT],
              [m[:, 1, 0:ROWW].rearrange("p (c r) -> p c r", c=DC) for m in vv]]

        def sh_qk(pe, b, j, which):
            (w, _) = w_tiles(S6)
            pe.wait_ge(ln_lo, S6 * BATCH + b + 1)
            B, lo, s = ((QB, q_lo, b_q), (KB, k_lo, b_k))[which]
            if not early(b, 1):
                pe.wait_ge(lo, b)
            for m in range(DC):
                for c in range(DC):
                    col = which * D + m * P
                    last = split3(pe, B[:, m * SEQ:(m + 1) * SEQ], [v[:, c, col:col + P] for v in w],
                                  [a[:, c, :] for a in a1[j]], c == 0, c == DC - 1)
            last.then_inc(s, 1)

        def sh_v(pe, b, j):
            (w, _) = w_tiles(S6)
            pe.wait_ge(v_lo, V0 + b)
            for r in range(TPB):
                for c in range(DC):
                    last = split3(pe, VB[:, r * D:(r + 1) * D], [a[:, c, r * P:(r + 1) * P] for a in a1[j]],
                                  [v[:, c, 2 * D:3 * D] for v in w], c == 0, c == DC - 1)
            last.then_inc(b_v, 1)

        def sh_scores(pe, b):
            pe.wait_ge(q_lo, b + 1)
            pe.wait_ge(k_lo, b + 1)
            pe.wait_ge(exp_ready, H0 + b)
            for q in range(TPB):
                for c in range(DC):
                    last = split3(pe, S1[:, q * SEQ:(q + 1) * SEQ],
                                  [m[:, c * SEQ + q * P:c * SEQ + (q + 1) * P] for m in qk1],
                                  [m[:, c * SEQ:(c + 1) * SEQ] for m in kk1], c == 0, c == DC - 1)
            last.then_inc(s_mm, 1)

        def sh_values(pe, b, j):
            pe.wait_ge(pt_lo, H0 + b + 1)
            pe.wait_ge(v_lo, V0 + b + 1)
            pe.wait_ge(ay_taken, BATCH + b)
            for q in range(TPB):
                for c in range(TPB):
                    last = split3(pe, O1[:, q * D:(q + 1) * D],
                                  [m[:, c * SEQ + q * P:c * SEQ + (q + 1) * P] for m in pt[0]],
                                  [m[:, c * D:(c + 1) * D] for m in vv1[j]], c == 0, c == TPB - 1)
            last.then_inc(pv_mm, 1)

        QK_OF = ((QB, qk1, b_q, q_hi, q_lo, 0), (KB, kk1, b_k, k_hi, k_lo, DC))

        def sh_qk_hi(act, b):
            for B, dst, mm, hi, _, at in QK_OF:
                act.wait_ge(mm, b + 1)
                act.wait_ge(s_mm, H0 + b)
                for m in range(DC):
                    n = BIAS_AT[S6] + at + m
                    l = act.activation(dst[0][:, m * SEQ:(m + 1) * SEQ], B[:, m * SEQ:(m + 1) * SEQ],
                                       ACT.Identity, bias=vecs[:, n:n + 1])
                l.then_inc(hi, 1)

        def sh_qk_lo(dve, b):
            for B, dst, _, hi, lo, at in QK_OF:
                dve.wait_ge(hi, b + 1)
                for m in range(DC):
                    n = BIAS_AT[S6] + at + m
                    cols = slice(m * SEQ, (m + 1) * SEQ)
                    l = dve.scalar_tensor_tensor(dst[1][:, cols], B[:, cols], vecs[:, n:n + 1],
                                                 dst[0][:, cols].bitcast(F32), ALU.add, ALU.subtract)
                l.then_inc(lo, 1)

        def sh_v_hi(act, b, j):
            act.wait_ge(b_v, b + 1)
            act.wait_ge(pv_mm, H0 + b - 1)
            act.activation(vv1[j][0], VB[:, :], ACT.Copy).then_inc(v_hi, 1)

        def sh_v_lo(dve, b, j):
            dve.wait_ge(v_hi, V0 + b + 1)
            dve.tensor_tensor(vv1[j][1], VB[:, :], vv1[j][0].bitcast(F32), ALU.subtract).then_inc(v_lo, 1)

        def sh_ln(name, eng, b, j):
            if isinstance(b, int) and b >= BATCH:
                if name == "scalar":
                    eng.wait_ge(b_v, BATCH - 1)
                head_unit(name, eng, S6 + 1, b - BATCH)
                return
            if name == "tensor":
                ln_transpose(eng, S6, b, j)
            if name == "scalar":
                if not early(b, 2):
                    eng.wait_ge(b_v, b - 1)
                ln_modulate(eng, S6, b, j, [a1[j][0][:, c, :] for c in range(DC)])
            if name == "vector":
                ln_rest(eng, S6, b, j, *a1[j])

        def sh_batch(b):
            return (S6 + 1, b - BATCH) if isinstance(b, int) and b >= BATCH else (S6, b)

        def sh_turn(name, eng, b, i, left):
            n = 1 - i
            first = isinstance(b, int) and b == 0
            if name == "tensor":
                sh_ln(name, eng, b + 2, i)
                if left >= 1:
                    sh_qk(eng, b + 1, n, 0)
                    sh_qk(eng, b + 1, n, 1)
                prob_transpose(eng, b, prob[0], 0, H0)
                if left >= 1:
                    sh_v(eng, b + 1, n)
                    sh_scores(eng, b + 1)
                sh_values(eng, b, i)
            if name == "scalar":
                prob_scale1(eng, b, 0, prob[0], H0)
                if left >= 1:
                    sh_qk_hi(eng, b + 1)
                pt_read(eng, b, 0, H0)
                if left >= 1:
                    sh_v_hi(eng, b + 1, n)
                sh_ln(name, eng, b + 2, i)
                if left >= 1:
                    score_exp(eng, b + 1, S1, 0, prob[0], SCALE1, H0)
            if name == "vector":
                if left >= 1:
                    ln_stats(eng, *sh_batch(b + 3), n)
                prob_scale(eng, b, 0, prob[0], H0)
                if not first:
                    res_vector(eng, S6, b - 1, O1, pv_mm, H0 + b, BATCH + b - 1)
                if left >= 1:
                    sh_qk_lo(eng, b + 1)
                pt_rest(eng, b, 0, H0)
                if left >= 1:
                    sh_v_lo(eng, b + 1, n)
                if left >= 1:
                    ln_norm(eng, *sh_batch(b + 3), n)
                if left >= 1:
                    score_max(eng, b + 1, S1[:, :], 0, SCALE1, H0)
                sh_ln(name, eng, b + 2, i)
                weights_hi(eng, S6 + 1, b)
                if left == 0:
                    res_vector(eng, S6, b, O1, pv_mm, H0 + b + 1, BATCH + b)
            if name == "gpsimd":
                if left >= 1:
                    ln_rsqrt(eng, *sh_batch(b + 3), n)
                res_gpsimd(eng, b, BATCH + b)
                weights_lo(eng, S6 + 1, b)
            if name == "sync":
                weights_load(eng, S6 + 1, b)
                gate_load(eng, S6, b, BATCH + b)

        def sh_start(name, eng):
            for b in range(3):
                j = b % 2
                if name == "gpsimd" and b == 2:
                    ln_rsqrt(eng, S6, b, j)
                if name == "vector" and b == 2:
                    ln_stats(eng, S6, b, j)
                    ln_norm(eng, S6, b, j)
                if b == 1:
                    sh_ln(name, eng, b, j)
                if b == 0:
                    if name == "tensor":
                        sh_qk(eng, 0, 0, 0)
                        sh_qk(eng, 0, 0, 1)
                        sh_v(eng, 0, 0)
                    if name == "scalar":
                        sh_qk_hi(eng, 0)
                        sh_v_hi(eng, 0, 0)
                    if name == "vector":
                        sh_qk_lo(eng, 0)
                        sh_v_lo(eng, 0, 0)
            if name == "tensor":
                sh_scores(eng, 0)
            if name == "scalar":
                score_exp(eng, 0, S1, 0, prob[0], SCALE1, H0)
            if name == "vector":
                score_max(eng, 0, S1[:, :], 0, SCALE1, H0)

        def sh_phase(name, eng):
            if name != "sync":
                sh_start(name, eng)
            for b in range(2):
                sh_turn(name, eng, b, b, BATCH - 1 - b)
            with eng.Fori(1, BATCH // 2 - 2) as pair:
                for i in range(2):
                    sh_turn(name, eng, 2 * pair + i, i, 3)
            for b in range(BATCH - 4, BATCH):
                sh_turn(name, eng, b, b % 2, BATCH - 1 - b)

        block = ctx.enter_context(nc.Block())

        def program(eng, name, mh_body, signs=True):
            for p in range(NPH):
                if p == L1_ATTN:
                    if name != "sync":
                        mh_start(name, eng)
                    mh_phase(eng, mh_body)
                elif p == L3_ATTN:
                    sh_phase(name, eng)
                else:
                    ff_phase(name, eng, p)
                if p < NPH - 1 and not chained(p + 1):
                    end_phase(eng, p, signs)

        row_srcs = [(condrows[n * NC:(n + 1) * NC, :], t[name].rearrange("b (k p) -> (b k) p", p=P))
                    for n, name in enumerate(("cond_1024", "fside_BxS_0"))]
        row_srcs.append((mask8[2 * NC:3 * NC, :], t["mask_BxS_bk0"].rearrange("b (k p) -> (b k) p", p=P)))
        row = 0
        for v in VEC_SRC:
            k = v.shape[0] // P
            row_srcs.append((vecrows[row:row + k, :], v.rearrange("(c p) -> c p", p=P)))
            row += k

        @block.sync
        def _(sp):
            sp.dma_start(*row_srcs[0]).then_inc(cond_loaded, 16)
            sp.dma_start(adaw[0][:, :, :], t[ADA[0][0]].rearrange("(k p) m -> p k m", p=P)).then_inc(ada_loaded[0], 16)
            rows = t["x"].rearrange("b (k p) d -> p (b k) d", p=P)
            xv = x[:, :].rearrange("p (n d) -> p n d", d=D)
            n = GB * TPB
            sp.dma_start(xv[:, 0:n, :], rows[:, 0:n, :]).then_inc(x_loaded, 16)
            weights_load(sp, 0, 0)
            cond_loads(sp, 0)
            for dst, src in row_srcs[1:]:
                sp.dma_start(dst, src).then_inc(pro_loads, 16)
            sp.dma_start(xv[:, n:3 * n, :], rows[:, n:3 * n, :]).then_inc(x_mid, 16)
            for m in range(1, len(ADA)):
                sp.dma_start(adaw[m][:, :, :], t[ADA[m][0]].rearrange("(k p) m -> p k m", p=P)).then_inc(ada_loaded[m], 16)
                if m == 1:
                    sp.dma_start(xv[:, 3 * n:, :], rows[:, 3 * n:, :]).then_inc(x_rest, 16)
            cond_store(sp, 0)
            cond_loads(sp, 1)
            end_phase(sp, -1, False)
            program(sp, "sync", mh_sync, signs=False)
            sp.wait_ge(x_stored, 16 * BATCH)

        @block.scalar
        def _(act):
            act.wait_ge(consts, 1)
            act.activation(spacer[:, 7:8], ident[:, 0:1], ACT.Silu)
            act.wait_ge(cond_cols, 1)
            act.activation(siluT[:, :, :], condT[:, 0, :, :], ACT.Silu).then_inc(silu_ready, 1)
            end_phase(act, -1)
            program(act, "scalar", mh_scalar)

        @block.tensor
        def _(pe):
            pe.wait_ge(consts, 1)
            pe.wait_ge(cond_loaded, 16)
            pe.transpose(bank[5][:, 0:NC], condrows[0:NC, :], ident[0:NC, 0:NC]).then_inc(cond_tp, 1)
            pe.wait_ge(silu_ready, 1)
            for k in range(FIRST - 1):
                cond_step_tensor(pe, k)
            pe.wait_ge(pro_loads, 16 * len(row_srcs[1:]))
            pe.wait_ge(mask_rows, 1)
            pe.transpose(bank[3][:, 0:3 * NC], condrows[:, :], ident[0:3 * NC, 0:3 * NC])
            pe.transpose(bank[4][:, 0:NVEC], vecrows[:, :], ident[0:NVEC, 0:NVEC]).then_inc(cond_tp, 1)
            cond_step_tensor(pe, FIRST - 1)
            end_phase(pe, -1)
            program(pe, "tensor", mh_tensor)

        @block.vector
        def _(dve):
            def columns(tile, src, n):
                return dve.tensor_copy(tile.rearrange("p b k -> p (b k)"), src[:, n * NC:(n + 1) * NC])

            dve.wait_ge(cond_tp, 1)
            columns(condT[:, 0, :, :], bank[5], 0).then_inc(cond_cols, 1)
            dve.wait_ge(x_loaded, 16)
            dve.memset(spacer[:, 1:2], 0.0)
            head_norms("vector", dve, 0)
            for k in range(FIRST - 1):
                cond_step_vector(dve, k)
            weights_hi(dve, 0, 0)
            dve.wait_ge(pro_loads, 16 * len(row_srcs[1:]))
            dve.tensor_copy(condrows[2 * NC:3 * NC, :], mask8[2 * NC:3 * NC, :]).then_inc(mask_rows, 1)
            dve.wait_ge(cond_tp, 2)
            columns(condT[:, 1, :, :], bank[3], 1)
            dve.tensor_copy(maski[:, :], bank[3][:, 2 * NC:3 * NC])
            dve.tensor_copy(vecs[:, :], bank[4][:, 0:NVEC])
            cond_step_vector(dve, FIRST - 1)
            end_phase(dve, -1)
            program(dve, "vector", mh_vector)

        @block.gpsimd
        def _(pool):
            pool.memset(mhalf[:, :], -0.5)
            pool.memset(ident[:, :], 0.0).then_inc(ident_zero, 1)
            pool.wait_ge(ident_zero, 1)
            pool.affine_select(out=ident[:, :], in_=ident[:, :], compare_op=ALU.not_equal, fill=1.0, base=0,
                               pattern=[[-1, P]], channel_multiplier=1).then_inc(consts, 1)
            head_norms("gpsimd", pool, 0)
            weights_lo(pool, 0, 0)
            end_phase(pool, -1)
            program(pool, "gpsimd", mh_gpsimd)


def kernel(**inputs):
    import numpy as _np
    import concourse.bacc as _bacc
    from concourse import mybir as _mybir
    from concourse.bass_utils import run_bass_kernel_spmd as _run

    nc = _bacc.Bacc("TRN2", target_bir_lowering=False, num_devices=1)
    arrays, aps = {}, {}
    for name, value in inputs.items():
        a = _np.ascontiguousarray(value)
        arrays[f"in_{name}"] = a
        aps[name] = nc.dram_tensor(f"in_{name}", a.shape, _mybir.dt.from_np(a.dtype), kind="ExternalInput").ap()
    out = nc.dram_tensor("out", (BATCH, SEQ, D), F32, kind="ExternalOutput").ap()
    bass_cond_blocks(nc, aps, out)
    r = _run(nc, [arrays], core_ids=[0])
    return r.results[0]["out"]
```
